# Optimizing a Trainium2 kernel written in Bass

```python
import numpy as np
import jax
import jax.numpy as jnp

def _softmax(x, axis=-1):
    return jax.nn.softmax(x, axis=axis)
def _gelu(x):
    return jax.nn.gelu(x, approximate=True)
def _silu(x):
    return jax.nn.silu(x)
def _sigmoid(x):
    return jax.nn.sigmoid(x)
def _layernorm(x, axis=-1, eps=1e-5):
    m = jnp.mean(x, axis=axis, keepdims=True)
    v = jnp.var(x, axis=axis, keepdims=True)
    return (x - m) / jnp.sqrt(v + eps)
def _scatter_add(tgt, idx, src, axis=0):
    return tgt.at[idx].add(src)
def _segment_sum(src, seg, n):
    return jax.ops.segment_sum(src, seg, n)

kernel_name = 'mk_metaformer_d1_conv_nchw256_4f2ba1'

def setup_inputs(seed: int = 0):
    np.random.seed(seed)
    _w = jnp.asarray
    def _rec_inputs():
        import jax
        import jax.numpy as jnp
        _gk = jax.random.key(seed)
        x = -0.0001732 + 1 * jax.random.normal(jax.random.fold_in(_gk, 1), (2, 256, 96, 96), jnp.float32)
        return x
    x = _rec_inputs()
    def _L0_conv_setup():
        import jax, jax.numpy as jnp
        import numpy as np
        EPS = 1e-05

        def _conv(x, w, pad):
            return jax.lax.conv_general_dilated(x, w, window_strides=(1, 1), padding=((pad, pad), (pad, pad)), dimension_numbers=('NCHW', 'OIHW', 'NCHW'))

        def _dyn_branch(x, w, d):
            N, C, H, W = x.shape
            xp = jnp.pad(x, ((0, 0), (0, 0), (d, d), (d, d)))
            out = jnp.zeros_like(x)
            k = 0
            for dy in (-d, 0, d):
                for dx in (-d, 0, d):
                    patch = xp[:, :, d + dy:d + dy + H, d + dx:d + dx + W]
                    out = out + patch * w[:, k:k + 1]
                    k += 1
            return out
        key = jax.random.key(seed)
        k1, k2, k3 = jax.random.split(key, 3)
        C = 256
        x = jax.random.normal(k1, (2, C, 96, 96), dtype=jnp.float32)
        W_cat = jax.random.normal(k2, (45, C, 3, 3), dtype=jnp.float32) * 0.05
        W_scale = jax.random.normal(k3, (C, 6 * C, 1, 1), dtype=jnp.float32) * 0.05
        gamma = jnp.ones((C,), dtype=jnp.float32)
        beta = jnp.zeros((C,), dtype=jnp.float32)
        return {'x': x, 'W_cat': W_cat, 'W_scale': W_scale, 'gamma': gamma, 'beta': beta}
    _L0_conv_all = _L0_conv_setup()
    _L0_conv_in = {k: v for k, v in _L0_conv_all.items() if k in ('W_cat', 'W_scale', 'gamma', 'beta', )}
    del _L0_conv_all

    def _L0_ffn_setup():
        import jax, jax.numpy as jnp
        import numpy as np
        B, N, D = (16, 4096, 256)
        NUM_EXPERTS, TOP_K, HEADS = (4, 2, 4)
        N_EDGES = 1048576
        LN_EPS = 1e-05

        def _layernorm(x, g, b):
            mu = x.mean(-1, keepdims=True)
            var = ((x - mu) ** 2).mean(-1, keepdims=True)
            return (x - mu) * jax.lax.rsqrt(var + LN_EPS) * g + b

        def _forward(x, edge_index, W_gat, att_src, att_dst, b_gat, ln_gamma, ln_beta, W1, b1, W2, b2):
            Bc, Nc, Dc = x.shape
            M = Bc * Nc
            x_flat = x.reshape(M, Dc)
            h = (x_flat @ W_gat).reshape(M, HEADS, NUM_EXPERTS)
            loops = jnp.arange(M, dtype=edge_index.dtype)
            src = jnp.concatenate([edge_index[0], loops])
            dst = jnp.concatenate([edge_index[1], loops])
            a_src = (h * att_src).sum(-1)
            a_dst = (h * att_dst).sum(-1)
            e = jax.nn.leaky_relu(a_src[src] + a_dst[dst], negative_slope=0.2)
            e_max = jax.ops.segment_max(e, dst, num_segments=M)
            ee = jnp.exp(e - e_max[dst])
            denom = jax.ops.segment_sum(ee, dst, num_segments=M)
            alpha = ee / (denom[dst] + 1e-16)
            msg = h[src] * alpha[:, :, None]
            agg = jax.ops.segment_sum(msg, dst, num_segments=M).reshape(M, HEADS * NUM_EXPERTS) + b_gat
            scores = _layernorm(agg, ln_gamma, ln_beta).reshape(M, HEADS, NUM_EXPERTS).mean(1)
            scores = scores.reshape(Bc, Nc, NUM_EXPERTS)
            topk_s, topk_i = jax.lax.top_k(scores, TOP_K)
            w = jax.nn.softmax(topk_s, axis=-1)
            out = jnp.zeros_like(x)
            for ei in range(NUM_EXPERTS):
                g = jnp.where(topk_i == ei, w, 0.0).sum(-1)
                hh = jax.nn.gelu(x @ W1[ei] + b1[ei], approximate=False)
                out = out + g[..., None] * (hh @ W2[ei] + b2[ei])
            return out
        key = jax.random.key(seed)
        ks = jax.random.split(key, 8)
        s = 0.05
        return {'x': jax.random.normal(ks[0], (B, N, D), jnp.float32), 'W_gat': jax.random.normal(ks[1], (D, HEADS * NUM_EXPERTS), jnp.float32) * s, 'att_src': jax.random.normal(ks[2], (HEADS, NUM_EXPERTS), jnp.float32) * s, 'att_dst': jax.random.normal(ks[3], (HEADS, NUM_EXPERTS), jnp.float32) * s, 'b_gat': jnp.zeros((HEADS * NUM_EXPERTS,), jnp.float32), 'ln_gamma': jnp.ones((HEADS * NUM_EXPERTS,), jnp.float32), 'ln_beta': jnp.zeros((HEADS * NUM_EXPERTS,), jnp.float32), 'W1': jax.random.normal(ks[4], (NUM_EXPERTS, D, 2 * D), jnp.float32) * s, 'b1': jnp.zeros((NUM_EXPERTS, 2 * D), jnp.float32), 'W2': jax.random.normal(ks[5], (NUM_EXPERTS, 2 * D, D), jnp.float32) * s, 'b2': jnp.zeros((NUM_EXPERTS, D), jnp.float32), 'edge_index': jax.random.randint(ks[6], (2, N_EDGES), 0, B * N, jnp.int32)}
    _L0_ffn_all = _L0_ffn_setup()
    _L0_ffn_in = {k: v for k, v in _L0_ffn_all.items() if k in ('W_gat', 'att_src', 'att_dst', 'b_gat', 'ln_gamma', 'ln_beta', 'W1', 'b1', 'W2', 'b2', 'edge_index', )}
    del _L0_ffn_all

    return {
        "x": x,
        "L0_conv_W_cat": _L0_conv_in["W_cat"],
        "L0_conv_W_scale": _L0_conv_in["W_scale"],
        "L0_conv_gamma": _L0_conv_in["gamma"],
        "L0_conv_beta": _L0_conv_in["beta"],
        "L0_ffn_W_gat": _L0_ffn_in["W_gat"],
        "L0_ffn_att_src": _L0_ffn_in["att_src"],
        "L0_ffn_att_dst": _L0_ffn_in["att_dst"],
        "L0_ffn_b_gat": _L0_ffn_in["b_gat"],
        "L0_ffn_ln_gamma": _L0_ffn_in["ln_gamma"],
        "L0_ffn_ln_beta": _L0_ffn_in["ln_beta"],
        "L0_ffn_W1": _L0_ffn_in["W1"],
        "L0_ffn_b1": _L0_ffn_in["b1"],
        "L0_ffn_W2": _L0_ffn_in["W2"],
        "L0_ffn_b2": _L0_ffn_in["b2"],
        "L0_ffn_edge_index": _L0_ffn_in["edge_index"],
    }

def reference(x, L0_conv_W_cat, L0_conv_W_scale, L0_conv_gamma, L0_conv_beta, L0_ffn_W_gat, L0_ffn_att_src, L0_ffn_att_dst, L0_ffn_b_gat, L0_ffn_ln_gamma, L0_ffn_ln_beta, L0_ffn_W1, L0_ffn_b1, L0_ffn_W2, L0_ffn_b2, L0_ffn_edge_index):
    import jax
    import jax.numpy as jnp
    def _L0_conv_ref(x, W_cat, W_scale, gamma, beta):
        import jax, jax.numpy as jnp
        import numpy as np
        EPS = 1e-05

        def _conv(x, w, pad):
            return jax.lax.conv_general_dilated(x, w, window_strides=(1, 1), padding=((pad, pad), (pad, pad)), dimension_numbers=('NCHW', 'OIHW', 'NCHW'))

        def _dyn_branch(x, w, d):
            N, C, H, W = x.shape
            xp = jnp.pad(x, ((0, 0), (0, 0), (d, d), (d, d)))
            out = jnp.zeros_like(x)
            k = 0
            for dy in (-d, 0, d):
                for dx in (-d, 0, d):
                    patch = xp[:, :, d + dy:d + dy + H, d + dx:d + dx + W]
                    out = out + patch * w[:, k:k + 1]
                    k += 1
            return out
        guidance = _conv(x, W_cat, pad=1)
        outs = [x]
        for i, d in enumerate((1, 6, 12, 24, 36)):
            w = jax.nn.softmax(guidance[:, 9 * i:9 * (i + 1)], axis=1)
            outs.append(_dyn_branch(x, w, d))
        cat = jnp.concatenate(outs, axis=1)
        y = _conv(cat, W_scale, pad=0)
        mean = jnp.mean(y, axis=(0, 2, 3), keepdims=True)
        var = jnp.var(y, axis=(0, 2, 3), keepdims=True)
        y = (y - mean) * jax.lax.rsqrt(var + EPS)
        return y * gamma[None, :, None, None] + beta[None, :, None, None]

    def _L0_ffn_ref(x, W_gat, att_src, att_dst, b_gat, ln_gamma, ln_beta, W1, b1, W2, b2, edge_index):
        import jax, jax.numpy as jnp
        import numpy as np
        B, N, D = (16, 4096, 256)
        NUM_EXPERTS, TOP_K, HEADS = (4, 2, 4)
        N_EDGES = 1048576
        LN_EPS = 1e-05

        def _layernorm(x, g, b):
            mu = x.mean(-1, keepdims=True)
            var = ((x - mu) ** 2).mean(-1, keepdims=True)
            return (x - mu) * jax.lax.rsqrt(var + LN_EPS) * g + b

        def _forward(x, edge_index, W_gat, att_src, att_dst, b_gat, ln_gamma, ln_beta, W1, b1, W2, b2):
            Bc, Nc, Dc = x.shape
            M = Bc * Nc
            x_flat = x.reshape(M, Dc)
            h = (x_flat @ W_gat).reshape(M, HEADS, NUM_EXPERTS)
            loops = jnp.arange(M, dtype=edge_index.dtype)
            src = jnp.concatenate([edge_index[0], loops])
            dst = jnp.concatenate([edge_index[1], loops])
            a_src = (h * att_src).sum(-1)
            a_dst = (h * att_dst).sum(-1)
            e = jax.nn.leaky_relu(a_src[src] + a_dst[dst], negative_slope=0.2)
            e_max = jax.ops.segment_max(e, dst, num_segments=M)
            ee = jnp.exp(e - e_max[dst])
            denom = jax.ops.segment_sum(ee, dst, num_segments=M)
            alpha = ee / (denom[dst] + 1e-16)
            msg = h[src] * alpha[:, :, None]
            agg = jax.ops.segment_sum(msg, dst, num_segments=M).reshape(M, HEADS * NUM_EXPERTS) + b_gat
            scores = _layernorm(agg, ln_gamma, ln_beta).reshape(M, HEADS, NUM_EXPERTS).mean(1)
            scores = scores.reshape(Bc, Nc, NUM_EXPERTS)
            topk_s, topk_i = jax.lax.top_k(scores, TOP_K)
            w = jax.nn.softmax(topk_s, axis=-1)
            out = jnp.zeros_like(x)
            for ei in range(NUM_EXPERTS):
                g = jnp.where(topk_i == ei, w, 0.0).sum(-1)
                hh = jax.nn.gelu(x @ W1[ei] + b1[ei], approximate=False)
                out = out + g[..., None] * (hh @ W2[ei] + b2[ei])
            return out
        return _forward(x, edge_index, W_gat, att_src, att_dst, b_gat, ln_gamma, ln_beta, W1, b1, W2, b2)

    def _gn(v, G=32, eps=1e-5):
        B_, C_, H_, W_ = v.shape
        g = v.reshape(B_, G, C_ // G, H_, W_)
        m = jnp.mean(g, axis=(2, 3, 4), keepdims=True)
        s = jnp.var(g, axis=(2, 3, 4), keepdims=True)
        return ((g - m) / jnp.sqrt(s + eps)).reshape(v.shape)

    def _ln_c(v, eps=1e-6):
        m = jnp.mean(v, axis=1, keepdims=True)
        s = jnp.var(v, axis=1, keepdims=True)
        return (v - m) / jnp.sqrt(s + eps)

    def _ln_t(v, eps=1e-5):
        m = jnp.mean(v, axis=-1, keepdims=True)
        s = jnp.var(v, axis=-1, keepdims=True)
        return (v - m) / jnp.sqrt(s + eps)

    def _to_tokens(v):
        B_, C_, H_, W_ = v.shape
        return v.reshape(B_, C_, H_ * W_).transpose(0, 2, 1)
    def _from_tokens(t, like):
        B_, C_, H_, W_ = like.shape
        return t.transpose(0, 2, 1).reshape(B_, C_, H_, W_)

    x = x + _L0_conv_ref(_ln_c(x), L0_conv_W_cat, L0_conv_W_scale, L0_conv_gamma, L0_conv_beta)
    t = _to_tokens(x)
    t = t + _L0_ffn_ref(_ln_t(t), L0_ffn_W_gat, L0_ffn_att_src, L0_ffn_att_dst, L0_ffn_b_gat, L0_ffn_ln_gamma, L0_ffn_ln_beta, L0_ffn_W1, L0_ffn_b1, L0_ffn_W2, L0_ffn_b2, L0_ffn_edge_index)
    x = _from_tokens(t, x)
    return x


_drawn_inputs = setup_inputs


def setup_inputs(seed=0):
    import zlib

    import numpy as np

    out = dict(_drawn_inputs(seed))
    spreads = {'L0_conv_gamma': (1.0, 0.2),
     'L0_conv_beta': (0.0, 0.1),
     'L0_ffn_b_gat': (0.0, 0.1),
     'L0_ffn_ln_gamma': (1.0, 0.2),
     'L0_ffn_ln_beta': (0.0, 0.1),
     'L0_ffn_b1': (0.0, 0.1),
     'L0_ffn_b2': (0.0, 0.1)}
    factors = {}
    for name, (base, spread) in spreads.items():
        noise = np.random.default_rng([zlib.crc32(name.encode()), seed]).standard_normal(out[name].shape)
        drawn = base * np.exp(spread * noise) if base else spread * noise
        out[name] = jnp.asarray(drawn.astype(out[name].dtype))
    for name, factor in factors.items():
        out[name] = (out[name] * factor).astype(out[name].dtype)
    return out
```

```python
from contextlib import ExitStack

import concourse.bass as bass
from concourse import mybir

P = 128
ALU = mybir.AluOpType
ACT = mybir.ActivationFunctionType
AX_X = mybir.AxisListType.X
F32 = mybir.dt.float32
BF16 = mybir.dt.bfloat16
F16 = mybir.dt.float16
I32 = mybir.dt.int32
U32 = mybir.dt.uint32
U16 = mybir.dt.uint16

IMGS, C, H, W = 2, 256, 96, 96
PIX = H * W
TOK = IMGS * PIX
TILES = TOK // P
E = 1048576
HEADS, EXPERTS = 4, 4
HE = HEADS * EXPERTS

SRC_BITS = 15
SRC_MASK = (1 << SRC_BITS) - 1
KEY_BASE = 256
KEY_LAST = 1 << 15
KEY_DROP = 0xFE00
LANE = E // P
CHUNK = P * P
CHUNKS = E // CHUNK
NODE = HE + 2 * HEADS
ROW = HE + HEADS


class Ctx:
    pass


def declare_scratch(nc, k):
    k.xn_rows = nc.dram_tensor("xn_rows", (C, IMGS, H + 2, W), F32, kind="Internal").ap()
    k.xn_pixels = nc.dram_tensor("xn_pixels", (IMGS, H + 2, W, C), F32, kind="Internal").ap()
    k.taps_left = nc.dram_tensor("taps_left", (SPLITS * LEFT, TOK), BF16, kind="Internal").ap()
    k.taps_right = nc.dram_tensor("taps_right", (SPLITS * RIGHT, TOK), BF16, kind="Internal").ap()
    k.conv_out = nc.dram_tensor("conv_out", (C, IMGS, H, W), F32, kind="Internal").ap()
    k.ln_rows = nc.dram_tensor("ln_rows", (C, IMGS, H, W), F32, kind="Internal").ap()
    k.residual = nc.dram_tensor("residual", (IMGS, P, PARTS_C, PIX), F32, kind="Internal").ap()
    k.table = nc.dram_tensor("table", (TOK, ROW), F32, kind="Internal").ap()
    k.dst_scores = nc.dram_tensor("dst_scores", (E + CHUNK, HEADS), F32, kind="Internal").ap()
    k.states = nc.dram_tensor("states", (E, NODE), F32, kind="Internal").ap()
    k.sorted_keys = nc.dram_tensor("sorted_keys", (P + E + CHUNK,), I32, kind="Internal").ap()


GROUP_ROWS = 4
GPX = GROUP_ROWS * W
ROW_GROUPS = H // GROUP_ROWS
PARTS_C = C // P
DILATIONS = (1, 6, 12, 24, 36)
BRANCHES = len(DILATIONS)
TAPS = 9
GUIDES = BRANCHES * TAPS
LN_C_EPS, LN_T_EPS, BN_EPS = 1e-6, 1e-5, 1e-5
SPLITS = 3
LEFT_BRANCHES = 3
LEFT = LEFT_BRANCHES * TAPS
RIGHT = GUIDES - LEFT


def edge_keys(nc, k):
    PART = 1024
    PARTS = LANE // PART
    edges = k.edge_index.rearrange("two (p f) -> two p f", p=P)
    with ExitStack() as ctx:
        src = [ctx.enter_context(nc.sbuf_tensor(f"ek_src{i}", [P, PART], I32)) for i in range(2)]
        dst = [ctx.enter_context(nc.sbuf_tensor(f"ek_dst{i}", [P, PART], I32)) for i in range(2)]
        t1 = ctx.enter_context(nc.sbuf_tensor("ek_t1", [P, PART], I32))
        t2 = ctx.enter_context(nc.sbuf_tensor("ek_t2", [P, PART], I32))
        t3 = ctx.enter_context(nc.sbuf_tensor("ek_t3", [P, PART], I32))
        part_count = ctx.enter_context(nc.sbuf_tensor("ek_part_count", [P, 2, PARTS], F32))
        counted = ctx.enter_context(nc.sbuf_tensor("ek_counted", [P, 2], F32))
        totals = ctx.enter_context(nc.psum_tensor("ek_totals", [P, 2], F32))
        src_in = [ctx.enter_context(nc.semaphore(f"ek_src_in{i}")) for i in range(2)]
        dst_in = [ctx.enter_context(nc.semaphore(f"ek_dst_in{i}")) for i in range(2)]
        part_done = ctx.enter_context(nc.semaphore("ek_part_done"))
        lane_counted = ctx.enter_context(nc.semaphore("ek_lane_counted"))
        totals_ready = ctx.enter_context(nc.semaphore("ek_totals_ready"))
        block = ctx.enter_context(nc.Block())

        @block.sync
        def _(sp):
            for c in range(PARTS):
                if c >= 2:
                    sp.wait_ge(part_done, c - 1)
                sp.dma_start(src[c % 2][:, :], edges[0, :, c * PART:(c + 1) * PART]).then_inc(src_in[c % 2], 16)
                sp.dma_start(dst[c % 2][:, :], edges[1, :, c * PART:(c + 1) * PART]).then_inc(dst_in[c % 2], 16)

        @block.vector
        def _(dve):
            for c in range(PARTS):
                s, d = src[c % 2], dst[c % 2]
                dve.wait_ge(src_in[c % 2], 16 * (c // 2 + 1))
                dve.wait_ge(dst_in[c % 2], 16 * (c // 2 + 1))
                dve.tensor_scalar(t1[:, :], s[:, :], float(TOK - 1), float(KEY_LAST), ALU.is_ge, ALU.mult)
                dve.tensor_scalar(t2[:, :], d[:, :], float(TOK), float(KEY_BASE), ALU.min, ALU.add)
                dve.tensor_scalar(t3[:, :], d[:, :], float(TOK), float(KEY_DROP), ALU.is_ge, ALU.mult)
                dve.tensor_scalar(s[:, :], s[:, :], float(TOK - 1), 0.0, ALU.min, ALU.max)
                dve.drain()
                dve.tensor_tensor(t2[:, :], t2[:, :], t1[:, :], ALU.add)
                dve.drain()
                dve.tensor_tensor(t2[:, :], t2[:, :], t3[:, :], ALU.max)
                dve.drain()
                dve.tensor_scalar(t1[:, :], t2[:, :], float(KEY_LAST), 0.0, ALU.is_ge, ALU.add,
                                  accum_out=part_count[:, 0, c:c + 1])
                dve.tensor_scalar(t3[:, :], t2[:, :], float(KEY_DROP), 0.0, ALU.is_ge, ALU.add,
                                  accum_out=part_count[:, 1, c:c + 1])
                dve.scalar_tensor_tensor(k.keys_a[:, c * PART:(c + 1) * PART].bitcast(I32), t2[:, :], SRC_BITS,
                                         s[:, :], ALU.logical_shift_left, ALU.bitwise_or).then_inc(part_done, 1)
                dve.drain()
            dve.tensor_reduce(counted[:, :], part_count[:, :, :], AX_X, ALU.add).then_inc(lane_counted, 1)
            dve.wait_ge(totals_ready, 1)
            dve.tensor_scalar(k.edge_counts[:, :], totals[:, :], -1.0, float(E), ALU.mult, ALU.add)
            dve.drain()
            dve.tensor_scalar(k.own_edges[:, :], k.edge_counts[:, 0:1], 1.0, None, ALU.max)

        @block.tensor
        def _(pe):
            pe.wait_ge(lane_counted, 1)
            pe.matmul(totals[:, :], k.ones_f[:, :], counted[:, :], start=True, stop=True).then_inc(totals_ready, 1)


def sort_views(buf, j, q):
    if q is None:
        v = buf[:, :].rearrange("p (a two c) -> p a two c", two=2, c=1 << j)
        return {0: (v[:, :, 0, :], v[:, :, 1, :])}
    hi, lo = max(j, q), min(j, q)
    v = buf[:, :].rearrange("p (a h b l c) -> p a h b l c", h=2, l=2, b=1 << (hi - lo - 1), c=1 << lo)
    out = {}
    for d in range(2):
        pair = []
        for side in range(2):
            h, l = (side, d) if j > q else (d, side)
            x = v[:, :, h, :, l, :]
            pair.append(x[:, :, 0, :] if hi - lo == 1 else x[:, 0, :, :])
        out[d] = tuple(pair)
    return out


def sort_edges(nc, k):
    FREE, TOP = 13, 20
    a, b = k.keys_a, k.keys_b

    def index_bit(bit, transposed):
        return bit if not transposed or bit < FREE else bit - FREE

    with ExitStack() as ctx:
        blocks_ps = [ctx.enter_context(nc.psum_tensor(f"so_ps{i}", [P, 4, P], F32)) for i in range(8)]
        to_transpose = ctx.enter_context(nc.semaphore("so_to_transpose"))
        transposed_ps = ctx.enter_context(nc.semaphore("so_transposed_ps"))
        evacuated = ctx.enter_context(nc.semaphore("so_evacuated"))
        block = ctx.enter_context(nc.Block())
        GROUPS = LANE // (4 * P)
        FILL = 1040
        FILLS = (E + CHUNK) // (P * FILL)
        assert FILLS * P * FILL == E + CHUNK
        zeros = ctx.enter_context(nc.sbuf_tensor("so_zeros", [P, FILL * HEADS], F32))
        zero_ready = ctx.enter_context(nc.semaphore("so_zero_ready"))
        zero_out = ctx.enter_context(nc.semaphore("so_zero_out"))

        @block.gpsimd
        def _(pool):
            pool.memset(zeros[:, :], 0.0).then_inc(zero_ready, 1)

        @block.sync
        def _(sp):
            sp.wait_ge(zero_ready, 1)
            fill = k.dst_scores.rearrange("(n p r) h -> n p (r h)", p=P, r=FILL)
            for n in range(FILLS):
                sp.dma_start(fill[n], zeros[:, :]).then_inc(zero_out, 16)
            fill = k.states.rearrange("(n p r) c -> n p (r c)", p=P, r=P)
            for n in range(CHUNKS):
                sp.dma_start(fill[n], zeros[:, 0:P * NODE]).then_inc(zero_out, 16)
            sp.wait_ge(zero_out, 16 * (FILLS + CHUNKS))

        state = {"cur": 0}
        turns = []

        def steps(level, first_bit, last_bit, transposed):
            out = []
            for bit in range(first_bit, last_bit - 1, -1):
                first = bit == level - 1
                q = index_bit(level, transposed) if first and level < TOP else None
                out.append((index_bit(bit, transposed), q, first, level < TOP))
            return out

        @block.vector
        def _(dve):
            bufs = [a, b]

            def run(todo):
                for j, q, first, flips in todo:
                    s, d = bufs[state["cur"]], bufs[1 - state["cur"]]
                    sv, dv = sort_views(s, j, q), sort_views(d, j, q)
                    for direction, (low, high) in sv.items():
                        out_low, out_high = dv[direction]
                        for out, op in ((out_low, ALU.min), (out_high, ALU.max)):
                            if not first:
                                dve.tensor_tensor(out, low, high, op)
                            elif state.get("level") == 1:
                                if direction == 0:
                                    dve.tensor_tensor(out, low, high, op)
                                else:
                                    other = ALU.max if op == ALU.min else ALU.min
                                    dve.tensor_tensor(out, low, high, other)
                            elif direction == 0:
                                dve.scalar_tensor_tensor(out, high, -1.0, low, ALU.mult, op)
                            else:
                                dve.scalar_tensor_tensor(out, low, -1.0, high, ALU.mult, op)
                    dve.drain()
                    if state.get("level") == 1:
                        x = sort_views(d, 0, 1)[1]
                        for side in x:
                            dve.tensor_scalar(side, side, -1.0, None, ALU.mult)
                        dve.drain()
                    state["cur"] = 1 - state["cur"]

            def turn():
                turns.append(state["cur"])
                dve.sem_inc(to_transpose, 1)
                dve.wait_ge(evacuated, GROUPS * len(turns))
                state["cur"] = 1 - state["cur"]

            for level in range(1, TOP + 1):
                state["level"] = level
                if level < FREE:
                    run(steps(level, level - 1, 0, False))
                else:
                    turn()
                    run(steps(level, level - 1, 7, True))
                    turn()
                    run(steps(level, 6, 0, False))
            k.sorted_buf = bufs[state["cur"]]

        @block.tensor
        def _(pe):
            bufs = [a, b]
            for n, source in enumerate(turns):
                pe.wait_ge(to_transpose, n + 1)
                for g in range(GROUPS):
                    if n * GROUPS + g >= 8:
                        pe.wait_ge(evacuated, n * GROUPS + g - 7)
                    for i in range(4):
                        c = (4 * g + i) * P
                        mm = pe.transpose(blocks_ps[g % 8][:, i, :], bufs[source][:, c:c + P], k.ident[:, :])
                    mm.then_inc(transposed_ps, 1)

        @block.scalar
        def _(act):
            bufs = [a, b]
            for n, source in enumerate(turns):
                for g in range(GROUPS):
                    act.wait_ge(transposed_ps, n * GROUPS + g + 1)
                    act.activation(bufs[1 - source][:, g * 4 * P:(g + 1) * 4 * P],
                                   blocks_ps[g % 8][:, :, :].rearrange("p a b -> p (a b)"),
                                   ACT.Copy).then_inc(evacuated, 1)


def store_sorted(nc, k):
    with ExitStack() as ctx:
        front = ctx.enter_context(nc.sbuf_tensor("ss_front", [1, P], I32))
        tail = ctx.enter_context(nc.sbuf_tensor("ss_tail", [P, P], I32))
        tail_out = ctx.enter_context(nc.semaphore("ss_tail_out"))
        front_zero = ctx.enter_context(nc.semaphore("ss_front_zero"))
        front_out = ctx.enter_context(nc.semaphore("ss_front_out"))
        keys_out = ctx.enter_context(nc.semaphore("ss_keys_out"))
        block = ctx.enter_context(nc.Block())

        @block.vector
        def _(dve):
            dve.memset(tail[:, :], 0)
            dve.memset(front[:, :], 0).then_inc(front_zero, 1)

        @block.sync
        def _(sp):
            sp.dma_start(k.sorted_keys[P:P + E].rearrange("(p f) -> p f", p=P),
                         k.sorted_buf[:, :].bitcast(I32)).then_inc(keys_out, 16)
            sp.wait_ge(front_zero, 1)
            sp.dma_start(k.sorted_keys[0:P].rearrange("(a f) -> a f", a=1), front[:, :]).then_inc(front_out, 16)
            sp.dma_start(k.sorted_keys[P + E:].rearrange("(p f) -> p f", p=P), tail[:, :]).then_inc(tail_out, 16)
            sp.wait_ge(keys_out, 16)
            sp.wait_ge(front_out, 16)
            sp.wait_ge(tail_out, 16)


def count_edges(nc, k):
    KINDS = 2 * TILES
    RING, GROUP = 16, 4
    GROUPS = P // GROUP
    with ExitStack() as ctx:
        def sb(name, shape, dt):
            return ctx.enter_context(nc.sbuf_tensor(name, shape, dt))

        def sem(name):
            return ctx.enter_context(nc.semaphore(name))
        keys = sb("ce_keys", [P, P], I32)
        token = sb("ce_token", [P, P], I32)
        high = sb("ce_high", [P, P], F32)
        low = sb("ce_low", [P, P], F32)
        high_i = sb("ce_high_i", [P, P], I32)
        low_i = sb("ce_low_i", [P, P], I32)
        hot_high = sb("ce_hot_high", [P, RING, KINDS], BF16)
        hot_low = sb("ce_hot_low", [P, RING, P], BF16)
        iota_high = sb("ce_iota_high", [P, KINDS], F16)
        iota_low = sb("ce_iota_low", [P, P], F16)
        before = sb("ce_before", [P, P], F32)
        counts = sb("ce_counts", [P, KINDS], F32)
        running = sb("ce_running", [P, TILES], F32)
        column = sb("ce_column", [P, TILES], F32)
        first = sb("ce_first", [P, TILES], F32)
        none = sb("ce_none", [P, TILES], F32)
        counts_ps = ctx.enter_context(nc.psum_tensor("ce_counts_ps", [P, KINDS], F32))
        within_ps = ctx.enter_context(nc.psum_tensor("ce_within_ps", [P, TILES], F32))
        column_ps = ctx.enter_context(nc.psum_tensor("ce_column_ps", [P, TILES], F32))
        iota_ready, before_ready, keys_in, keys_read = (sem("ce_" + x) for x in (
            "iota_ready", "before_ready", "keys_in", "keys_read"))
        hot_ready, hot_free, chunk_added = (sem("ce_" + x) for x in (
            "hot_ready", "hot_free", "chunk_added"))
        sums_ready = sem("ce_sums_ready")
        counts_whole = sem("ce_counts_whole")
        block = ctx.enter_context(nc.Block())

        @block.gpsimd
        def _(pool):
            pool.memset(before[:, :], 1.0).then_inc(before_ready, 1)
            pool.iota(iota_high[:, :].rearrange("p (a b) -> p a b", a=2), [[KEY_LAST // P, 2], [1, TILES]], base=0,
                      channel_multiplier=0, allow_small_or_imprecise_dtypes=True)
            pool.iota(iota_low[:, :], [[1, P]], base=0, channel_multiplier=0,
                      allow_small_or_imprecise_dtypes=True).then_inc(iota_ready, 1)
            pool.wait_ge(before_ready, 1)
            pool.affine_select(out=before[:, :], in_=before[:, :], compare_op=ALU.is_gt, fill=0.0, base=0,
                               pattern=[[1, P]], channel_multiplier=-1).then_inc(before_ready, 1)

        @block.sync
        def _(sp):
            kept = sp.value_load(k.edge_counts[0:1, 1:2], min_val=0, max_val=E)
            with sp.Fori(0, CHUNKS) as c:
                with sp.If(c * CHUNK < kept):
                    sp.wait_ge(keys_read, c + 1)
                    sp.dma_start(keys[:, :], k.sorted_keys[bass.ds(c * CHUNK + P, CHUNK)].rearrange(
                        "(p f) -> p f", p=P)).then_inc(keys_in, 16)

        @block.vector
        def _(dve):
            dve.memset(counts[:, :], 0.0)
            dve.sem_inc(keys_read, 1)
            dve.sem_inc(chunk_added, 1)
            dve.wait_ge(iota_ready, 1)
            kept = dve.value_load(k.edge_counts[0:1, 1:2], min_val=0, max_val=E)
            with dve.Fori(0, CHUNKS) as c:
                with dve.If(c * CHUNK < kept):
                    dve.wait_ge(keys_in, c * 16 + 16)
                    dve.tensor_scalar(token[:, :], keys[:, :], SRC_BITS, None,
                                      ALU.logical_shift_right).then_inc(keys_read, 1)
                    dve.drain()
                    dve.tensor_scalar(token[:, :], token[:, :], float(KEY_BASE), None, ALU.subtract)
                    dve.drain()
                    dve.tensor_scalar(high_i[:, :], token[:, :], 7, None, ALU.logical_shift_right)
                    dve.tensor_scalar(low_i[:, :], token[:, :], P - 1, None, ALU.bitwise_and)
                    dve.drain()
                    dve.tensor_copy(high[:, :], high_i[:, :])
                    dve.tensor_copy(low[:, :], low_i[:, :])
                    dve.drain()
                    for g in range(GROUPS):
                        dve.wait_ge(hot_free, c * GROUPS + g + 1)
                        for i in range(GROUP):
                            j = GROUP * g + i
                            dve.tensor_scalar(hot_high[:, j % RING, :], iota_high[:, :], high[:, j:j + 1], None,
                                              ALU.is_equal)
                            last = dve.tensor_scalar(hot_low[:, j % RING, :], iota_low[:, :], low[:, j:j + 1],
                                                     None, ALU.is_equal)
                        last.then_inc(hot_ready, 1)
                    dve.wait_ge(hot_free, c * GROUPS + GROUPS + RING // GROUP)
                    dve.tensor_tensor(counts[:, :], counts[:, :], counts_ps[:, :], ALU.add).then_inc(chunk_added, 1)
                    dve.drain()
            dve.sem_inc(counts_whole, 1)
            own = counts[:, 0:TILES]
            dve.wait_ge(sums_ready, 1)
            dve.tensor_copy(column[:, :], column_ps[:, :])
            dve.drain()
            dve.tensor_tensor_scan(running[:, :], column[:, :], column[:, :], 0.0, ALU.add, ALU.bypass)
            dve.tensor_scalar(none[:, :], own, 0.5, float(2 * E), ALU.is_lt, ALU.mult)
            dve.drain()
            dve.tensor_tensor(first[:, :], running[:, :], column[:, :], ALU.subtract)
            dve.tensor_scalar(k.has_own[:, :], own, 0.5, None, ALU.is_gt)
            dve.tensor_scalar(k.has_last[:, :], counts[:, TILES:KINDS], 0.5, None, ALU.is_gt)
            dve.tensor_copy(k.count_last[:, :], counts[:, TILES:KINDS])
            dve.drain()
            dve.tensor_tensor(first[:, :], first[:, :], within_ps[:, :], ALU.add)
            dve.drain()
            dve.tensor_tensor(k.first_place[:, :], first[:, :], none[:, :], ALU.add)
            dve.tensor_tensor(running[:, :], first[:, :], own, ALU.add)
            dve.drain()
            dve.scalar_tensor_tensor(k.last_place[:, :], running[:, :], 1.0, k.has_own[:, :], ALU.subtract, ALU.mult)

        @block.tensor
        def _(pe):
            pe.sem_inc(hot_free, RING // GROUP)
            kept = pe.value_load(k.edge_counts[0:1, 1:2], min_val=0, max_val=E)
            with pe.Fori(0, CHUNKS) as c:
                with pe.If(c * CHUNK < kept):
                    pe.wait_ge(chunk_added, c + 1)
                    for g in range(GROUPS):
                        pe.wait_ge(hot_ready, c * GROUPS + g + 1)
                        for i in range(GROUP):
                            j = GROUP * g + i
                            mm = pe.matmul(counts_ps[:, :], hot_low[:, j % RING, :], hot_high[:, j % RING, :],
                                           start=(j == 0), stop=(j == P - 1))
                        mm.then_inc(hot_free, 1)
            pe.wait_ge(counts_whole, 1)
            pe.wait_ge(before_ready, 2)
            pe.matmul(within_ps[:, :], before[:, :], counts[:, 0:TILES], start=True, stop=True)
            pe.matmul(column_ps[:, :], k.ones_f[:, :], counts[:, 0:TILES], start=True,
                      stop=True).then_inc(sums_ready, 1)


def wait_alone(eng, sem, value, passed):
    eng.wait_ge(sem, value)
    eng.sem_inc(passed, 1)


UNROLL = 8


def over_tiles(eng, stages):
    for img in range(IMGS):
        with eng.Fori(0, ROW_GROUPS // UNROLL) as i:
            for step in range(UNROLL + max(lag for _, lag in stages)):
                for body, lag in stages:
                    u = step - lag
                    if 0 <= u < UNROLL:
                        body(img, i * UNROLL + u, i * UNROLL + (img * ROW_GROUPS + u), u)


def layer_norm_tiles(nc, k, tokens):
    x_tiles = k.x.rearrange("b (h p) y w -> b p h (y w)", p=P)
    y_tiles = k.conv_out.rearrange("(h p) b y w -> b p h (y w)", p=P)
    BUFS, CREDIT = 4, 2
    tag = "lt_" if tokens else "lc_"
    TILE_TOKENS = GPX // P
    with ExitStack() as ctx:
        def sb(name, shape, dt):
            return ctx.enter_context(nc.sbuf_tensor(tag + name, shape, dt))

        def sem(name):
            return ctx.enter_context(nc.semaphore(tag + name))

        def ps(name, shape):
            return ctx.enter_context(nc.psum_tensor(tag + name, shape, F32))
        x = [sb(f"x{b}", [P, PARTS_C, GPX], F32) for b in range(BUFS)]
        y = [sb(f"y{b}", [P, PARTS_C, GPX], F32) for b in range(BUFS)] if tokens else x
        square = [sb(f"square{c}", [P, PARTS_C, GPX], F32) for c in range(2)]
        spread = [sb(f"spread{c}", [P, GPX], F32) for c in range(2)]
        pixels = [sb(f"pixels{c}", [W, GROUP_ROWS, C], F32) for c in range(2)]
        zeros = sb("zeros", [P, C], F32)
        mean_ps = [ps(f"mean{c}", [P, GPX]) for c in range(2)]
        var_ps = [ps(f"var{c}", [P, GPX]) for c in range(2)]
        post_ps = [ps(f"post{c}", [P, TILE_TOKENS, NODE] if tokens else [W, GROUP_ROWS, C]) for c in range(2)]
        x_in = [sem(f"x_in{b}") for b in range(BUFS)]
        rows_out = [sem(f"rows_out{b}") for b in range(BUFS)]
        sums_out = [sem(f"sums_out{b}") for b in range(BUFS)] if tokens else None
        pixels_out = None if tokens else [sem(f"pixels_out{c}") for c in range(2)]
        summed, mean_ready, squared = sem("summed"), sem("mean_ready"), sem("squared")
        centred, var_ready, spread_ready, normed, copied, posted = (
            sem(n) for n in ("centred", "var_ready", "spread_ready", "normed", "copied", "posted"))
        zero_ready, zero_out, table_out = sem("zero_ready"), sem("zero_out"), sem("table_out")
        block = ctx.enter_context(nc.Block())
        eps = k.eps_t if tokens else k.eps_c
        TILES_ALL = IMGS * ROW_GROUPS
        LOADED = 32 if tokens else 16

        @block.sync
        def _(sp):
            def load(img, g, n, u):
                b = u % BUFS
                wait_alone(sp, posted, n + 1, k.passed)
                wait_alone(sp, rows_out[b], (n - b) * (16 * PARTS_C // BUFS) + 1, k.passed)
                if tokens:
                    sp.wait_ge(sums_out[b], (n - b) * (16 // BUFS) + 1)
                    sp.dma_start(y[b][:, :, :], y_tiles[img, :, :, bass.ds(g * GPX, GPX)]).then_inc(x_in[b], 16)
                sp.dma_start(x[b][:, :, :], x_tiles[img, :, :, bass.ds(g * GPX, GPX)]).then_inc(x_in[b], 16)
            if not tokens:
                sp.wait_ge(zero_ready, 1)
                for img in range(IMGS):
                    for row in (0, H + 1):
                        for h in range(PARTS_C):
                            sp.dma_start(k.xn_rows[h * P:(h + 1) * P, img, row, :],
                                         zeros[:, 0:W]).then_inc(zero_out, 16)
                        sp.dma_start(k.xn_pixels[img, row], zeros[0:W, :]).then_inc(zero_out, 16)
            over_tiles(sp, [(load, 0)])
            if tokens:
                sp.wait_ge(copied, TILES_ALL + CREDIT)
                sp.dma_start(k.table.rearrange("(t p) r -> p t r", p=P), k.node[:, :, 0:ROW]).then_inc(table_out, 16)
                sp.wait_ge(table_out, 16)
            else:
                sp.wait_ge(zero_out, 16 * IMGS * 2 * (PARTS_C + 1))

        @block.gpsimd
        def _(pool):
            pool.memset(zeros[:, :], 0.0).then_inc(zero_ready, 1)

        @block.tensor
        def _(pe):
            pe.sem_inc(var_ready, CREDIT)
            pe.sem_inc(posted, BUFS)

            def mean(img, g, n, u):
                b, c = u % BUFS, u % 2
                if tokens:
                    pe.wait_ge(summed, n + 1)
                else:
                    pe.wait_ge(x_in[b], (n - b) * (LOADED // BUFS) + LOADED)
                pe.wait_ge(centred, n + 1)
                for h in range(PARTS_C):
                    mm = pe.matmul(mean_ps[c][:, :], k.mean_c[:, :], x[b][:, h, :], start=(h == 0), stop=(h == 1))
                mm.then_inc(mean_ready, 1)

            def variance(img, g, n, u):
                c = u % 2
                pe.wait_ge(squared, n + 1)
                pe.wait_ge(spread_ready, n + 1)
                for h in range(PARTS_C):
                    mm = pe.matmul(var_ps[c][:, :], k.mean_c[:, :], square[c][:, h, :], start=(h == 0),
                                   stop=(h == 1))
                mm.then_inc(var_ready, 1)

            def post(img, g, n, u):
                b, c = u % BUFS, u % 2
                pe.wait_ge(normed, n + 1 + CREDIT)
                pe.wait_ge(copied, n + 1)
                if tokens:
                    for t in range(TILE_TOKENS):
                        for h in range(PARTS_C):
                            mm = pe.matmul(post_ps[c][:, t, :], y[b][:, h, t * P:(t + 1) * P],
                                           k.w_graph[:, h, :], start=(h == 0), stop=(h == 1))
                else:
                    for r in range(GROUP_ROWS):
                        for h in range(PARTS_C):
                            mm = pe.transpose(post_ps[c][:, r, h * P:(h + 1) * P], x[b][:, h, r * W:(r + 1) * W],
                                              k.ident[:, :])
                mm.then_inc(posted, 1)
            over_tiles(pe, [(mean, 0), (variance, 1), (post, 2)])

        @block.vector
        def _(dve):
            dve.sem_inc(centred, CREDIT)
            dve.sem_inc(normed, CREDIT)

            def add_conv(img, g, n, u):
                b = u % BUFS
                dve.wait_ge(x_in[b], (n - b) * (LOADED // BUFS) + LOADED)
                for h in range(PARTS_C):
                    dve.tensor_scalar(y[b][:, h, :], y[b][:, h, :], k.bn_scale[:, h:h + 1], k.bn_shift[:, h:h + 1],
                                      ALU.mult, ALU.add)
                dve.drain()
                dve.tensor_tensor(x[b][:, :, :], x[b][:, :, :], y[b][:, :, :], ALU.add).then_inc(summed, 1)

            def centre(img, g, n, u):
                b, c = u % BUFS, u % 2
                dve.wait_ge(mean_ready, n + 1)
                dve.tensor_tensor(y[b][:, :, :], x[b][:, :, :],
                                  mean_ps[c][:, :].unsqueeze(1).to_broadcast([P, PARTS_C, GPX]),
                                  ALU.subtract).then_inc(centred, 1)

            def normalise(img, g, n, u):
                b, c = u % BUFS, u % 2
                dve.wait_ge(spread_ready, n + 1 + CREDIT)
                dve.reciprocal(spread[c][:, :], spread[c][:, :])
                dve.drain()
                dve.tensor_tensor(y[b][:, :, :], y[b][:, :, :],
                                  spread[c][:, :].unsqueeze(1).to_broadcast([P, PARTS_C, GPX]),
                                  ALU.mult).then_inc(normed, 1)
            over_tiles(dve, ([(add_conv, 0)] if tokens else []) + [(centre, 1), (normalise, 2)])

        @block.scalar
        def _(act):
            act.sem_inc(spread_ready, CREDIT)
            act.sem_inc(copied, CREDIT)
            for b in range(BUFS):
                act.sem_inc(rows_out[b], 1)
                if tokens:
                    act.sem_inc(sums_out[b], 1)
            if not tokens:
                for c in range(2):
                    act.sem_inc(pixels_out[c], 1)

            def squares(img, g, n, u):
                b, c = u % BUFS, u % 2
                act.wait_ge(centred, n + 1 + CREDIT)
                act.wait_ge(var_ready, n + 1)
                act.activation(square[c][:, :, :], y[b][:, :, :], ACT.Square).then_inc(squared, 1)

            def root(img, g, n, u):
                c = u % 2
                act.wait_ge(var_ready, n + 1 + CREDIT)
                act.wait_ge(normed, n + 1)
                act.activation(spread[c][:, :], var_ps[c][:, :], ACT.Sqrt, bias=eps[:, :]).then_inc(spread_ready, 1)

            def store(img, g, n, u):
                b, c = u % BUFS, u % 2
                act.wait_ge(normed, n + 1 + CREDIT)
                for h in range(PARTS_C):
                    rows = (k.ln_rows if tokens else k.xn_rows)[h * P:(h + 1) * P, img]
                    rows = rows[:, bass.ds(g * GROUP_ROWS, GROUP_ROWS) if tokens else
                                bass.ds(g * GROUP_ROWS + 1, GROUP_ROWS), :]
                    act.dma_start(rows, y[b][:, h, :].rearrange("p (r w) -> p r w", w=W)).then_inc(rows_out[b], 16)
                if tokens:
                    act.dma_start(k.residual[img, :, :, bass.ds(g * GPX, GPX)], x[b][:, :, :]
                                  ).then_inc(sums_out[b], 16)
                act.wait_ge(posted, n + 1 + BUFS)
                if tokens:
                    act.activation(k.node[:, bass.ds(n * TILE_TOKENS, TILE_TOKENS), :], post_ps[c][:, :, :],
                                   ACT.Copy).then_inc(copied, 1)
                else:
                    act.wait_ge(pixels_out[c], (n - c) * (16 // 2) + 1)
                    act.activation(pixels[c][:, :, :], post_ps[c][:, :, :], ACT.Copy).then_inc(copied, 1)
                    act.wait_ge(copied, n + 1 + CREDIT)
                    act.dma_start(k.xn_pixels[img, bass.ds(g * GROUP_ROWS + 1, GROUP_ROWS)].rearrange(
                        "r w c -> w r c"), pixels[c][:, :, :]).then_inc(pixels_out[c], 16)
            over_tiles(act, [(squares, 1), (root, 2), (store, 3)])
            for b in range(BUFS):
                act.wait_ge(rows_out[b], TILES_ALL // BUFS * 16 * PARTS_C + 1)
                if tokens:
                    act.wait_ge(sums_out[b], TILES_ALL // BUFS * 16 + 1)
            if not tokens:
                for c in range(2):
                    act.wait_ge(pixels_out[c], TILES_ALL // 2 * 16 + 1)


def token_constants(nc, k):
    with ExitStack() as ctx:
        def sb(name, shape, dt):
            return ctx.enter_context(nc.sbuf_tensor("tc_" + name, shape, dt))

        def sem(name):
            return ctx.enter_context(nc.semaphore("tc_" + name))
        gamma, beta = sb("gamma", [P, PARTS_C], F32), sb("beta", [P, PARTS_C], F32)
        moments = sb("moments", [P, PARTS_C, 2], F32)
        spread = sb("spread", [P, PARTS_C], F32)
        gat_t = sb("gat_t", [HE, C], F32)
        attention = sb("attention", [HE, 2], F32)
        blocks = sb("blocks", [HE, 2, HEADS], F32)
        part_ps = [ctx.enter_context(nc.psum_tensor(f"tc_part{h}", [P, 2 * HEADS], F32)) for h in range(PARTS_C)]
        loaded, var_ready, root_ready, ones_ready, blocks_made, blocks_ready, parts_ready = (
            sem(n) for n in ("loaded", "var_ready", "root_ready", "ones_ready", "blocks_made", "blocks_ready",
                             "parts_ready"))
        block = ctx.enter_context(nc.Block())

        @block.sync
        def _(sp):
            with nc.allow_non_contiguous_dma(reason="a few hundred parameters"):
                sp.dma_start(gamma[:, :], k.gamma.rearrange("(h p) -> p h", p=P)).then_inc(loaded, 16)
                sp.dma_start(beta[:, :], k.beta.rearrange("(h p) -> p h", p=P)).then_inc(loaded, 16)
                sp.dma_start(gat_t[:, :], k.w_gat.rearrange("c o -> o c")).then_inc(loaded, 16)
                sp.dma_start(attention[:, 0:1], k.att_src.rearrange("h (e a) -> (h e) a", a=1)).then_inc(loaded, 16)
                sp.dma_start(attention[:, 1:2], k.att_dst.rearrange("h (e a) -> (h e) a", a=1)).then_inc(loaded, 16)
                sp.dma_start(k.w_graph[:, :, 0:HE], k.w_gat.rearrange("(h p) o -> p h o", p=P)).then_inc(loaded, 16)

        @block.gpsimd
        def _(pool):
            pool.memset(blocks[:, :, :], 1.0).then_inc(ones_ready, 1)
            pool.wait_ge(ones_ready, 1)
            pool.affine_select(out=blocks[:, :, :], in_=blocks[:, :, :], compare_op=ALU.is_ge, fill=0.0, base=0,
                               pattern=[[0, 2], [-EXPERTS, HEADS]], channel_multiplier=1).then_inc(blocks_made, 1)
            pool.wait_ge(blocks_made, 1)
            pool.affine_select(out=blocks[:, :, :], in_=blocks[:, :, :], compare_op=ALU.is_ge, fill=0.0,
                               base=EXPERTS - 1, pattern=[[0, 2], [EXPERTS, HEADS]],
                               channel_multiplier=-1).then_inc(blocks_made, 1)

        @block.vector
        def _(dve):
            for h in range(PARTS_C):
                dve.bn_aggr(moments[:, h, :], k.y_stats[:, h, :, :].rearrange("p n s -> p (n s)"))
            dve.wait_ge(loaded, 96)
            dve.wait_ge(blocks_made, 2)
            for s in range(2):
                last = dve.tensor_scalar(blocks[:, s, :], blocks[:, s, :], attention[:, s:s + 1], None, ALU.mult)
            last.then_inc(blocks_ready, 1)
            dve.drain()
            dve.tensor_scalar(spread[:, :], moments[:, :, 1], BN_EPS, None, ALU.add).then_inc(var_ready, 1)
            dve.wait_ge(root_ready, 1)
            dve.reciprocal(spread[:, :], spread[:, :])
            dve.drain()
            dve.tensor_tensor(k.bn_scale[:, :], spread[:, :], gamma[:, :], ALU.mult)
            dve.drain()
            dve.tensor_tensor(spread[:, :], moments[:, :, 0], k.bn_scale[:, :], ALU.mult)
            dve.drain()
            dve.tensor_tensor(k.bn_shift[:, :], beta[:, :], spread[:, :], ALU.subtract)
            dve.wait_ge(parts_ready, 1)
            for h in range(PARTS_C):
                dve.tensor_copy(k.w_graph[:, h, HE:NODE], part_ps[h][:, :])

        @block.scalar
        def _(act):
            act.wait_ge(var_ready, 1)
            act.activation(spread[:, :], spread[:, :], ACT.Sqrt).then_inc(root_ready, 1)

        @block.tensor
        def _(pe):
            pe.wait_ge(loaded, 96)
            pe.wait_ge(blocks_ready, 1)
            for h in range(PARTS_C):
                mm = pe.matmul(part_ps[h][:, :], gat_t[:, h * P:(h + 1) * P],
                               blocks[:, :, :].rearrange("p s h -> p (s h)"), start=True, stop=True)
            mm.then_inc(parts_ready, 1)


def guide_taps(nc, k):
    with ExitStack() as ctx:
        def sb(name, shape, dt):
            return ctx.enter_context(nc.sbuf_tensor(name, shape, dt))

        def sem(name):
            return ctx.enter_context(nc.semaphore(name))
        w_cat = sb("gt_w_cat", [P, PARTS_C, TAPS, GUIDES], F32)
        strip = [sb(f"gt_strip{u}", [P, PARTS_C, GROUP_ROWS + 2, W + 2], F32) for u in range(2)]
        guide = [sb(f"gt_guide{u}", [GUIDES, GPX], F32) for u in range(2)]
        SETS = 2
        SOFTMAXES = GROUP_ROWS * BRANCHES
        highest = sb("gt_highest", [W, SOFTMAXES], F32)
        total = sb("gt_total", [W, SOFTMAXES], F32)
        weight = [sb(f"gt_weight{u}", [W, SOFTMAXES, TAPS], F32) for u in range(2)]
        rest = sb("gt_rest", [W, GROUP_ROWS, GUIDES], F32)
        parts = [sb(f"gt_parts{u}", [W, GROUP_ROWS, SPLITS * GUIDES], BF16) for u in range(2)]
        left = [sb(f"gt_left{u}", [SPLITS * LEFT, GPX], BF16) for u in range(2)]
        right = [sb(f"gt_right{u}", [SPLITS * RIGHT, GPX], BF16) for u in range(2)]
        conv_ps = [ctx.enter_context(nc.psum_tensor(f"gt_conv{u}", [GUIDES, GPX], F32)) for u in range(2)]
        pixel_ps = [ctx.enter_context(nc.psum_tensor(f"gt_pixel{u}", [W, SOFTMAXES, TAPS], F32)) for u in range(2)]
        left_ps = [ctx.enter_context(nc.psum_tensor(f"gt_left_ps{u}", [SPLITS * LEFT, GPX], BF16)) for u in range(2)]
        right_ps = [ctx.enter_context(nc.psum_tensor(f"gt_right_ps{u}", [SPLITS * RIGHT, GPX], BF16))
                    for u in range(2)]
        w_in = sem("gt_w_in")
        strip_in = [sem(f"gt_strip_in{u}") for u in range(2)]
        left_out = [sem(f"gt_left_out{u}") for u in range(2)]
        right_out = [sem(f"gt_right_out{u}") for u in range(2)]
        edges_zero, conv_ready, guide_ready, pixel_ready, shifted, raised, parts_ready, taps_ready, taps_copied = (
            sem("gt_" + n) for n in ("edges_zero", "conv_ready", "guide_ready", "pixel_ready", "shifted", "raised",
                                     "parts_ready", "taps_ready", "taps_copied"))
        block = ctx.enter_context(nc.Block())

        @block.sync
        def _(sp):
            sp.dma_start(w_cat[:, :, :, :], k.w_cat_t.rearrange("(h p) t o -> p h t o", p=P)).then_inc(w_in, 16)
            sp.wait_ge(edges_zero, 1)

            def body(img, g, n, u):
                sp.wait_ge(conv_ready, n + 1)
                for h in range(PARTS_C):
                    sp.dma_start(strip[u % 2][:, h, :, 1:W + 1],
                                 k.xn_rows[h * P:(h + 1) * P, img, bass.ds(g * GROUP_ROWS, GROUP_ROWS + 2), :]
                                 ).then_inc(strip_in[u % 2], 16)
            over_tiles(sp, [(body, 0)])

        @block.tensor
        def _(pe):
            for freed in (conv_ready, pixel_ready, taps_ready):
                pe.sem_inc(freed, SETS)
            pe.wait_ge(w_in, 16)

            def conv(img, g, n, u):
                b = u % 2
                pe.wait_ge(strip_in[b], (n - b) * 16 + 32)
                pe.wait_ge(guide_ready, n + 1)
                step = 0
                for h in range(PARTS_C):
                    for t in range(TAPS):
                        dy, dx = t // 3, t % 3
                        mm = pe.matmul(conv_ps[b][:, :], w_cat[:, h, t, :],
                                       strip[b][:, h, dy:dy + GROUP_ROWS, dx:dx + W],
                                       start=(step == 0), stop=(step == PARTS_C * TAPS - 1))
                        step += 1
                mm.then_inc(conv_ready, 1)

            def to_pixels(img, g, n, u):
                b = u % 2
                pe.wait_ge(guide_ready, n + 1 + SETS)
                wait_alone(pe, shifted, n + 1, k.passed)
                for r in range(GROUP_ROWS):
                    mm = pe.transpose(pixel_ps[b][:, r * BRANCHES:(r + 1) * BRANCHES, :].rearrange("p a b -> p (a b)"),
                                      guide[b][:, r * W:(r + 1) * W], k.ident[0:GUIDES, 0:GUIDES])
                mm.then_inc(pixel_ready, 1)

            def to_rows(img, g, n, u):
                b = u % 2
                pe.wait_ge(parts_ready, n + 1)
                pe.wait_ge(taps_copied, n + 1)
                for r in range(GROUP_ROWS):
                    pe.transpose(left_ps[b][:, r * W:(r + 1) * W], parts[b][:, r, 0:SPLITS * LEFT], k.ident_b[0:W, 0:W])
                    mm = pe.transpose(right_ps[b][:, r * W:(r + 1) * W], parts[b][:, r, SPLITS * LEFT:],
                                      k.ident_b[0:W, 0:W])
                mm.then_inc(taps_ready, 1)
            over_tiles(pe, [(conv, 0), (to_pixels, 1), (to_rows, 2)])

        @block.scalar
        def _(act):
            act.sem_inc(guide_ready, SETS)
            act.sem_inc(taps_copied, SETS)
            for b in range(2):
                act.sem_inc(left_out[b], 1)
                act.sem_inc(right_out[b], 1)
            def copy_guide(img, g, n, u):
                b = u % 2
                act.wait_ge(conv_ready, n + 1 + SETS)
                act.wait_ge(pixel_ready, n + 1)
                act.activation(guide[b][:, :], conv_ps[b][:, :], ACT.Copy).then_inc(guide_ready, 1)

            def exponent(img, g, n, u):
                act.wait_ge(shifted, n + 1 + SETS)
                act.activation(weight[u % 2][:, :, :], weight[u % 2][:, :, :], ACT.Exp).then_inc(raised, 1)

            def copy_taps(img, g, n, u):
                b = u % 2
                act.wait_ge(taps_ready, n + 1 + SETS)
                act.wait_ge(left_out[b], (n - b) * 8 + 1)
                act.wait_ge(right_out[b], (n - b) * 8 + 1)
                act.activation(left[b][:, :], left_ps[b][:, :], ACT.Copy)
                act.activation(right[b][:, :], right_ps[b][:, :], ACT.Copy).then_inc(taps_copied, 1)
                act.wait_ge(taps_copied, n + 1 + SETS)
                act.dma_start(k.taps_left[:, bass.ds(g * GPX + img * PIX, GPX)], left[b][:, :]).then_inc(left_out[b], 16)
                act.dma_start(k.taps_right[:, bass.ds(g * GPX + img * PIX, GPX)],
                              right[b][:, :]).then_inc(right_out[b], 16)
            over_tiles(act, [(copy_guide, 0), (exponent, 1), (copy_taps, 2)])
            for b in range(2):
                act.wait_ge(left_out[b], IMGS * ROW_GROUPS * 8 + 1)
                act.wait_ge(right_out[b], IMGS * ROW_GROUPS * 8 + 1)

        @block.vector
        def _(dve):
            for b in range(2):
                dve.memset(strip[b][:, :, :, :], 0.0)
            dve.drain()
            dve.sem_inc(edges_zero, 1)
            dve.sem_inc(shifted, SETS)

            def body(img, g, n, u):
                b = u % 2
                dve.wait_ge(pixel_ready, n + 1 + SETS)
                dve.tensor_reduce(highest[:, :], pixel_ps[b][:, :, :], AX_X, ALU.max)
                dve.drain()
                dve.tensor_tensor(weight[b][:, :, :], pixel_ps[b][:, :, :],
                                  highest[:, :].unsqueeze(2).to_broadcast([W, SOFTMAXES, TAPS]),
                                  ALU.subtract).then_inc(shifted, 1)
                dve.wait_ge(raised, n + 1)
                dve.tensor_reduce(total[:, :], weight[b][:, :, :], AX_X, ALU.add)
                dve.drain()
                dve.reciprocal(total[:, :], total[:, :])
                dve.drain()
                dve.tensor_tensor(weight[b][:, :, :], weight[b][:, :, :],
                                  total[:, :].unsqueeze(2).to_broadcast([W, SOFTMAXES, TAPS]), ALU.mult)
                dve.drain()
                dve.wait_ge(taps_ready, n + 1)
                value = weight[b][:, :, :].rearrange("p (r i) t -> p r (i t)", i=BRANCHES)
                for s in range(SPLITS):
                    at = SPLITS * LEFT + s * RIGHT
                    lots = ((slice(0, LEFT), parts[b][:, :, s * LEFT:(s + 1) * LEFT]),
                            (slice(LEFT, GUIDES), parts[b][:, :, at:at + RIGHT]))
                    for lot, part in lots:
                        dve.tensor_copy(part, value[:, :, lot])
                    dve.drain()
                    if s < SPLITS - 1:
                        for lot, part in lots:
                            dve.tensor_tensor(rest[:, :, lot], value[:, :, lot], part, ALU.subtract)
                        dve.drain()
                        value = rest[:, :, :]
                dve.sem_inc(parts_ready, 1)
            over_tiles(dve, [(body, 0)])


CLASSES = 6
CLASS_ROWS = H // CLASSES
CLASS_GROUPS = CLASS_ROWS // GROUP_ROWS


def branch_masks(nc, k):
    with ExitStack() as ctx:
        zeroed = ctx.enter_context(nc.semaphore("bm_zeroed"))
        made = ctx.enter_context(nc.semaphore("bm_made"))
        wide = ctx.enter_context(nc.sbuf_tensor("bm_wide", [W, len(k.offsets), GPX], F32))
        block = ctx.enter_context(nc.Block())

        @block.gpsimd
        def _(pool):
            pool.memset(wide[:, :, :], 0.0)
            pool.memset(k.pick_left[:, :, :], 0.0)
            pool.memset(k.pick_right[:, :, :], 0.0).then_inc(zeroed, 1)
            pool.wait_ge(zeroed, 1)
            for n, dx in enumerate(k.offsets):
                v = wide[:, n, :].rearrange("p (r w) -> p r w", w=W)
                pool.affine_select(out=v, in_=v, compare_op=ALU.not_equal, fill=1.0, base=-dx,
                                   pattern=[[0, GROUP_ROWS], [-1, W]], channel_multiplier=1)
            for pick, taps in ((k.pick_left, LEFT), (k.pick_right, RIGHT)):
                for s in range(SPLITS):
                    pool.affine_select(out=pick[:, :, :], in_=pick[:, :, :], compare_op=ALU.not_equal, fill=1.0,
                                       base=-s * taps, pattern=[[-1, taps], [0, W]], channel_multiplier=1
                                       ).then_inc(made, 1)
                    pool.wait_ge(made, (s + 1) if taps == LEFT else SPLITS + s + 1)

        @block.vector
        def _(dve):
            dve.wait_ge(made, 1)
            dve.tensor_copy(k.masks[:, :, :], wide[:, :, :])


def dilated_branches(nc, k):
    SETS = 2
    PAIR = 2
    assert CLASSES % PAIR == 0
    with ExitStack() as ctx:
        def sb(name, shape, dt):
            return ctx.enter_context(nc.sbuf_tensor(name, shape, dt))

        def sem(name):
            return ctx.enter_context(nc.semaphore(name))
        w_scale = sb("db_w_scale", [P, (BRANCHES + 1) * PARTS_C, C], F32)
        own, above, below = ([sb(f"db_{name}{c}", [W, CLASS_ROWS, C], F32) for c in range(PAIR)]
                             for name in ("own", "above", "below"))
        rows = [sb(f"db_rows{c}", [P, PARTS_C, CLASS_ROWS, W], F32) for c in range(PAIR)]
        left = [sb(f"db_left{c}", [SPLITS * LEFT, CLASS_ROWS, W], BF16) for c in range(PAIR)]
        right = [sb(f"db_right{c}", [SPLITS * RIGHT, CLASS_ROWS, W], BF16) for c in range(PAIR)]
        diagonals = [sb(f"db_diagonals{i}", [W, 3, GPX], F32) for i in range(BRANCHES)]
        branch = [sb(f"db_branch{u}", [P, PARTS_C, GPX], F32) for u in range(SETS)]
        y = [sb(f"db_y{u}", [P, PARTS_C, GPX], F32) for u in range(SETS)]
        tap_ps = [ctx.enter_context(nc.psum_tensor(f"db_tap{u}", [W, GPX], F32)) for u in range(2)]
        branch_ps = [[ctx.enter_context(nc.psum_tensor(f"db_branch_ps{u}{h}", [P, GPX], F32))
                      for h in range(PARTS_C)] for u in range(2)]
        y_ps = [ctx.enter_context(nc.psum_tensor(f"db_y_ps{h}", [P, GPX], F32)) for h in range(PARTS_C)]
        w_in, y_copied, y_used = (sem("db_" + n) for n in ("w_in", "y_copied", "y_used"))
        class_in = [sem(f"db_class_in{c}") for c in range(PAIR)]
        zeroed, tap_ready, tap_placed, branch_ready, branch_copied, branch_used = (
            sem("db_" + n) for n in ("zeroed", "tap_ready", "tap_placed", "branch_ready", "branch_copied",
                                     "branch_used"))
        y_out = [sem(f"db_y_out{u}") for u in range(SETS)]
        LOADS = 3 + PARTS_C + 2
        CLASS_STEPS = CLASS_GROUPS * BRANCHES
        STEPS = PAIR * CLASS_STEPS
        GROUPS = PAIR * CLASS_GROUPS
        USED = CLASS_STEPS + SETS
        block = ctx.enter_context(nc.Block())

        def class_pairs(eng, body):
            for img in range(IMGS):
                with eng.Fori(0, CLASSES // PAIR) as i:
                    body(img, i, i + img * (CLASSES // PAIR))

        def place(step):
            group, b = divmod(step, BRANCHES)
            return group // CLASS_GROUPS, group % CLASS_GROUPS, b

        @block.sync
        def _(sp):
            sp.dma_start(w_scale[:, :, :], k.w_scale_t.rearrange("(c p) o -> p c o", p=P)).then_inc(w_in, 16)

            def body(img, i, n):
                for c in range(PAIR):
                    r = i * PAIR + c
                    wait_alone(sp, branch_used, n * STEPS + (USED + (c - 1) * CLASS_STEPS), k.passed)
                    pixels = k.xn_pixels[img, 0:H].rearrange("(k s) w c -> w s k c", s=CLASSES)
                    pixels_1 = k.xn_pixels[img, 1:H + 1].rearrange("(k s) w c -> w s k c", s=CLASSES)
                    pixels_2 = k.xn_pixels[img, 2:H + 2].rearrange("(k s) w c -> w s k c", s=CLASSES)
                    for tile, source in ((above[c], pixels), (own[c], pixels_1), (below[c], pixels_2)):
                        sp.dma_start(tile[:, :, :], source[:, bass.ds(r, 1), :, :].rearrange(
                            "w s k c -> w (s k) c")).then_inc(class_in[c], 16)
                    by_rows = k.xn_rows[:, img, 1:H + 1, :].rearrange("(h p) (k s) w -> p h s k w", p=P, s=CLASSES)
                    for h in range(PARTS_C):
                        sp.dma_start(rows[c][:, h, :, :], by_rows[:, h, bass.ds(r, 1), :, :].rearrange(
                            "p s k w -> p (s k) w")).then_inc(class_in[c], 16)
                    for tile, source in ((left[c], k.taps_left), (right[c], k.taps_right)):
                        v = source[:, img * PIX:(img + 1) * PIX].rearrange("t (k s w) -> t s k w", s=CLASSES, w=W)
                        sp.dma_start(tile[:, :, :], v[:, bass.ds(r, 1), :, :].rearrange("t s k w -> t (s k) w")
                                     ).then_inc(class_in[c], 16)
            class_pairs(sp, body)

        @block.tensor
        def _(pe):
            pe.wait_ge(w_in, 16)
            pe.wait_ge(zeroed, 1)
            pe.sem_inc(branch_used, USED)

            def body(img, i, n):
                def spread_tap(step, at):
                    c, q, b = place(step)
                    if step % CLASS_STEPS == 0 and at == 0:
                        pe.wait_ge(class_in[c], n * (16 * LOADS) + 16 * LOADS)
                    m = step * TAPS + at
                    t = at % 3 * 3 + at // 3
                    pick, taps, base = ((k.pick_left, left[c], b * TAPS) if b < LEFT_BRANCHES else
                                        (k.pick_right, right[c], (b - LEFT_BRANCHES) * TAPS))
                    pe.wait_ge(tap_placed, n * (STEPS * TAPS) + m + 1)
                    pe.matmul(tap_ps[m % 2][:, :], pick[:, base + t, :],
                              taps[:, q * GROUP_ROWS:(q + 1) * GROUP_ROWS, :],
                              start=True, stop=True).then_inc(tap_ready, 1)

                def gather_rows(step):
                    c, q, b = place(step)
                    jump = DILATIONS[b] // CLASSES
                    pe.wait_ge(branch_copied, n * STEPS + step + 1)
                    pe.wait_ge(tap_placed, n * (STEPS * TAPS) + (step + 1) * TAPS + 2)
                    spreads = TAPS if step + 1 < STEPS else 0
                    parts = PARTS_C * GROUP_ROWS
                    for h in range(PARTS_C):
                        for i in range(GROUP_ROWS):
                            row = q * GROUP_ROWS + i
                            if DILATIONS[b] == 1:
                                used = [(0, above[c], row), (1, own[c], row), (2, below[c], row)]
                            else:
                                used = [(dy, own[c], row + (dy - 1) * jump) for dy in range(3)
                                        if 0 <= row + (dy - 1) * jump < CLASS_ROWS]
                            for at, (dy, tile, source) in enumerate(used):
                                mm = pe.matmul(branch_ps[step % 2][h][:, i * W:(i + 1) * W],
                                               tile[:, source, h * P:(h + 1) * P],
                                               diagonals[b][:, dy, i * W:(i + 1) * W],
                                               start=(at == 0), stop=(at == len(used) - 1))
                            done = h * GROUP_ROWS + i
                            if done == parts - 1:
                                mm.then_inc(branch_ready, 1)
                            for at in range(spreads * done // parts, spreads * (done + 1) // parts):
                                spread_tap(step + 1, at)

                def scale(step):
                    c, q, b = place(step)
                    if b == 0:
                        pe.wait_ge(y_copied, n * GROUPS + (c * CLASS_GROUPS + q + 1))
                        for o in range(PARTS_C):
                            for h in range(PARTS_C):
                                pe.matmul(y_ps[o][:, :], w_scale[:, h, o * P:(o + 1) * P],
                                          rows[c][:, h, q * GROUP_ROWS:(q + 1) * GROUP_ROWS, :],
                                          start=(h == 0), stop=False)
                    pe.wait_ge(branch_copied, n * STEPS + step + 1 + SETS)
                    for o in range(PARTS_C):
                        for h in range(PARTS_C):
                            last = b == BRANCHES - 1 and h == PARTS_C - 1
                            mm = pe.matmul(y_ps[o][:, :], w_scale[:, (b + 1) * PARTS_C + h, o * P:(o + 1) * P],
                                           branch[step % 2][:, h, :], start=False, stop=last)
                    mm.then_inc(branch_used, 1)

                for at in range(TAPS):
                    spread_tap(0, at)
                for step in range(STEPS):
                    gather_rows(step)
                    if step >= 1:
                        scale(step - 1)
                scale(STEPS - 1)
            class_pairs(pe, body)

        @block.vector
        def _(dve):
            for b in range(BRANCHES):
                dve.memset(diagonals[b][:, :, :], 0.0)
            dve.drain()
            dve.sem_inc(zeroed, 1)
            dve.sem_inc(tap_placed, 2)

            def body(img, i, n):
                for step in range(STEPS):
                    c, q, b = place(step)
                    for at in range(TAPS):
                        dx, dy = divmod(at, 3)
                        m = step * TAPS + at
                        if dy == 0:
                            dve.drain()
                        mask = k.offsets.index((dx - 1) * DILATIONS[b])
                        wait_alone(dve, tap_ready, n * (STEPS * TAPS) + m + 1, k.passed)
                        dve.copy_predicated(diagonals[b][:, dy, :], k.masks[:, mask, :],
                                            tap_ps[m % 2][:, :]).then_inc(tap_placed, 1)
                    if b == 1 and step >= BRANCHES:
                        statistics(n, step // BRANCHES - 1)
                statistics(n, GROUPS - 1)

            def statistics(n, q):
                dve.wait_ge(y_copied, n * GROUPS + q + 2)
                for h in range(PARTS_C):
                    last = dve.bn_stats(k.y_stats[:, h, bass.ds(n * GROUPS + q, 1), :].rearrange(
                        "p a s -> p (a s)"), y[q % 2][:, h, :])
                last.then_inc(y_used, 1)
            class_pairs(dve, body)

        @block.scalar
        def _(act):
            act.sem_inc(y_used, 2)
            act.sem_inc(branch_copied, SETS)
            act.sem_inc(y_copied, 1)
            for u in range(SETS):
                act.sem_inc(y_out[u], 1)

            def body(img, i, n):
                for step in range(STEPS):
                    act.wait_ge(branch_ready, n * STEPS + step + 1)
                    act.wait_ge(branch_used, n * STEPS + (step + 1 + CLASS_STEPS))
                    for h in range(PARTS_C):
                        last = act.activation(branch[step % 2][:, h, :], branch_ps[step % 2][h][:, :], ACT.Copy)
                    last.then_inc(branch_copied, 1)
                    if step % BRANCHES == 0 and step >= BRANCHES:
                        copy_y(img, i, n, step // BRANCHES - 1)
                copy_y(img, i, n, GROUPS - 1)

            def copy_y(img, i, n, group):
                c, q = divmod(group, CLASS_GROUPS)
                act.wait_ge(branch_used, n * STEPS + ((group + 1) * BRANCHES + USED))
                act.wait_ge(y_used, n * GROUPS + group + 1)
                act.wait_ge(y_out[q % 2], n * (16 * PARTS_C * GROUPS // 2) + 16 * PARTS_C * (group // 2) + 1)
                for h in range(PARTS_C):
                    last = act.activation(y[q % 2][:, h, :], y_ps[h][:, :], ACT.Copy)
                last.then_inc(y_copied, 1)
                act.wait_ge(y_copied, n * GROUPS + group + 2)
                for h in range(PARTS_C):
                    v = k.conv_out[h * P:(h + 1) * P, img, :, :].rearrange("p (k s) w -> p s k w", s=CLASSES)
                    act.dma_start(v[:, bass.ds(i * PAIR + c, 1), q * GROUP_ROWS:(q + 1) * GROUP_ROWS, :].rearrange(
                        "p s k w -> p (s k) w"), y[q % 2][:, h, :].rearrange("p (k w) -> p k w", w=W)
                        ).then_inc(y_out[q % 2], 16)
            class_pairs(act, body)
            for u in range(2):
                act.wait_ge(y_out[u], IMGS * CLASSES * PARTS_C * CLASS_GROUPS // 2 * 16 + 1)


LEAK = 0.2
FAR = 1e30


def place_scores(nc, k):
    with ExitStack() as ctx:
        placed = ctx.enter_context(nc.semaphore("ps_placed"))
        scores = ctx.enter_context(nc.sbuf_tensor("ps_scores", [P, TILES, HEADS], F32))
        scores_ready = ctx.enter_context(nc.semaphore("ps_scores_ready"))
        block = ctx.enter_context(nc.Block())

        @block.vector
        def _(dve):
            dve.tensor_copy(scores[:, :, :], k.node[:, :, HE + HEADS:NODE]).then_inc(scores_ready, 1)

        @block.gpsimd
        def _(pool):
            pool.wait_ge(scores_ready, 1)
            for t in range(TILES):
                pool.indirect_dma_start(k.dst_scores[:, :],
                                        bass.IndirectOffsetOnAxis(k.first_place[:, t:t + 1], 0),
                                        scores[:, t, :], None, bounds_check=E - 1,
                                        oob_is_err=False).then_inc(placed, 16)
            pool.wait_ge(placed, 16 * TILES)


def edge_softmax(nc, k):
    SUMS = HE + HEADS
    with ExitStack() as ctx:
        def sb(name, shape, dt):
            return ctx.enter_context(nc.sbuf_tensor("es_" + name, shape, dt))

        def sem(name):
            return ctx.enter_context(nc.semaphore("es_" + name))

        def ps(name, shape):
            return ctx.enter_context(nc.psum_tensor("es_" + name, shape, F32))
        keys, before = sb("keys", [P, P], I32), sb("before", [P, P], I32)
        given = sb("given", [P, P, HEADS], F32)
        run, run_before = sb("run", [P, P], I32), sb("run_before", [P, P], I32)
        source_i = sb("source_i", [P, P], I32)
        source = sb("source", [P, P], U32)
        fetched = sb("fetched", [P, P, ROW], F32)
        same_next = sb("same_next", [P, P], F32)
        given_next = sb("given_next", [P, HEADS, P], F32)
        same = sb("same", [P, HEADS, P], F32)
        given_row = sb("given_row", [P, HEADS, P], F32)
        first = sb("first", [P, 4], F32)
        penalty = sb("penalty", [P, HEADS, P], F32)
        src_score = sb("src_score", [P, HEADS, P], F32)
        dst_score = sb("dst_score", [P, HEADS, P], F32)
        score = sb("score", [P, HEADS, P], F32)
        score_0 = sb("score_0", [P, HEADS], F32)
        peak = sb("peak", [P, HEADS, P], F32)
        peak_in = sb("peak_in", [P, HEADS], F32)
        powers = sb("powers", [P, 2 * HEADS * P + HEADS], F32)
        decay = powers[:, 0:HEADS * P].rearrange("p (h j) -> p h j", h=HEADS)
        weight = powers[:, HEADS * P:2 * HEADS * P].rearrange("p (h j) -> p h j", h=HEADS)
        decay_all = powers[:, 2 * HEADS * P:]
        decay_0 = sb("decay_0", [P, SUMS], F32)
        value = sb("value", [P, SUMS, P], F32)
        value_decay = sb("value_decay", [P, SUMS, P], F32)
        sums = sb("sums", [P, SUMS, P], F32)
        ends = sb("ends", [P, 2, SUMS], F32)
        rows_out = sb("rows_out", [P, P, NODE], F32)
        factor_row = sb("factor_row", [SUMS, P], F32)
        handed = [sb("handed_score", [HEADS, P + 1], F32), sb("handed_peak", [HEADS, P + 1], F32),
                  sb("handed_sums", [SUMS, P + 1], F32)]
        turned_ps = ps("turned_ps", [SUMS, 2, P])
        back_ps = ps("back_ps", [P, SUMS])
        (chunk_in, decoded, source_ready, fetched_all, rows_taken, ends_ready, ends_turned, handed_ready,
         handed_turned, powers_ready, raised, rows_ready, stored) = (sem(n) for n in (
             "chunk_in", "decoded", "source_ready", "fetched_all", "rows_taken", "ends_ready", "ends_turned",
             "handed_ready", "handed_turned", "powers_ready", "raised", "rows_ready", "stored"))
        block = ctx.enter_context(nc.Block())

        def over_chunks(eng, body):
            own = eng.value_load(k.own_edges[0:1, 0:1], min_val=1, max_val=E)
            with eng.Fori(0, CHUNKS) as c:
                with eng.If(c * CHUNK < own):
                    body(c)

        @block.sync
        def _(sp):
            def load(c):
                sp.dma_start(keys[:, :], k.sorted_keys[bass.ds(c * CHUNK + P, CHUNK)].rearrange(
                    "(p f) -> p f", p=P)).then_inc(chunk_in, 16)
                sp.dma_start(before[:, :], k.sorted_keys[bass.ds(c * CHUNK + (P - 1), CHUNK)].rearrange(
                    "(p f) -> p f", p=P)).then_inc(chunk_in, 16)
                sp.dma_start(given[:, :, :], k.dst_scores[bass.ds(c * CHUNK, CHUNK), :].rearrange(
                    "(p f) h -> p f h", p=P)).then_inc(chunk_in, 16)
            load(0)
            sp.sem_inc(stored, 1)

            def body(c):
                wait_alone(sp, decoded, c + 1, k.passed)
                load(c + 1)
                wait_alone(sp, rows_ready, c + 1, k.passed)
                sp.dma_start(k.states[bass.ds(c * CHUNK, CHUNK), :].rearrange("(p f) r -> p f r", p=P),
                             rows_out[:, :, :]).then_inc(stored, 16)
                wait_alone(sp, stored, c * 16 + 17, k.passed)
            over_chunks(sp, body)
            sp.wait_ge(chunk_in, 48)

        @block.gpsimd
        def _(pool):
            def body(c):
                wait_alone(pool, rows_taken, c + 1, k.passed)
                wait_alone(pool, source_ready, c + 1, k.passed)
                for j in range(P):
                    pool.indirect_dma_start(fetched[:, j, :], None, k.table[:, :],
                                            bass.IndirectOffsetOnAxis(source[:, j:j + 1], 0)
                                            ).then_inc(fetched_all, 16)
            over_chunks(pool, body)

        @block.scalar
        def _(act):
            def body(c):
                act.wait_ge(powers_ready, c + 1)
                act.activation(powers[:, :], powers[:, :], ACT.Exp).then_inc(raised, 1)
            over_chunks(act, body)

        @block.tensor
        def _(pe):
            def body(c):
                for r, channels in enumerate((HEADS, HEADS, SUMS)):
                    wait_alone(pe, ends_ready, c * 3 + r + 1, k.passed)
                    for i in range(2):
                        mm = pe.transpose(turned_ps[0:channels, i, :], ends[:, i, 0:channels], k.ident[:, :])
                    mm.then_inc(ends_turned, 1)
                    wait_alone(pe, handed_ready, c * 3 + r + 1, k.passed)
                    pe.transpose(back_ps[:, 0:channels], handed[r][:, 0:P],
                                 k.ident[0:channels, 0:channels]).then_inc(handed_turned, 1)
            over_chunks(pe, body)

        @block.vector
        def _(dve):
            def flat(t):
                return t[:, :, :].rearrange("p c j -> p (c j)")

            def decode(c):
                dve.wait_ge(chunk_in, c * 48 + 48)
                dve.tensor_scalar(run[:, :], keys[:, :], SRC_BITS, None, ALU.logical_shift_right)
                dve.tensor_scalar(run_before[:, :], before[:, :], SRC_BITS, None, ALU.logical_shift_right)
                dve.tensor_scalar(source_i[:, :], keys[:, :], SRC_MASK, None, ALU.bitwise_and)
                dve.tensor_copy(given_next[:, :, :], given[:, :, :].rearrange("p j h -> p h j"))
                dve.drain().then_inc(decoded, 1)
                dve.tensor_scalar(source[:, :], source_i[:, :], float(TOK - 1), None, ALU.min).then_inc(source_ready, 1)
                dve.tensor_tensor(same_next[:, :], run[:, :], run_before[:, :], ALU.is_equal)
                dve.drain()

            def hand_on(c, r, channels, initial_op, op):
                dve.drain().then_inc(ends_ready, 1)
                dve.wait_ge(ends_turned, c * 3 + r + 1)
                dve.tensor_copy(factor_row[0:channels, :], turned_ps[0:channels, 1, :])
                dve.tensor_copy(handed[r][:, 0:1], handed[r][:, P:P + 1])
                dve.drain()
                dve.tensor_tensor_scan(handed[r][:, 1:P + 1], factor_row[0:channels, :], turned_ps[0:channels, 0, :],
                                       handed[r][:, 0:1], initial_op, op).then_inc(handed_ready, 1)
                dve.wait_ge(handed_turned, c * 3 + r + 1)

            dve.sem_inc(rows_taken, 1)
            for r, start in enumerate((0.0, -FAR, 0.0)):
                dve.memset(handed[r][:, :], start)
            dve.drain()
            decode(0)

            def body(c):
                wait_alone(dve, fetched_all, c * (16 * P) + 16 * P, k.passed)
                dve.tensor_copy(value[:, 0:HE, :], fetched[:, :, 0:HE].rearrange("p j v -> p v j"))
                dve.tensor_copy(src_score[:, :, :], fetched[:, :, HE:ROW].rearrange("p j v -> p v j"))
                dve.tensor_copy(same[:, :, :], same_next[:, :].unsqueeze(1).to_broadcast([P, HEADS, P]))
                dve.tensor_copy(given_row[:, :, :], given_next[:, :, :])
                dve.tensor_copy(first[:, 0:1], same_next[:, 0:1])
                dve.tensor_reduce(first[:, 2:3], same_next[:, :], AX_X, ALU.min)
                dve.drain().then_inc(rows_taken, 1)
                decode(c + 1)
                dve.memset(same[:, :, 0:1], 0.0)
                for i in (0, 2):
                    dve.tensor_scalar(first[:, i + 1:i + 2], first[:, i:i + 1], -1.0, FAR, ALU.add, ALU.mult)
                dve.drain()

                dve.tensor_scalar(penalty[:, :, :], same[:, :, :], -1.0, FAR, ALU.add, ALU.mult)
                dve.tensor_tensor_scan(flat(dst_score), flat(same), flat(given_row), 0.0, ALU.mult, ALU.add)
                dve.drain()
                dve.tensor_copy(ends[:, 0, 0:HEADS], dst_score[:, :, P - 1])
                dve.tensor_copy(ends[:, 1, 0:HEADS], first[:, 2:3].to_broadcast([P, HEADS]))
                hand_on(c, 0, HEADS, ALU.mult, ALU.add)
                dve.scalar_tensor_tensor(given_row[:, :, 0], back_ps[:, 0:HEADS], first[:, 0:1], given_row[:, :, 0],
                                         ALU.mult, ALU.add)
                dve.drain()
                dve.tensor_tensor_scan(flat(dst_score), flat(same), flat(given_row), 0.0, ALU.mult, ALU.add)
                dve.drain()

                dve.tensor_tensor(dst_score[:, :, :], dst_score[:, :, :], src_score[:, :, :], ALU.add)
                dve.drain()
                dve.scalar_tensor_tensor(score[:, :, :], dst_score[:, :, :], LEAK, dst_score[:, :, :], ALU.mult,
                                         ALU.max)
                dve.drain()
                dve.tensor_tensor_scan(flat(peak), flat(penalty), flat(score), -FAR, ALU.add, ALU.max)
                dve.tensor_copy(score_0[:, :], score[:, :, 0])
                dve.drain()
                dve.tensor_copy(ends[:, 0, 0:HEADS], peak[:, :, P - 1])
                dve.tensor_copy(ends[:, 1, 0:HEADS], first[:, 3:4].to_broadcast([P, HEADS]))
                hand_on(c, 1, HEADS, ALU.add, ALU.max)
                dve.tensor_copy(peak_in[:, :], back_ps[:, 0:HEADS])
                dve.drain()
                dve.scalar_tensor_tensor(score[:, :, 0], peak_in[:, :], first[:, 1:2], score[:, :, 0], ALU.add,
                                         ALU.max)
                dve.drain()
                dve.tensor_tensor_scan(flat(peak), flat(penalty), flat(score), -FAR, ALU.add, ALU.max)
                dve.drain()

                dve.tensor_copy(score[:, :, 0], score_0[:, :])
                dve.tensor_tensor(decay[:, :, 1:P], peak[:, :, 0:P - 1], peak[:, :, 1:P], ALU.subtract)
                dve.tensor_tensor(decay[:, :, 0], peak_in[:, :], peak[:, :, 0], ALU.subtract)
                dve.tensor_tensor(decay_all, peak_in[:, :], peak[:, :, P - 1], ALU.subtract)
                dve.drain()
                dve.tensor_tensor(weight, score[:, :, :], peak[:, :, :], ALU.subtract)
                dve.drain()
                dve.tensor_scalar(powers[:, :], powers[:, :], 0.0, None, ALU.min).then_inc(powers_ready, 1)
                wait_alone(dve, raised, c + 1, k.passed)
                dve.tensor_scalar(decay_0[:, HE:SUMS], decay[:, :, 0], first[:, 0:1], None, ALU.mult)
                dve.tensor_scalar(ends[:, 1, HE:SUMS], decay_all, first[:, 2:3], None, ALU.mult)
                dve.tensor_tensor(value_decay[:, HE:SUMS, :], decay, same[:, :, :], ALU.mult)
                dve.tensor_copy(value[:, HE:SUMS, :], weight)
                dve.drain()
                for h in range(HEADS):
                    own = slice(h * EXPERTS, (h + 1) * EXPERTS)
                    one = slice(HE + h, HE + h + 1)
                    dve.tensor_copy(value_decay[:, own, :], value_decay[:, one, :].to_broadcast([P, EXPERTS, P]))
                    dve.tensor_tensor(value[:, own, :], value[:, own, :],
                                      value[:, one, :].to_broadcast([P, EXPERTS, P]), ALU.mult)
                    dve.tensor_copy(decay_0[:, own], decay_0[:, one].to_broadcast([P, EXPERTS]))
                    dve.tensor_copy(ends[:, 1, own], ends[:, 1, one].to_broadcast([P, EXPERTS]))
                dve.drain()
                dve.tensor_tensor_scan(flat(sums), flat(value_decay), flat(value), 0.0, ALU.mult, ALU.add)
                dve.drain()
                dve.tensor_copy(ends[:, 0, :], sums[:, :, P - 1])
                hand_on(c, 2, SUMS, ALU.mult, ALU.add)
                dve.tensor_tensor(decay_0[:, :], decay_0[:, :], back_ps[:, :], ALU.mult)
                dve.drain()
                dve.tensor_tensor(value[:, :, 0], value[:, :, 0], decay_0[:, :], ALU.add)
                dve.drain()
                dve.tensor_tensor_scan(flat(sums), flat(value_decay), flat(value), 0.0, ALU.mult, ALU.add)
                dve.drain()
                wait_alone(dve, stored, c * 16 + 1, k.passed)
                dve.tensor_copy(rows_out[:, :, 0:SUMS], sums[:, :, :].rearrange("p c j -> p j c"))
                dve.tensor_copy(rows_out[:, :, SUMS:NODE], peak[:, :, :].rearrange("p c j -> p j c"))
                dve.drain().then_inc(rows_ready, 1)
            over_chunks(dve, body)


def gates(nc, k):
    with ExitStack() as ctx:
        def sb(name, shape):
            return ctx.enter_context(nc.sbuf_tensor("ga_" + name, shape, F32))

        def sem(name):
            return ctx.enter_context(nc.semaphore("ga_" + name))
        state = sb("state", [P, TILES, NODE])
        last = sb("last", [P, ROW])
        b_gat, ln_gamma, ln_beta = sb("b_gat", [P, HE]), sb("ln_gamma", [P, HE]), sb("ln_beta", [P, HE])
        S4 = [P, TILES, HEADS]
        loop, late, own, peak, total, part = (sb(n, S4) for n in ("loop", "late", "own", "peak", "total", "part"))
        S16 = [P, TILES, HEADS, EXPERTS]
        agg, term = sb("agg", S16), sb("term", S16)
        mean, spread = sb("mean", [P, TILES]), sb("spread", [P, TILES])
        fetched, loaded, powers_ready, raised, var_ready, root_ready, gaps_ready, gaps_raised = (
            sem(n) for n in ("fetched", "loaded", "powers_ready", "raised", "var_ready", "root_ready",
                             "gaps_ready", "gaps_raised"))
        block = ctx.enter_context(nc.Block())

        @block.gpsimd
        def _(pool):
            for t in range(TILES):
                pool.indirect_dma_start(state[:, t, :], None, k.states[:, :],
                                        bass.IndirectOffsetOnAxis(k.last_place[:, t:t + 1], 0)).then_inc(fetched, 16)

        @block.sync
        def _(sp):
            sp.dma_start(last[:, :], k.table[TOK - 1:TOK, :].to_broadcast([P, ROW])).then_inc(loaded, 16)
            for tile, source in ((b_gat, k.b_gat), (ln_gamma, k.ln_gamma), (ln_beta, k.ln_beta)):
                sp.dma_start(tile[:, :], source.rearrange("(a n) -> a n", a=1).to_broadcast([P, HE])
                             ).then_inc(loaded, 16)

        @block.scalar
        def _(act):
            act.wait_ge(powers_ready, 1)
            for tile in (loop, late, own):
                mm = act.activation(tile[:, :, :], tile[:, :, :], ACT.Exp)
            mm.then_inc(raised, 1)
            act.wait_ge(var_ready, 1)
            act.activation(spread[:, :], spread[:, :], ACT.Sqrt).then_inc(root_ready, 1)
            act.wait_ge(gaps_ready, 1)
            act.activation(k.gate[:, :, :], k.gate[:, :, :], ACT.Exp).then_inc(gaps_raised, 1)

        @block.vector
        def _(dve):
            def tt(out, a, b, op):
                dve.tensor_tensor(out, a, b, op)
                dve.drain()

            def ts(out, a, s1, s2, op0, op1=ALU.bypass):
                dve.tensor_scalar(out, a, s1, s2, op0, op1)
                dve.drain()

            def by_tile(t, n):
                return t[:, :].unsqueeze(2).to_broadcast([P, TILES, n])

            def over_experts(t):
                return t.unsqueeze(3).to_broadcast(S16)

            def vector(v):
                return v.rearrange("p (h e) -> p h e", h=HEADS).unsqueeze(1).to_broadcast(S16)

            def masked(t, flag):
                dve.tensor_scalar(part[:, :, :], by_tile(flag, HEADS), -1.0, FAR, ALU.add, ALU.mult)
                tt(t[:, :, :], t[:, :, :], by_tile(flag, HEADS), ALU.mult)
                tt(t[:, :, :], t[:, :, :], part[:, :, :], ALU.add)

            def leaky(t):
                dve.scalar_tensor_tensor(t[:, :, :], t[:, :, :], LEAK, t[:, :, :], ALU.mult, ALU.max)
                dve.drain()
            to_score = k.node[:, :, HE + HEADS:NODE]
            dve.wait_ge(loaded, 64)
            tt(loop[:, :, :], k.node[:, :, HE:HE + HEADS], to_score, ALU.add)
            tt(late[:, :, :], last[:, HE:ROW].unsqueeze(1).to_broadcast(S4), to_score, ALU.add)
            leaky(loop)
            leaky(late)
            masked(late, k.has_last)
            dve.wait_ge(fetched, 16 * TILES)
            dve.tensor_copy(own[:, :, :], state[:, :, ROW:NODE])
            dve.drain()
            masked(own, k.has_own)
            tt(peak[:, :, :], loop[:, :, :], late[:, :, :], ALU.max)
            tt(peak[:, :, :], peak[:, :, :], own[:, :, :], ALU.max)
            for t in (loop, late, own):
                dve.tensor_tensor(t[:, :, :], t[:, :, :], peak[:, :, :], ALU.subtract)
            dve.drain().then_inc(powers_ready, 1)
            dve.wait_ge(raised, 1)
            tt(late[:, :, :], late[:, :, :], by_tile(k.count_last, HEADS), ALU.mult)
            tt(total[:, :, :], own[:, :, :], state[:, :, HE:ROW], ALU.mult)
            tt(total[:, :, :], total[:, :, :], loop[:, :, :], ALU.add)
            tt(total[:, :, :], total[:, :, :], late[:, :, :], ALU.add)
            ts(total[:, :, :], total[:, :, :], 1e-16, None, ALU.add)
            dve.reciprocal(total[:, :, :], total[:, :, :])

            def heads(t):
                return t.rearrange("p t (h e) -> p t h e", h=HEADS)
            tt(agg[:, :, :, :], heads(state[:, :, 0:HE]), over_experts(own[:, :, :]), ALU.mult)
            tt(term[:, :, :, :], heads(k.node[:, :, 0:HE]), over_experts(loop[:, :, :]), ALU.mult)
            tt(agg[:, :, :, :], agg[:, :, :, :], term[:, :, :, :], ALU.add)
            tt(term[:, :, :, :], vector(last[:, 0:HE]), over_experts(late[:, :, :]), ALU.mult)
            tt(agg[:, :, :, :], agg[:, :, :, :], term[:, :, :, :], ALU.add)
            tt(agg[:, :, :, :], agg[:, :, :, :], over_experts(total[:, :, :]), ALU.mult)
            tt(agg[:, :, :, :], agg[:, :, :, :], vector(b_gat[:, :]), ALU.add)

            rows, term_rows = (t[:, :, :, :].rearrange("p t h e -> p t (h e)") for t in (agg, term))
            dve.tensor_reduce(mean[:, :], rows, AX_X, ALU.add)
            dve.drain()
            ts(mean[:, :], mean[:, :], 1.0 / HE, None, ALU.mult)
            tt(rows, rows, by_tile(mean, HE), ALU.subtract)
            tt(term_rows, rows, rows, ALU.mult)
            dve.tensor_reduce(spread[:, :], term_rows, AX_X, ALU.add)
            dve.drain()
            dve.tensor_scalar(spread[:, :], spread[:, :], 1.0 / HE, LN_T_EPS, ALU.mult, ALU.add).then_inc(var_ready, 1)
            dve.wait_ge(root_ready, 1)
            dve.reciprocal(spread[:, :], spread[:, :])
            dve.drain()
            tt(rows, rows, by_tile(spread, HE), ALU.mult)
            tt(agg[:, :, :, :], agg[:, :, :, :], vector(ln_gamma[:, :]), ALU.mult)
            tt(agg[:, :, :, :], agg[:, :, :, :], vector(ln_beta[:, :]), ALU.add)
            score = part
            dve.tensor_reduce(score[:, :, :], agg[:, :, :, :].rearrange("p t h e -> p t e h"), AX_X, ALU.add)
            dve.drain()
            ts(score[:, :, :], score[:, :, :], 1.0 / HEADS, None, ALU.mult)

            rank, ahead = total, loop
            dve.memset(rank[:, :, :], 0.0)
            dve.drain()
            for a in range(EXPERTS):
                for b in range(a + 1, EXPERTS):
                    tt(ahead[:, :, 0], score[:, :, a], score[:, :, b], ALU.is_ge)
                    ts(ahead[:, :, 1], ahead[:, :, 0], -1.0, 1.0, ALU.mult, ALU.add)
                    dve.tensor_tensor(rank[:, :, b], rank[:, :, b], ahead[:, :, 0], ALU.add)
                    tt(rank[:, :, a], rank[:, :, a], ahead[:, :, 1], ALU.add)
            dve.tensor_reduce(mean[:, :], score[:, :, :], AX_X, ALU.max)
            dve.drain()
            dve.tensor_tensor(k.gate[:, :, :], score[:, :, :], by_tile(mean, EXPERTS),
                              ALU.subtract).then_inc(gaps_ready, 1)
            ts(rank[:, :, :], rank[:, :, :], 1.5, None, ALU.is_lt)
            dve.wait_ge(gaps_raised, 1)
            tt(k.gate[:, :, :], k.gate[:, :, :], rank[:, :, :], ALU.mult)
            dve.tensor_reduce(mean[:, :], k.gate[:, :, :], AX_X, ALU.add)
            dve.drain()
            dve.reciprocal(mean[:, :], mean[:, :])
            dve.drain()
            tt(k.gate[:, :, :], k.gate[:, :, :], by_tile(mean, EXPERTS), ALU.mult)


def feed_forward(nc, k, out):
    HID = k.w1.shape[2]
    HID_C = HID // P
    STEPS = EXPERTS * HID_C
    T = GPX // P
    HIDDEN_BUFS, GELU_BUFS, TILE_BUFS = 2, 4, 2
    LEAD = STEPS
    out_tiles = out.rearrange("b (h p) y w -> b p h (y w)", p=P)
    ln_tiles = k.ln_rows.rearrange("(h p) b y w -> b p h (y w)", p=P)

    def over_steps(eng, stages):
        for img in range(IMGS):
            with eng.Fori(0, ROW_GROUPS // UNROLL) as i:
                for step in range(UNROLL * STEPS + max(lag for _, lag, _ in stages)):
                    for body, lag, own in stages:
                        u, j = divmod(step - lag, STEPS)
                        if 0 <= u < UNROLL and j in own:
                            body(img, i * UNROLL + u, i * UNROLL + (img * ROW_GROUPS + u), u, j)

    with ExitStack() as ctx:
        def sb(name, shape, dt=F32):
            return ctx.enter_context(nc.sbuf_tensor("ff_" + name, shape, dt))

        def sem(name):
            return ctx.enter_context(nc.semaphore("ff_" + name))

        def ps(name, shape):
            return ctx.enter_context(nc.psum_tensor("ff_" + name, shape, F32))
        w1 = sb("w1", [P, EXPERTS, PARTS_C, HID])
        w2 = sb("w2", [P, STEPS, C])
        b1 = sb("b1", [P, STEPS])
        b1_rows = sb("b1_rows", [STEPS, P])
        b2 = sb("b2", [EXPERTS, C])
        pick = sb("pick", [EXPERTS, EXPERTS, P])
        x = [sb(f"x{b}", [P, PARTS_C, GPX]) for b in range(TILE_BUFS)]
        res = [sb(f"res{b}", [P, PARTS_C, GPX]) for b in range(TILE_BUFS)]
        hidden = [sb(f"hidden{b}", [P, GPX]) for b in range(GELU_BUFS)]
        gate_column = [sb(f"gate_column{b}", [P, T, EXPERTS]) for b in range(2)]
        gate_row = [sb(f"gate_row{b}", [EXPERTS, GPX]) for b in range(2)]
        gate_all = [sb(f"gate_all{b}", [P, EXPERTS, GPX]) for b in range(2)]
        hidden_ps = [ps(f"hidden_ps{b}", [P, GPX]) for b in range(HIDDEN_BUFS)]
        acc_ps = [[ps(f"acc_ps{b}_{h}", [P, GPX]) for h in range(PARTS_C)] for b in range(2)]
        row_ps = ps("row_ps", [P, GPX])
        all_ps = ps("all_ps", [P, GPX])
        x_in = [sem(f"x_in{b}") for b in range(TILE_BUFS)]
        res_in = [sem(f"res_in{b}") for b in range(TILE_BUFS)]
        stored = [sem(f"stored{b}") for b in range(TILE_BUFS)]
        weights_in, pick_ready = sem("weights_in"), sem("pick_ready")
        b1_turned, b1_ready = sem("b1_turned"), sem("b1_ready")
        multiplied, gelu_done, gated, summed, tile_ready, row_taken, all_taken = (sem(n) for n in (
            "multiplied", "gelu_done", "gated", "summed", "tile_ready", "row_taken", "all_taken"))
        column_ready, row_turned, all_ready = sem("column_ready"), sem("row_turned"), sem("all_ready")
        block = ctx.enter_context(nc.Block())
        WEIGHT_LOADS = 4
        TAKE_ROW = 2
        SPREADS = (4, 7, 10, 13)
        assert len(SPREADS) == EXPERTS
        ALL = range(STEPS)

        @block.sync
        def _(sp):
            sp.dma_start(w1[:, :, :, :], k.w1.rearrange("e (h p) n -> p e h n", p=P)).then_inc(weights_in, 16)
            sp.dma_start(w2[:, :, :], k.w2.rearrange("e (c p) o -> p (e c) o", p=P)).then_inc(weights_in, 16)
            sp.dma_start(b1_rows[:, :], k.b1.rearrange("e (c p) -> (e c) p", p=P)).then_inc(weights_in, 16)
            sp.dma_start(b2[:, :], k.b2).then_inc(weights_in, 16)

            def load(img, g, n, u):
                b = u % TILE_BUFS
                wait_alone(sp, multiplied, n * STEPS + 1, k.passed)
                sp.dma_start(x[b][:, :, :], ln_tiles[img, :, :, bass.ds(g * GPX, GPX)]).then_inc(x_in[b], 16)
                wait_alone(sp, stored[b], (n - b) * (16 // TILE_BUFS) + 1, k.passed)
                sp.dma_start(res[b][:, :, :],
                             k.residual[img, :, :, bass.ds(g * GPX, GPX)]).then_inc(res_in[b], 16)

            def store(img, g, n, u):
                b = u % TILE_BUFS
                wait_alone(sp, tile_ready, n + 3, k.passed)
                sp.dma_start(out_tiles[img, :, :, bass.ds(g * GPX, GPX)], res[b][:, :, :]).then_inc(stored[b], 16)
            for b in range(TILE_BUFS):
                sp.sem_inc(stored[b], 1)
            over_tiles(sp, [(load, 0), (store, 1)])
            for b in range(TILE_BUFS):
                sp.wait_ge(stored[b], 16 * IMGS * ROW_GROUPS // TILE_BUFS + 1)

        @block.tensor
        def _(pe):
            pe.sem_inc(multiplied, STEPS + 1)
            pe.sem_inc(summed, GELU_BUFS)
            pe.wait_ge(weights_in, 16 * WEIGHT_LOADS)
            pe.wait_ge(pick_ready, 2)
            pe.transpose(all_ps[:, 0:STEPS], b1_rows[:, :], k.ident[0:STEPS, 0:STEPS]).then_inc(b1_turned, 1)
            pe.wait_ge(b1_ready, 1)

            def turn_gates(img, g, n, u, j):
                pe.wait_ge(column_ready, n + 1)
                pe.wait_ge(row_taken, n + 1)
                for t in range(T):
                    mm = pe.transpose(row_ps[0:EXPERTS, t * P:(t + 1) * P], gate_column[u % 2][:, t, :], k.ident[:, :])
                mm.then_inc(row_turned, 1)

            def spread_gate(img, g, n, u, j):
                e = SPREADS.index(j)
                pe.wait_ge(row_taken, n + 2)
                pe.wait_ge(all_taken, n * EXPERTS + (e + 1))
                pe.matmul(all_ps[:, :], pick[:, e, :], gate_row[u % 2][:, :], start=True,
                          stop=True).then_inc(all_ready, 1)

            def first_product(img, g, n, u, j):
                b, e = u % TILE_BUFS, j // HID_C
                if j == 0:
                    pe.wait_ge(x_in[b], (n - b) * (16 // TILE_BUFS) + 16)
                pe.wait_ge(gelu_done, n * STEPS + (j + 1))
                part = slice(j % HID_C * P, (j % HID_C + 1) * P)
                for h in range(PARTS_C):
                    mm = pe.matmul(hidden_ps[j % HIDDEN_BUFS][:, :], w1[:, e, h, part], x[b][:, h, :],
                                   start=(h == 0), stop=(h == PARTS_C - 1))
                mm.then_inc(multiplied, 1)

            def second_product(img, g, n, u, j):
                acc = acc_ps[u % 2]
                if j == 0:
                    pe.wait_ge(tile_ready, n + 1)
                    for h in range(PARTS_C):
                        pe.matmul(acc[h][:, :], b2[:, h * P:(h + 1) * P], gate_row[u % 2][:, :], start=True,
                                  stop=False)
                pe.wait_ge(gated, n * STEPS + (j + 2 + STEPS))
                for h in range(PARTS_C):
                    mm = pe.matmul(acc[h][:, :], w2[:, j, h * P:(h + 1) * P], hidden[j % GELU_BUFS][:, :],
                                   start=False, stop=(j == STEPS - 1))
                mm.then_inc(summed, 1)
            over_steps(pe, [(turn_gates, 0, (0,)), (spread_gate, 0, SPREADS), (first_product, LEAD, ALL),
                            (second_product, LEAD + 2, ALL)])

        @block.scalar
        def _(act):
            act.sem_inc(gelu_done, HIDDEN_BUFS)
            act.sem_inc(all_taken, 1)
            act.wait_ge(b1_turned, 1)
            act.activation(b1[:, :], all_ps[:, 0:STEPS], ACT.Copy).then_inc(b1_ready, 1)
            act.wait_ge(b1_ready, 1)

            def take_gate(img, g, n, u, j):
                e = SPREADS.index(j)
                act.wait_ge(gated, n * STEPS + 1)
                act.wait_ge(all_ready, n * EXPERTS + (e + 1))
                act.activation(gate_all[u % 2][:, e, :], all_ps[:, :], ACT.Copy).then_inc(all_taken, 1)

            def gelu(img, g, n, u, j):
                act.wait_ge(multiplied, n * STEPS + (j + 2 + STEPS))
                act.wait_ge(summed, n * STEPS + (j + 1))
                act.activation(hidden[j % GELU_BUFS][:, :], hidden_ps[j % HIDDEN_BUFS][:, :], ACT.Gelu,
                               bias=b1[:, j:j + 1]).then_inc(gelu_done, 1)
            over_steps(act, [(take_gate, 0, SPREADS), (gelu, LEAD, ALL)])

        @block.vector
        def _(dve):
            dve.sem_inc(gated, STEPS + 1)
            dve.sem_inc(tile_ready, 2)
            dve.sem_inc(row_taken, 1)

            def gate_columns(img, g, n, u, j):
                dve.tensor_copy(gate_column[u % 2][:, :, :],
                                k.gate[:, bass.ds(n * T, T), :]).then_inc(column_ready, 1)

            def take_row(img, g, n, u, j):
                dve.wait_ge(row_turned, n + 1)
                dve.tensor_copy(gate_row[u % 2][:, :], row_ps[0:EXPERTS, :]).then_inc(row_taken, 1)

            def times_gate(img, g, n, u, j):
                e = j // HID_C
                if j % HID_C == 0:
                    dve.wait_ge(all_taken, n * EXPERTS + (e + 2))
                dve.wait_ge(gelu_done, n * STEPS + (j + 1 + HIDDEN_BUFS))
                x = hidden[j % GELU_BUFS]
                dve.tensor_tensor(x[:, :], x[:, :], gate_all[u % 2][:, e, :], ALU.mult).then_inc(gated, 1)

            def add_residual(img, g, n, u, j):
                b = u % TILE_BUFS
                dve.wait_ge(res_in[b], (n - b) * (16 // TILE_BUFS) + 16)
                dve.wait_ge(summed, n * STEPS + (STEPS + GELU_BUFS))
                for h in range(PARTS_C):
                    last = dve.tensor_tensor(res[b][:, h, :], res[b][:, h, :], acc_ps[u % 2][h][:, :], ALU.add)
                last.then_inc(tile_ready, 1)
            over_steps(dve, [(gate_columns, 0, (0,)), (take_row, 0, (TAKE_ROW,)), (times_gate, LEAD, ALL),
                             (add_residual, LEAD + 3, (STEPS - 1,))])

        @block.gpsimd
        def _(pool):
            pool.memset(pick[:, :, :], 1.0).then_inc(pick_ready, 1)
            pool.wait_ge(pick_ready, 1)
            pool.affine_select(out=pick[:, :, :], in_=pick[:, :, :], compare_op=ALU.is_equal, fill=0.0, base=0,
                               pattern=[[-1, EXPERTS], [0, P]], channel_multiplier=1).then_inc(pick_ready, 1)


def constants(nc, k):
    with ExitStack() as ctx:
        zeroed = ctx.enter_context(nc.semaphore("co_zeroed"))
        block = ctx.enter_context(nc.Block())

        @block.gpsimd
        def _(pool):
            pool.memset(k.ident[:, :], 0.0).then_inc(zeroed, 1)
            pool.memset(k.ones_f[:, :], 1.0)
            pool.wait_ge(zeroed, 1)
            pool.affine_select(out=k.ident[:, :], in_=k.ident[:, :], compare_op=ALU.not_equal, fill=1.0, base=0,
                               pattern=[[-1, P]], channel_multiplier=1).then_inc(zeroed, 1)
            pool.memset(k.mean_c[:, :], 1.0 / C)
            pool.memset(k.eps_c[:, :], LN_C_EPS)
            pool.memset(k.eps_t[:, :], LN_T_EPS)
            pool.wait_ge(zeroed, 2)
            pool.tensor_copy(k.ident_b[:, :], k.ident[:, :])


ARGS = ("x", "w_cat_t", "w_scale_t", "gamma", "beta", "w_gat", "att_src", "att_dst", "b_gat", "ln_gamma",
        "ln_beta", "w1", "b1", "w2", "b2", "edge_index")


def build(nc, args, out):
    k = Ctx()
    (k.x, k.w_cat_t, k.w_scale_t, k.gamma, k.beta, k.w_gat, k.att_src, k.att_dst, k.b_gat, k.ln_gamma, k.ln_beta,
     k.w1, k.b1, k.w2, k.b2, k.edge_index) = (args[name] for name in ARGS)
    declare_scratch(nc, k)
    with ExitStack() as ctx:
        def sb(name, shape, dt):
            return ctx.enter_context(nc.sbuf_tensor(name, shape, dt))
        k.passed = ctx.enter_context(nc.semaphore("passed"))
        k.ident = sb("ident", [P, P], F32)
        k.ones_f = sb("ones_f", [P, P], F32)
        k.mean_c = sb("mean_c", [P, P], F32)
        k.eps_c = sb("eps_c", [P, 1], F32)
        k.eps_t = sb("eps_t", [P, 1], F32)
        k.ident_b = sb("ident_b", [P, P], BF16)
        k.own_edges = sb("own_edges", [P, 1], I32)
        k.edge_counts = sb("edge_counts", [P, 2], I32)
        constants(nc, k)
        layer_norm_tiles(nc, k, tokens=False)
        guide_taps(nc, k)
        k.y_stats = sb("y_stats", [P, PARTS_C, TOK // GPX, 6], F32)
        with ExitStack() as conv_ctx:
            k.offsets = [0] + [sign * d for d in DILATIONS for sign in (-1, 1)]
            k.masks = conv_ctx.enter_context(nc.sbuf_tensor("masks", [W, len(k.offsets), GPX], U16))
            k.pick_left = conv_ctx.enter_context(nc.sbuf_tensor("pick_left", [SPLITS * LEFT, LEFT, W], BF16))
            k.pick_right = conv_ctx.enter_context(nc.sbuf_tensor("pick_right", [SPLITS * RIGHT, RIGHT, W], BF16))
            branch_masks(nc, k)
            dilated_branches(nc, k)
        k.bn_scale, k.bn_shift = sb("bn_scale", [P, PARTS_C], F32), sb("bn_shift", [P, PARTS_C], F32)
        k.w_graph = sb("w_graph", [P, PARTS_C, NODE], F32)
        k.node = sb("node", [P, TILES, NODE], F32)
        token_constants(nc, k)
        layer_norm_tiles(nc, k, tokens=True)
        with ExitStack() as sort_ctx:
            k.keys_a = sort_ctx.enter_context(nc.sbuf_tensor("keys_a", [P, LANE], F32))
            k.keys_b = sort_ctx.enter_context(nc.sbuf_tensor("keys_b", [P, LANE], F32))
            edge_keys(nc, k)
            sort_edges(nc, k)
            store_sorted(nc, k)
        k.first_place = sb("first_place", [P, TILES], U32)
        k.last_place = sb("last_place", [P, TILES], U32)
        k.has_own = sb("has_own", [P, TILES], F32)
        k.has_last = sb("has_last", [P, TILES], F32)
        k.count_last = sb("count_last", [P, TILES], F32)
        count_edges(nc, k)
        place_scores(nc, k)
        edge_softmax(nc, k)
        k.gate = sb("gate", [P, TILES, EXPERTS], F32)
        gates(nc, k)
        feed_forward(nc, k, out)


def kernel(**inputs):
    import numpy as np
    import concourse.bacc as bacc
    from concourse.bass_utils import run_bass_kernel_spmd

    conv, ffn = "L0_conv_", "L0_ffn_"
    given = {name: np.asarray(a) for name, a in inputs.items()}
    arrays = {
        "x": given["x"],
        "w_cat_t": given[conv + "W_cat"].transpose(1, 2, 3, 0).reshape(C, TAPS, GUIDES),
        "w_scale_t": given[conv + "W_scale"].reshape(C, (BRANCHES + 1) * C).T,
        "gamma": given[conv + "gamma"], "beta": given[conv + "beta"],
        "w_gat": given[ffn + "W_gat"], "att_src": given[ffn + "att_src"], "att_dst": given[ffn + "att_dst"],
        "b_gat": given[ffn + "b_gat"], "ln_gamma": given[ffn + "ln_gamma"], "ln_beta": given[ffn + "ln_beta"],
        "w1": given[ffn + "W1"], "b1": given[ffn + "b1"], "w2": given[ffn + "W2"], "b2": given[ffn + "b2"],
        "edge_index": given[ffn + "edge_index"],
    }
    arrays = {"in_" + name: np.ascontiguousarray(a) for name, a in arrays.items()}
    nc = bacc.Bacc("TRN2", target_bir_lowering=False, num_devices=1)
    args = {name: nc.dram_tensor("in_" + name, arrays["in_" + name].shape,
                                 mybir.dt.from_np(arrays["in_" + name].dtype), kind="ExternalInput").ap()
            for name in ARGS}
    out = nc.dram_tensor("out", (IMGS, C, H, W), F32, kind="ExternalOutput").ap()
    build(nc, args, out)
    return run_bass_kernel_spmd(nc, [arrays], core_ids=[0]).results[0]["out"]
```

```python
from contextlib import ExitStack

import concourse.bass as bass
from concourse import mybir

P = 128
ALU = mybir.AluOpType
ACT = mybir.ActivationFunctionType
AX_X = mybir.AxisListType.X
F32 = mybir.dt.float32
BF16 = mybir.dt.bfloat16
F16 = mybir.dt.float16
I32 = mybir.dt.int32
U32 = mybir.dt.uint32
U16 = mybir.dt.uint16

IMGS, C, H, W = 2, 256, 96, 96
PIX = H * W
TOK = IMGS * PIX
TILES = TOK // P
E = 1048576
HEADS, EXPERTS = 4, 4
HE = HEADS * EXPERTS

SRC_BITS = 15
SRC_MASK = (1 << SRC_BITS) - 1
KEY_BASE = 256
KEY_LAST = 1 << 15
KEY_DROP = 0xFE00
LANE = E // P
CHUNK = P * P
CHUNKS = E // CHUNK
NODE = HE + 2 * HEADS
ROW = HE + HEADS


class Ctx:
    pass


def declare_scratch(nc, k):
    k.xn_rows = nc.dram_tensor("xn_rows", (C, IMGS, H + 2, W), F32, kind="Internal").ap()
    k.xn_pixels = nc.dram_tensor("xn_pixels", (IMGS, H + 2, W, C), F32, kind="Internal").ap()
    k.taps_left = nc.dram_tensor("taps_left", (SPLITS * LEFT, TOK), BF16, kind="Internal").ap()
    k.taps_right = nc.dram_tensor("taps_right", (SPLITS * RIGHT, TOK), BF16, kind="Internal").ap()
    k.conv_out = nc.dram_tensor("conv_out", (C, IMGS, H, W), F32, kind="Internal").ap()
    k.ln_rows = nc.dram_tensor("ln_rows", (C, IMGS, H, W), F32, kind="Internal").ap()
    k.residual = nc.dram_tensor("residual", (IMGS, P, PARTS_C, PIX), F32, kind="Internal").ap()
    k.table = nc.dram_tensor("table", (TOK, ROW), F32, kind="Internal").ap()
    k.dst_scores = nc.dram_tensor("dst_scores", (E + CHUNK, HEADS), F32, kind="Internal").ap()
    k.states = nc.dram_tensor("states", (E, NODE), F32, kind="Internal").ap()
    k.expert_out = nc.dram_tensor("expert_out", (IMGS * ROW_GROUPS, P, EXPERTS * PARTS_C * GPX), F32,
                                  kind="Internal").ap()
    k.edge_rows = nc.dram_tensor("edge_rows", (CHUNKS + 1, P, P * ROW), F32, kind="Internal").ap()
    k.sorted_keys = nc.dram_tensor("sorted_keys", (P + E + CHUNK,), I32, kind="Internal").ap()


GROUP_ROWS = 4
GPX = GROUP_ROWS * W
ROW_GROUPS = H // GROUP_ROWS
PARTS_C = C // P
DILATIONS = (1, 6, 12, 24, 36)
BRANCHES = len(DILATIONS)
TAPS = 9
GUIDES = BRANCHES * TAPS
LN_C_EPS, LN_T_EPS, BN_EPS = 1e-6, 1e-5, 1e-5
SPLITS = 3
LEFT_BRANCHES = 3
LEFT = LEFT_BRANCHES * TAPS
RIGHT = GUIDES - LEFT


def edge_keys(nc, k):
    PART = 1024
    PARTS = LANE // PART
    edges = k.edge_index.rearrange("two (p f) -> two p f", p=P)
    with ExitStack() as ctx:
        src = [ctx.enter_context(nc.sbuf_tensor(f"ek_src{i}", [P, PART], I32)) for i in range(2)]
        dst = [ctx.enter_context(nc.sbuf_tensor(f"ek_dst{i}", [P, PART], I32)) for i in range(2)]
        t1 = ctx.enter_context(nc.sbuf_tensor("ek_t1", [P, PART], I32))
        t2 = ctx.enter_context(nc.sbuf_tensor("ek_t2", [P, PART], I32))
        t3 = ctx.enter_context(nc.sbuf_tensor("ek_t3", [P, PART], I32))
        part_count = ctx.enter_context(nc.sbuf_tensor("ek_part_count", [P, 2, PARTS], F32))
        counted = ctx.enter_context(nc.sbuf_tensor("ek_counted", [P, 2], F32))
        totals = ctx.enter_context(nc.psum_tensor("ek_totals", [P, 2], F32))
        src_in = [ctx.enter_context(nc.semaphore(f"ek_src_in{i}")) for i in range(2)]
        dst_in = [ctx.enter_context(nc.semaphore(f"ek_dst_in{i}")) for i in range(2)]
        part_done = ctx.enter_context(nc.semaphore("ek_part_done"))
        lane_counted = ctx.enter_context(nc.semaphore("ek_lane_counted"))
        totals_ready = ctx.enter_context(nc.semaphore("ek_totals_ready"))
        block = ctx.enter_context(nc.Block())

        @block.sync
        def _(sp):
            for c in range(PARTS):
                if c >= 2:
                    sp.wait_ge(part_done, c - 1)
                sp.dma_start(src[c % 2][:, :], edges[0, :, c * PART:(c + 1) * PART]).then_inc(src_in[c % 2], 16)
                sp.dma_start(dst[c % 2][:, :], edges[1, :, c * PART:(c + 1) * PART]).then_inc(dst_in[c % 2], 16)

        @block.vector
        def _(dve):
            for c in range(PARTS):
                s, d = src[c % 2], dst[c % 2]
                dve.wait_ge(src_in[c % 2], 16 * (c // 2 + 1))
                dve.wait_ge(dst_in[c % 2], 16 * (c // 2 + 1))
                dve.tensor_scalar(t1[:, :], s[:, :], float(TOK - 1), float(KEY_LAST), ALU.is_ge, ALU.mult)
                dve.tensor_scalar(t2[:, :], d[:, :], float(TOK), float(KEY_BASE), ALU.min, ALU.add)
                dve.tensor_scalar(t3[:, :], d[:, :], float(TOK), float(KEY_DROP), ALU.is_ge, ALU.mult)
                dve.tensor_scalar(s[:, :], s[:, :], float(TOK - 1), 0.0, ALU.min, ALU.max)
                dve.drain()
                dve.tensor_tensor(t2[:, :], t2[:, :], t1[:, :], ALU.add)
                dve.drain()
                dve.tensor_tensor(t2[:, :], t2[:, :], t3[:, :], ALU.max)
                dve.drain()
                dve.tensor_scalar(t1[:, :], t2[:, :], float(KEY_LAST), 0.0, ALU.is_ge, ALU.add,
                                  accum_out=part_count[:, 0, c:c + 1])
                dve.tensor_scalar(t3[:, :], t2[:, :], float(KEY_DROP), 0.0, ALU.is_ge, ALU.add,
                                  accum_out=part_count[:, 1, c:c + 1])
                dve.scalar_tensor_tensor(k.keys_a[:, c * PART:(c + 1) * PART].bitcast(I32), t2[:, :], SRC_BITS,
                                         s[:, :], ALU.logical_shift_left, ALU.bitwise_or).then_inc(part_done, 1)
                dve.drain()
            dve.tensor_reduce(counted[:, :], part_count[:, :, :], AX_X, ALU.add).then_inc(lane_counted, 1)
            dve.wait_ge(totals_ready, 1)
            dve.tensor_scalar(k.edge_counts[:, :], totals[:, :], -1.0, float(E), ALU.mult, ALU.add)
            dve.drain()
            dve.tensor_scalar(k.edge_counts[:, :], k.edge_counts[:, :], 1.0, None, ALU.max)

        @block.tensor
        def _(pe):
            pe.wait_ge(lane_counted, 1)
            pe.matmul(totals[:, :], k.ones_f[:, :], counted[:, :], start=True, stop=True).then_inc(totals_ready, 1)


def sort_views(buf, j, q):
    if q is None:
        v = buf[:, :].rearrange("p (a two c) -> p a two c", two=2, c=1 << j)
        return {0: (v[:, :, 0, :], v[:, :, 1, :])}
    hi, lo = max(j, q), min(j, q)
    v = buf[:, :].rearrange("p (a h b l c) -> p a h b l c", h=2, l=2, b=1 << (hi - lo - 1), c=1 << lo)
    out = {}
    for d in range(2):
        pair = []
        for side in range(2):
            h, l = (side, d) if j > q else (d, side)
            x = v[:, :, h, :, l, :]
            pair.append(x[:, :, 0, :] if hi - lo == 1 else x[:, 0, :, :])
        out[d] = tuple(pair)
    return out


def sort_and_experts(nc, k):
    FREE, QUARTER, TOP = 13, 18, 20
    QUARTERS = 4
    a, b = k.keys_a, k.keys_b
    HID = k.w1.shape[2]
    HID_C = HID // P
    STEPS = EXPERTS * HID_C
    HIDDEN_BANKS, HIDDEN_BUFS, ACC_BANKS, TILE_BUFS = 4, 4, 2, 2
    TILES_ALL = IMGS * ROW_GROUPS
    ln_tiles = k.ln_rows.rearrange("(h p) b y w -> b p h (y w)", p=P)

    def over_steps(eng, stages):
        for img in range(IMGS):
            with eng.Fori(0, ROW_GROUPS // UNROLL) as i:
                for step in range(UNROLL * STEPS + max(lag for _, lag, _ in stages)):
                    for body, lag, own in stages:
                        u, j = divmod(step - lag, STEPS)
                        if 0 <= u < UNROLL and j in own:
                            body(i * UNROLL + (img * ROW_GROUPS + u), u, j)

    with ExitStack() as ctx:
        def sb(name, shape):
            return ctx.enter_context(nc.sbuf_tensor("se_" + name, shape, F32))

        def sem(name):
            return ctx.enter_context(nc.semaphore("se_" + name))

        def ps(name, shape):
            return ctx.enter_context(nc.psum_tensor("se_" + name, shape, F32))
        w1 = sb("w1", [P, EXPERTS, PARTS_C, HID])
        w2 = sb("w2", [P, STEPS, C])
        b1, b1_rows = sb("b1", [P, STEPS]), sb("b1_rows", [STEPS, P])
        BIASES = EXPERTS * PARTS_C
        b2, b2_rows = sb("b2", [P, BIASES]), sb("b2_rows", [BIASES, P])
        x = [sb(f"x{b}", [P, PARTS_C, GPX]) for b in range(TILE_BUFS)]
        hidden = [sb(f"hidden{b}", [P, GPX]) for b in range(HIDDEN_BUFS)]
        given = [sb(f"given{b}", [P, EXPERTS, PARTS_C, GPX]) for b in range(TILE_BUFS)]
        ZEROS = 1040 * HEADS
        zeros = sb("zeros", [P, ZEROS])
        sign = sb("sign", [P, 1])
        hidden_ps = [ps(f"hidden_ps{b}", [P, GPX]) for b in range(HIDDEN_BANKS)]
        acc_ps = [[ps(f"acc_ps{b}_{h}", [P, GPX]) for h in range(PARTS_C)] for b in range(ACC_BANKS)]
        x_in = [sem(f"x_in{b}") for b in range(TILE_BUFS)]
        stored = [sem(f"stored{b}") for b in range(TILE_BUFS)]
        (weights_in, biases_turned, biases_ready, zero_ready, zero_out, sign_ready, to_swap, swapped) = (
            sem(n) for n in ("weights_in", "biases_turned", "biases_ready", "zero_ready", "zero_out", "sign_ready",
                             "to_swap", "swapped"))
        multiplied, gelu_done, summed, copied = (sem(n) for n in ("multiplied", "gelu_done", "summed", "copied"))
        block = ctx.enter_context(nc.Block())
        ALL = range(STEPS)
        LAST_OF_EXPERT = range(HID_C - 1, STEPS, HID_C)

        @block.sync
        def _(sp):
            sp.dma_start(w1[:, :, :, :], k.w1.rearrange("e (h p) n -> p e h n", p=P)).then_inc(weights_in, 16)
            sp.dma_start(w2[:, :, :], k.w2.rearrange("e (c p) o -> p (e c) o", p=P)).then_inc(weights_in, 16)
            sp.dma_start(b1_rows[:, :], k.b1.rearrange("e (c p) -> (e c) p", p=P)).then_inc(weights_in, 16)
            sp.dma_start(b2_rows[:, :], k.b2.rearrange("e (h p) -> (e h) p", p=P)).then_inc(weights_in, 16)
            sp.wait_ge(zero_ready, 1)
            states = k.states.rearrange("(c p r) v -> c p (r v)", p=P, r=P)

            def load(img, g, n, u):
                b = u % TILE_BUFS
                wait_alone(sp, multiplied, n * STEPS + 1, k.passed)
                sp.dma_start(x[b][:, :, :], ln_tiles[img, :, :, bass.ds(g * GPX, GPX)]).then_inc(x_in[b], 16)

            def store(img, g, n, u):
                b = u % TILE_BUFS
                wait_alone(sp, copied, n * EXPERTS + (EXPERTS + ACC_BANKS), k.passed)
                sp.dma_start(k.expert_out[bass.ds(n, 1)].rearrange("a p v -> p (a v)"),
                             given[b][:, :, :, :].rearrange("p e h t -> p (e h t)")).then_inc(stored[b], 16)
                sp.dma_start(states[bass.ds(n, 1)].rearrange("a p v -> p (a v)"),
                             zeros[:, 0:P * NODE]).then_inc(zero_out, 16)
            for b in range(TILE_BUFS):
                sp.sem_inc(stored[b], 1)
            over_tiles(sp, [(load, 0), (store, 1)])
            for c in range(TILES_ALL, CHUNKS):
                sp.dma_start(states[c], zeros[:, 0:P * NODE]).then_inc(zero_out, 16)
            scores = k.dst_scores.rearrange("(n p r) h -> n p (r h)", p=P, r=ZEROS // HEADS)
            for n in range(scores.shape[0]):
                sp.dma_start(scores[n], zeros[:, :]).then_inc(zero_out, 16)
            sp.wait_ge(zero_out, 16 * (CHUNKS + scores.shape[0]))
            for b in range(TILE_BUFS):
                sp.wait_ge(stored[b], 16 * TILES_ALL // TILE_BUFS + 1)

        @block.tensor
        def _(pe):
            pe.sem_inc(multiplied, STEPS + 1)
            pe.sem_inc(summed, HIDDEN_BUFS)
            pe.wait_ge(weights_in, 16 * 4)
            pe.transpose(hidden_ps[0][:, 0:STEPS], b1_rows[:, :], k.ident[0:STEPS, 0:STEPS])
            pe.transpose(hidden_ps[1][:, 0:BIASES], b2_rows[:, :],
                         k.ident[0:BIASES, 0:BIASES]).then_inc(biases_turned, 1)
            pe.wait_ge(biases_ready, 1)

            def first_product(n, u, j):
                b, e = u % TILE_BUFS, j // HID_C
                if j == 0:
                    pe.wait_ge(x_in[b], (n - b) * (16 // TILE_BUFS) + 16)
                pe.wait_ge(gelu_done, n * STEPS + (j + 1))
                part = slice(j % HID_C * P, (j % HID_C + 1) * P)
                for h in range(PARTS_C):
                    mm = pe.matmul(hidden_ps[j % HIDDEN_BANKS][:, :], w1[:, e, h, part], x[b][:, h, :],
                                   start=(h == 0), stop=(h == PARTS_C - 1))
                mm.then_inc(multiplied, 1)

            def second_product(n, u, j):
                e, c = divmod(j, HID_C)
                if c == 0:
                    pe.wait_ge(copied, n * EXPERTS + (e + 1))
                pe.wait_ge(gelu_done, n * STEPS + (j + 1 + HIDDEN_BANKS))
                for h in range(PARTS_C):
                    mm = pe.matmul(acc_ps[e % ACC_BANKS][h][:, :], w2[:, j, h * P:(h + 1) * P],
                                   hidden[j % HIDDEN_BUFS][:, :], start=(c == 0), stop=(c == HID_C - 1))
                mm.then_inc(summed, 1)
            over_steps(pe, [(first_product, 0, ALL), (second_product, 2, ALL)])

        @block.scalar
        def _(act):
            act.sem_inc(gelu_done, HIDDEN_BANKS)
            act.sem_inc(copied, ACC_BANKS)
            act.wait_ge(biases_turned, 1)
            act.activation(b1[:, :], hidden_ps[0][:, 0:STEPS], ACT.Copy)
            act.activation(b2[:, :], hidden_ps[1][:, 0:BIASES], ACT.Copy).then_inc(biases_ready, 1)
            act.wait_ge(biases_ready, 1)

            def gelu(n, u, j):
                act.wait_ge(multiplied, n * STEPS + (j + 2 + STEPS))
                act.wait_ge(summed, n * STEPS + (j + 1))
                act.activation(hidden[j % HIDDEN_BUFS][:, :], hidden_ps[j % HIDDEN_BANKS][:, :], ACT.Gelu,
                               bias=b1[:, j:j + 1]).then_inc(gelu_done, 1)

            def copy_out(n, u, j):
                b, e = u % TILE_BUFS, j // HID_C
                if e == 0:
                    act.wait_ge(stored[b], (n - b) * (16 // TILE_BUFS) + 1)
                act.wait_ge(summed, n * STEPS + (j + 1 + HIDDEN_BUFS))
                for h in range(PARTS_C):
                    last = act.activation(given[b][:, e, h, :], acc_ps[e % ACC_BANKS][h][:, :], ACT.Identity,
                                          bias=b2[:, e * PARTS_C + h:e * PARTS_C + h + 1])
                last.then_inc(copied, 1)
            over_steps(act, [(gelu, 0, ALL), (copy_out, 3, LAST_OF_EXPERT)])

        swap_sources = []

        @block.vector
        def _(dve):
            bufs = [a, b]
            cur = 0

            def index_bit(bit, layout):
                return {"plain": bit, "turned": bit if bit < FREE else bit - FREE,
                        "swapped": bit - QUARTER + FREE - 2}[layout]

            def run(level, bits, layout, split=True):
                nonlocal cur
                for bit in bits:
                    first = bit == level - 1
                    q = index_bit(level, layout) if first and split else None
                    s, d = bufs[cur], bufs[1 - cur]
                    sv, dv = (sort_views(t, index_bit(bit, layout), q) for t in (s, d))
                    for direction, (low, high) in sv.items():
                        for out, op, other in zip(dv[direction], (ALU.min, ALU.max), (ALU.max, ALU.min)):
                            if not first:
                                dve.tensor_tensor(out, low, high, op)
                            elif level == 1:
                                dve.tensor_tensor(out, low, high, op if direction == 0 else other)
                            elif direction == 0:
                                dve.scalar_tensor_tensor(out, high, -1.0, low, ALU.mult, op)
                            else:
                                dve.scalar_tensor_tensor(out, low, -1.0, high, ALU.mult, op)
                    dve.drain()
                    if level == 1:
                        for side in sort_views(d, 0, 1)[1]:
                            dve.tensor_scalar(side, side, -1.0, None, ALU.mult)
                        dve.drain()
                    cur = 1 - cur

            def turn():
                nonlocal cur
                dve.transpose(bufs[1 - cur][:, :], bufs[cur][:, :])
                dve.drain()
                cur = 1 - cur

            def swap():
                nonlocal cur
                swap_sources.append(cur)
                dve.sem_inc(to_swap, 1)
                dve.wait_ge(swapped, 16 * QUARTERS * QUARTERS * len(swap_sources))
                cur = 1 - cur

            def down(first, last):
                return range(first, last - 1, -1)
            for level in range(1, TOP + 1):
                if level < FREE:
                    run(level, down(level - 1, 0), "plain")
                    continue
                if level == QUARTER:
                    dve.wait_ge(sign_ready, 3)
                    dve.tensor_scalar(bufs[cur][:, :], bufs[cur][:, :], sign[:, 0:1], None, ALU.mult)
                    dve.drain()
                if level > QUARTER:
                    swap()
                    run(level, down(level - 1, QUARTER), "swapped", split=level < TOP)
                    swap()
                turn()
                run(level, down(min(level, QUARTER) - 1, 5), "turned", split=level != QUARTER)
                turn()
                run(level, down(4, 0), "plain")
            k.sorted_buf = bufs[cur]

        @block.gpsimd
        def _(pool):
            pool.memset(zeros[:, :], 0.0).then_inc(zero_ready, 1)
            pool.memset(sign[:, :], 1.0).then_inc(sign_ready, 1)
            pool.wait_ge(sign_ready, 1)
            pool.memset(sign[P // QUARTERS:2 * P // QUARTERS, :], -1.0).then_inc(sign_ready, 1)
            pool.wait_ge(sign_ready, 2)
            pool.memset(sign[3 * P // QUARTERS:P, :], -1.0).then_inc(sign_ready, 1)
            span, rows = LANE // QUARTERS, P // QUARTERS
            for n, source in enumerate(swap_sources):
                pool.wait_ge(to_swap, n + 1)
                s, d = (a, b) if source == 0 else (b, a)
                for i in range(QUARTERS):
                    for j in range(QUARTERS):
                        pool.dma_start(d[i * rows:(i + 1) * rows, j * span:(j + 1) * span],
                                       s[j * rows:(j + 1) * rows, i * span:(i + 1) * span]).then_inc(swapped, 16)


def store_sorted(nc, k):
    with ExitStack() as ctx:
        front = ctx.enter_context(nc.sbuf_tensor("ss_front", [1, P], I32))
        tail = ctx.enter_context(nc.sbuf_tensor("ss_tail", [P, P], I32))
        front_zero = ctx.enter_context(nc.semaphore("ss_front_zero"))
        keys_out = ctx.enter_context(nc.semaphore("ss_keys_out"))
        block = ctx.enter_context(nc.Block())

        @block.vector
        def _(dve):
            dve.memset(tail[:, :], 0)
            dve.memset(front[:, :], 0).then_inc(front_zero, 1)

        @block.sync
        def _(sp):
            sp.dma_start(k.sorted_keys[P:P + E].rearrange("(p f) -> p f", p=P),
                         k.sorted_buf[:, :].bitcast(I32)).then_inc(keys_out, 16)
            sp.wait_ge(front_zero, 1)
            sp.dma_start(k.sorted_keys[0:P].rearrange("(a f) -> a f", a=1), front[:, :]).then_inc(keys_out, 16)
            sp.dma_start(k.sorted_keys[P + E:].rearrange("(p f) -> p f", p=P), tail[:, :]).then_inc(keys_out, 16)
            sp.wait_ge(keys_out, 3 * 16)


def count_edges(nc, k):
    KINDS = 2 * TILES
    RING, GROUP = 16, 4
    GROUPS = P // GROUP
    with ExitStack() as ctx:
        def sb(name, shape, dt):
            return ctx.enter_context(nc.sbuf_tensor(name, shape, dt))

        def sem(name):
            return ctx.enter_context(nc.semaphore(name))
        keys = sb("ce_keys", [P, P], I32)
        token = sb("ce_token", [P, P], I32)
        high = sb("ce_high", [P, P], F32)
        low = sb("ce_low", [P, P], F32)
        high_i = sb("ce_high_i", [P, P], I32)
        low_i = sb("ce_low_i", [P, P], I32)
        hot_high = sb("ce_hot_high", [P, RING, KINDS], BF16)
        hot_low = sb("ce_hot_low", [P, RING, P], BF16)
        iota_high = sb("ce_iota_high", [P, KINDS], F16)
        iota_low = sb("ce_iota_low", [P, P], F16)
        before = sb("ce_before", [P, P], F32)
        counts = sb("ce_counts", [P, KINDS], F32)
        running = sb("ce_running", [P, TILES], F32)
        column = sb("ce_column", [P, TILES], F32)
        first = sb("ce_first", [P, TILES], F32)
        none = sb("ce_none", [P, TILES], F32)
        counts_ps = ctx.enter_context(nc.psum_tensor("ce_counts_ps", [P, KINDS], F32))
        within_ps = ctx.enter_context(nc.psum_tensor("ce_within_ps", [P, TILES], F32))
        column_ps = ctx.enter_context(nc.psum_tensor("ce_column_ps", [P, TILES], F32))
        source_i = sb("ce_source_i", [P, P], I32)
        sources = sb("ce_sources", [P, LANE], U32)
        source = sb("ce_source", [P, P], U32)
        fetched = sb("ce_fetched", [P, P, ROW], F32)
        source_ready, source_taken, rows_fetched, rows_stored = (sem("ce_" + x) for x in (
            "source_ready", "source_taken", "rows_fetched", "rows_stored"))
        iota_ready, before_ready, keys_in, keys_read = (sem("ce_" + x) for x in (
            "iota_ready", "before_ready", "keys_in", "keys_read"))
        hot_ready, hot_free, chunk_added = (sem("ce_" + x) for x in (
            "hot_ready", "hot_free", "chunk_added"))
        sums_ready = sem("ce_sums_ready")
        counts_whole = sem("ce_counts_whole")
        block = ctx.enter_context(nc.Block())

        @block.gpsimd
        def _(pool):
            pool.memset(before[:, :], 1.0).then_inc(before_ready, 1)
            pool.iota(iota_high[:, :].rearrange("p (a b) -> p a b", a=2), [[KEY_LAST // P, 2], [1, TILES]], base=0,
                      channel_multiplier=0, allow_small_or_imprecise_dtypes=True)
            pool.iota(iota_low[:, :], [[1, P]], base=0, channel_multiplier=0,
                      allow_small_or_imprecise_dtypes=True).then_inc(iota_ready, 1)
            pool.wait_ge(before_ready, 1)
            pool.affine_select(out=before[:, :], in_=before[:, :], compare_op=ALU.is_gt, fill=0.0, base=0,
                               pattern=[[1, P]], channel_multiplier=-1).then_inc(before_ready, 1)
            own = pool.value_load(k.edge_counts[0:1, 0:1], min_val=1, max_val=E)
            with pool.Fori(0, CHUNKS) as c:
                with pool.If(c * CHUNK < own):
                    wait_alone(pool, source_ready, c + 1, k.passed)
                    wait_alone(pool, rows_stored, c * 16 + 1, k.passed)
                    pool.tensor_copy(source[:, :], sources[:, bass.ds(c * P, P)]).then_inc(source_taken, 1)
                    wait_alone(pool, source_taken, c + 1, k.passed)
                    for j in range(P):
                        pool.indirect_dma_start(fetched[:, j, :], None, k.table[:, :],
                                                bass.IndirectOffsetOnAxis(source[:, j:j + 1], 0)
                                                ).then_inc(rows_fetched, 16)

        @block.scalar
        def _(act):
            act.sem_inc(rows_stored, 1)
            own = act.value_load(k.edge_counts[0:1, 0:1], min_val=1, max_val=E)
            with act.Fori(0, CHUNKS) as c:
                with act.If(c * CHUNK < own):
                    wait_alone(act, rows_fetched, c * (16 * P) + 16 * P, k.passed)
                    act.dma_start(k.edge_rows[bass.ds(c, 1)].rearrange("a p v -> p (a v)"),
                                  fetched[:, :, :].rearrange("p j v -> p (j v)")).then_inc(rows_stored, 16)
                    wait_alone(act, rows_stored, c * 16 + 17, k.passed)

        @block.sync
        def _(sp):
            kept = sp.value_load(k.edge_counts[0:1, 1:2], min_val=1, max_val=E)
            with sp.Fori(0, CHUNKS) as c:
                with sp.If(c * CHUNK < kept):
                    sp.wait_ge(keys_read, c + 1)
                    sp.dma_start(keys[:, :], k.sorted_keys[bass.ds(c * CHUNK + P, CHUNK)].rearrange(
                        "(p f) -> p f", p=P)).then_inc(keys_in, 16)

        @block.vector
        def _(dve):
            dve.memset(counts[:, :], 0.0)
            dve.sem_inc(keys_read, 1)
            dve.sem_inc(chunk_added, 1)
            dve.wait_ge(iota_ready, 1)
            own_edges = dve.value_load(k.edge_counts[0:1, 0:1], min_val=1, max_val=E)
            kept = dve.value_load(k.edge_counts[0:1, 1:2], min_val=1, max_val=E)
            with dve.Fori(0, CHUNKS) as c:
                with dve.If(c * CHUNK < kept):
                    wait_alone(dve, keys_in, c * 16 + 16, k.passed)
                    with dve.If(c * CHUNK < own_edges):
                        dve.tensor_scalar(source_i[:, :], keys[:, :], SRC_MASK, None, ALU.bitwise_and)
                        dve.drain()
                        dve.tensor_scalar(sources[:, bass.ds(c * P, P)], source_i[:, :], float(TOK - 1), None,
                                          ALU.min).then_inc(source_ready, 1)
                    dve.tensor_scalar(token[:, :], keys[:, :], SRC_BITS, None,
                                      ALU.logical_shift_right).then_inc(keys_read, 1)
                    dve.drain()
                    dve.tensor_scalar(token[:, :], token[:, :], float(KEY_BASE), None, ALU.subtract)
                    dve.drain()
                    dve.tensor_scalar(high_i[:, :], token[:, :], 7, None, ALU.logical_shift_right)
                    dve.tensor_scalar(low_i[:, :], token[:, :], P - 1, None, ALU.bitwise_and)
                    dve.drain()
                    dve.tensor_copy(high[:, :], high_i[:, :])
                    dve.tensor_copy(low[:, :], low_i[:, :])
                    dve.drain()
                    for g in range(GROUPS):
                        dve.wait_ge(hot_free, c * GROUPS + g + 1)
                        for i in range(GROUP):
                            j = GROUP * g + i
                            dve.tensor_scalar(hot_high[:, j % RING, :], iota_high[:, :], high[:, j:j + 1], None,
                                              ALU.is_equal)
                            last = dve.tensor_scalar(hot_low[:, j % RING, :], iota_low[:, :], low[:, j:j + 1],
                                                     None, ALU.is_equal)
                        last.then_inc(hot_ready, 1)
                    dve.wait_ge(hot_free, c * GROUPS + GROUPS + RING // GROUP)
                    dve.tensor_tensor(counts[:, :], counts[:, :], counts_ps[:, :], ALU.add).then_inc(chunk_added, 1)
                    dve.drain()
            dve.sem_inc(counts_whole, 1)
            own = counts[:, 0:TILES]
            dve.wait_ge(sums_ready, 1)
            dve.tensor_copy(column[:, :], column_ps[:, :])
            dve.drain()
            dve.tensor_tensor_scan(running[:, :], column[:, :], column[:, :], 0.0, ALU.add, ALU.bypass)
            dve.tensor_scalar(none[:, :], own, 0.5, float(2 * E), ALU.is_lt, ALU.mult)
            dve.drain()
            dve.tensor_tensor(first[:, :], running[:, :], column[:, :], ALU.subtract)
            dve.tensor_scalar(k.has_own[:, :], own, 0.5, None, ALU.is_gt)
            dve.tensor_scalar(k.has_last[:, :], counts[:, TILES:KINDS], 0.5, None, ALU.is_gt)
            dve.tensor_copy(k.count_last[:, :], counts[:, TILES:KINDS])
            dve.drain()
            dve.tensor_tensor(first[:, :], first[:, :], within_ps[:, :], ALU.add)
            dve.drain()
            dve.tensor_tensor(k.first_place[:, :], first[:, :], none[:, :], ALU.add)
            dve.tensor_tensor(running[:, :], first[:, :], own, ALU.add)
            dve.drain()
            dve.scalar_tensor_tensor(k.last_place[:, :], running[:, :], 1.0, k.has_own[:, :], ALU.subtract, ALU.mult)

        @block.tensor
        def _(pe):
            pe.sem_inc(hot_free, RING // GROUP)
            kept = pe.value_load(k.edge_counts[0:1, 1:2], min_val=1, max_val=E)
            with pe.Fori(0, CHUNKS) as c:
                with pe.If(c * CHUNK < kept):
                    pe.wait_ge(chunk_added, c + 1)
                    for g in range(GROUPS):
                        pe.wait_ge(hot_ready, c * GROUPS + g + 1)
                        for i in range(GROUP):
                            j = GROUP * g + i
                            mm = pe.matmul(counts_ps[:, :], hot_low[:, j % RING, :], hot_high[:, j % RING, :],
                                           start=(j == 0), stop=(j == P - 1))
                        mm.then_inc(hot_free, 1)
            pe.wait_ge(counts_whole, 1)
            pe.wait_ge(before_ready, 2)
            pe.matmul(within_ps[:, :], before[:, :], counts[:, 0:TILES], start=True, stop=True)
            pe.matmul(column_ps[:, :], k.ones_f[:, :], counts[:, 0:TILES], start=True,
                      stop=True).then_inc(sums_ready, 1)


def wait_alone(eng, sem, value, passed):
    eng.wait_ge(sem, value)
    eng.sem_inc(passed, 1)


UNROLL = 8


def over_tiles(eng, stages):
    for img in range(IMGS):
        with eng.Fori(0, ROW_GROUPS // UNROLL) as i:
            for step in range(UNROLL + max(lag for _, lag in stages)):
                for body, lag in stages:
                    u = step - lag
                    if 0 <= u < UNROLL:
                        body(img, i * UNROLL + u, i * UNROLL + (img * ROW_GROUPS + u), u)


def layer_norm_tiles(nc, k, tokens):
    x_tiles = k.x.rearrange("b (h p) y w -> b p h (y w)", p=P)
    y_tiles = k.conv_out.rearrange("(h p) b y w -> b p h (y w)", p=P)
    BUFS, CREDIT = 4, 2
    tag = "lt_" if tokens else "lc_"
    TILE_TOKENS = GPX // P
    with ExitStack() as ctx:
        def sb(name, shape, dt):
            return ctx.enter_context(nc.sbuf_tensor(tag + name, shape, dt))

        def sem(name):
            return ctx.enter_context(nc.semaphore(tag + name))

        def ps(name, shape):
            return ctx.enter_context(nc.psum_tensor(tag + name, shape, F32))
        x = [sb(f"x{b}", [P, PARTS_C, GPX], F32) for b in range(BUFS)]
        y = [sb(f"y{b}", [P, PARTS_C, GPX], F32) for b in range(BUFS)] if tokens else x
        square = [sb(f"square{c}", [P, PARTS_C, GPX], F32) for c in range(2)]
        spread = [sb(f"spread{c}", [P, GPX], F32) for c in range(2)]
        pixels = [sb(f"pixels{c}", [W, GROUP_ROWS, C], F32) for c in range(2)]
        zeros = sb("zeros", [P, C], F32)
        mean_ps = [ps(f"mean{c}", [P, GPX]) for c in range(2)]
        var_ps = [ps(f"var{c}", [P, GPX]) for c in range(2)]
        post_ps = [ps(f"post{c}", [P, TILE_TOKENS, NODE] if tokens else [W, GROUP_ROWS, C]) for c in range(2)]
        x_in = [sem(f"x_in{b}") for b in range(BUFS)]
        rows_out = [sem(f"rows_out{b}") for b in range(BUFS)]
        sums_out = [sem(f"sums_out{b}") for b in range(BUFS)] if tokens else None
        pixels_out = None if tokens else [sem(f"pixels_out{c}") for c in range(2)]
        summed, mean_ready, squared = sem("summed"), sem("mean_ready"), sem("squared")
        centred, var_ready, spread_ready, normed, copied, posted = (
            sem(n) for n in ("centred", "var_ready", "spread_ready", "normed", "copied", "posted"))
        zero_ready, zero_out, table_out = (None, None, sem("table_out")) if tokens else (
            sem("zero_ready"), sem("zero_out"), None)
        block = ctx.enter_context(nc.Block())
        eps = k.eps_t if tokens else k.eps_c
        TILES_ALL = IMGS * ROW_GROUPS
        LOADED = 32 if tokens else 16

        @block.sync
        def _(sp):
            def load(img, g, n, u):
                b = u % BUFS
                wait_alone(sp, posted, n + 1, k.passed)
                wait_alone(sp, rows_out[b], (n - b) * (16 * PARTS_C // BUFS) + 1, k.passed)
                if tokens:
                    sp.wait_ge(sums_out[b], (n - b) * (16 // BUFS) + 1)
                    sp.dma_start(y[b][:, :, :], y_tiles[img, :, :, bass.ds(g * GPX, GPX)]).then_inc(x_in[b], 16)
                sp.dma_start(x[b][:, :, :], x_tiles[img, :, :, bass.ds(g * GPX, GPX)]).then_inc(x_in[b], 16)
            if not tokens:
                sp.wait_ge(zero_ready, 1)
                for img in range(IMGS):
                    for row in (0, H + 1):
                        for h in range(PARTS_C):
                            sp.dma_start(k.xn_rows[h * P:(h + 1) * P, img, row, :],
                                         zeros[:, 0:W]).then_inc(zero_out, 16)
                        sp.dma_start(k.xn_pixels[img, row], zeros[0:W, :]).then_inc(zero_out, 16)
            over_tiles(sp, [(load, 0)])
            if tokens:
                sp.wait_ge(copied, TILES_ALL + CREDIT)
                sp.dma_start(k.table.rearrange("(t p) r -> p t r", p=P), k.node[:, :, 0:ROW]).then_inc(table_out, 16)
                sp.wait_ge(table_out, 16)
            else:
                sp.wait_ge(zero_out, 16 * IMGS * 2 * (PARTS_C + 1))

        if not tokens:
            @block.gpsimd
            def _(pool):
                pool.memset(zeros[:, :], 0.0).then_inc(zero_ready, 1)

        @block.tensor
        def _(pe):
            pe.sem_inc(var_ready, CREDIT)
            pe.sem_inc(posted, BUFS)

            def mean(img, g, n, u):
                b, c = u % BUFS, u % 2
                if tokens:
                    pe.wait_ge(summed, n + 1)
                else:
                    pe.wait_ge(x_in[b], (n - b) * (LOADED // BUFS) + LOADED)
                pe.wait_ge(centred, n + 1)
                for h in range(PARTS_C):
                    mm = pe.matmul(mean_ps[c][:, :], k.mean_c[:, :], x[b][:, h, :], start=(h == 0), stop=(h == 1))
                mm.then_inc(mean_ready, 1)

            def variance(img, g, n, u):
                c = u % 2
                pe.wait_ge(squared, n + 1)
                pe.wait_ge(spread_ready, n + 1)
                for h in range(PARTS_C):
                    mm = pe.matmul(var_ps[c][:, :], k.mean_c[:, :], square[c][:, h, :], start=(h == 0),
                                   stop=(h == 1))
                mm.then_inc(var_ready, 1)

            def post(img, g, n, u):
                b, c = u % BUFS, u % 2
                pe.wait_ge(normed, n + 1 + CREDIT)
                pe.wait_ge(copied, n + 1)
                if tokens:
                    for t in range(TILE_TOKENS):
                        for h in range(PARTS_C):
                            mm = pe.matmul(post_ps[c][:, t, :], y[b][:, h, t * P:(t + 1) * P],
                                           k.w_graph[:, h, :], start=(h == 0), stop=(h == 1))
                else:
                    for r in range(GROUP_ROWS):
                        for h in range(PARTS_C):
                            mm = pe.transpose(post_ps[c][:, r, h * P:(h + 1) * P], x[b][:, h, r * W:(r + 1) * W],
                                              k.ident[:, :])
                mm.then_inc(posted, 1)
            over_tiles(pe, [(mean, 0), (variance, 1), (post, 2)])

        @block.vector
        def _(dve):
            dve.sem_inc(centred, CREDIT)
            dve.sem_inc(normed, CREDIT)

            def add_conv(img, g, n, u):
                b = u % BUFS
                dve.wait_ge(x_in[b], (n - b) * (LOADED // BUFS) + LOADED)
                for h in range(PARTS_C):
                    dve.tensor_scalar(y[b][:, h, :], y[b][:, h, :], k.bn_scale[:, h:h + 1], k.bn_shift[:, h:h + 1],
                                      ALU.mult, ALU.add)
                dve.drain()
                dve.tensor_tensor(x[b][:, :, :], x[b][:, :, :], y[b][:, :, :], ALU.add).then_inc(summed, 1)

            def centre(img, g, n, u):
                b, c = u % BUFS, u % 2
                dve.wait_ge(mean_ready, n + 1)
                dve.tensor_tensor(y[b][:, :, :], x[b][:, :, :],
                                  mean_ps[c][:, :].unsqueeze(1).to_broadcast([P, PARTS_C, GPX]),
                                  ALU.subtract).then_inc(centred, 1)

            def normalise(img, g, n, u):
                b, c = u % BUFS, u % 2
                dve.wait_ge(spread_ready, n + 1 + CREDIT)
                dve.reciprocal(spread[c][:, :], spread[c][:, :])
                dve.drain()
                dve.tensor_tensor(y[b][:, :, :], y[b][:, :, :],
                                  spread[c][:, :].unsqueeze(1).to_broadcast([P, PARTS_C, GPX]),
                                  ALU.mult).then_inc(normed, 1)
            over_tiles(dve, ([(add_conv, 0)] if tokens else []) + [(centre, 1), (normalise, 2)])

        @block.scalar
        def _(act):
            act.sem_inc(spread_ready, CREDIT)
            act.sem_inc(copied, CREDIT)
            for b in range(BUFS):
                act.sem_inc(rows_out[b], 1)
                if tokens:
                    act.sem_inc(sums_out[b], 1)
            if not tokens:
                for c in range(2):
                    act.sem_inc(pixels_out[c], 1)

            def squares(img, g, n, u):
                b, c = u % BUFS, u % 2
                act.wait_ge(centred, n + 1 + CREDIT)
                act.wait_ge(var_ready, n + 1)
                act.activation(square[c][:, :, :], y[b][:, :, :], ACT.Square).then_inc(squared, 1)

            def root(img, g, n, u):
                c = u % 2
                act.wait_ge(var_ready, n + 1 + CREDIT)
                act.wait_ge(normed, n + 1)
                act.activation(spread[c][:, :], var_ps[c][:, :], ACT.Sqrt, bias=eps[:, :]).then_inc(spread_ready, 1)

            def store(img, g, n, u):
                b, c = u % BUFS, u % 2
                act.wait_ge(normed, n + 1 + CREDIT)
                for h in range(PARTS_C):
                    rows = (k.ln_rows if tokens else k.xn_rows)[h * P:(h + 1) * P, img]
                    rows = rows[:, bass.ds(g * GROUP_ROWS, GROUP_ROWS) if tokens else
                                bass.ds(g * GROUP_ROWS + 1, GROUP_ROWS), :]
                    act.dma_start(rows, y[b][:, h, :].rearrange("p (r w) -> p r w", w=W)).then_inc(rows_out[b], 16)
                if tokens:
                    act.dma_start(k.residual[img, :, :, bass.ds(g * GPX, GPX)], x[b][:, :, :]
                                  ).then_inc(sums_out[b], 16)
                act.wait_ge(posted, n + 1 + BUFS)
                if tokens:
                    act.activation(k.node[:, bass.ds(n * TILE_TOKENS, TILE_TOKENS), :], post_ps[c][:, :, :],
                                   ACT.Copy).then_inc(copied, 1)
                else:
                    act.wait_ge(pixels_out[c], (n - c) * (16 // 2) + 1)
                    act.activation(pixels[c][:, :, :], post_ps[c][:, :, :], ACT.Copy).then_inc(copied, 1)
                    act.wait_ge(copied, n + 1 + CREDIT)
                    act.dma_start(k.xn_pixels[img, bass.ds(g * GROUP_ROWS + 1, GROUP_ROWS)].rearrange(
                        "r w c -> w r c"), pixels[c][:, :, :]).then_inc(pixels_out[c], 16)
            over_tiles(act, [(squares, 1), (root, 2), (store, 3)])
            for b in range(BUFS):
                act.wait_ge(rows_out[b], TILES_ALL // BUFS * 16 * PARTS_C + 1)
                if tokens:
                    act.wait_ge(sums_out[b], TILES_ALL // BUFS * 16 + 1)
            if not tokens:
                for c in range(2):
                    act.wait_ge(pixels_out[c], TILES_ALL // 2 * 16 + 1)


def token_constants(nc, k):
    with ExitStack() as ctx:
        def sb(name, shape, dt):
            return ctx.enter_context(nc.sbuf_tensor("tc_" + name, shape, dt))

        def sem(name):
            return ctx.enter_context(nc.semaphore("tc_" + name))
        gamma, beta = sb("gamma", [P, PARTS_C], F32), sb("beta", [P, PARTS_C], F32)
        moments = sb("moments", [P, PARTS_C, 2], F32)
        spread = sb("spread", [P, PARTS_C], F32)
        gat_t = sb("gat_t", [HE, C], F32)
        attention = sb("attention", [HE, 2], F32)
        blocks = sb("blocks", [HE, 2, HEADS], F32)
        part_ps = [ctx.enter_context(nc.psum_tensor(f"tc_part{h}", [P, 2 * HEADS], F32)) for h in range(PARTS_C)]
        loaded, var_ready, root_ready, ones_ready, blocks_made, blocks_ready, parts_ready = (
            sem(n) for n in ("loaded", "var_ready", "root_ready", "ones_ready", "blocks_made", "blocks_ready",
                             "parts_ready"))
        block = ctx.enter_context(nc.Block())

        @block.sync
        def _(sp):
            with nc.allow_non_contiguous_dma(reason="a few hundred parameters"):
                sp.dma_start(gamma[:, :], k.gamma.rearrange("(h p) -> p h", p=P)).then_inc(loaded, 16)
                sp.dma_start(beta[:, :], k.beta.rearrange("(h p) -> p h", p=P)).then_inc(loaded, 16)
                sp.dma_start(gat_t[:, :], k.w_gat.rearrange("c o -> o c")).then_inc(loaded, 16)
                sp.dma_start(attention[:, 0:1], k.att_src.rearrange("h (e a) -> (h e) a", a=1)).then_inc(loaded, 16)
                sp.dma_start(attention[:, 1:2], k.att_dst.rearrange("h (e a) -> (h e) a", a=1)).then_inc(loaded, 16)
                sp.dma_start(k.w_graph[:, :, 0:HE], k.w_gat.rearrange("(h p) o -> p h o", p=P)).then_inc(loaded, 16)

        @block.gpsimd
        def _(pool):
            pool.memset(blocks[:, :, :], 1.0).then_inc(ones_ready, 1)
            pool.wait_ge(ones_ready, 1)
            pool.affine_select(out=blocks[:, :, :], in_=blocks[:, :, :], compare_op=ALU.is_ge, fill=0.0, base=0,
                               pattern=[[0, 2], [-EXPERTS, HEADS]], channel_multiplier=1).then_inc(blocks_made, 1)
            pool.wait_ge(blocks_made, 1)
            pool.affine_select(out=blocks[:, :, :], in_=blocks[:, :, :], compare_op=ALU.is_ge, fill=0.0,
                               base=EXPERTS - 1, pattern=[[0, 2], [EXPERTS, HEADS]],
                               channel_multiplier=-1).then_inc(blocks_made, 1)

        @block.vector
        def _(dve):
            for h in range(PARTS_C):
                dve.bn_aggr(moments[:, h, :], k.y_stats[:, h, :, :].rearrange("p n s -> p (n s)"))
            dve.wait_ge(loaded, 96)
            dve.wait_ge(blocks_made, 2)
            for s in range(2):
                last = dve.tensor_scalar(blocks[:, s, :], blocks[:, s, :], attention[:, s:s + 1], None, ALU.mult)
            last.then_inc(blocks_ready, 1)
            dve.drain()
            dve.tensor_scalar(spread[:, :], moments[:, :, 1], BN_EPS, None, ALU.add).then_inc(var_ready, 1)
            dve.wait_ge(root_ready, 1)
            dve.reciprocal(spread[:, :], spread[:, :])
            dve.drain()
            dve.tensor_tensor(k.bn_scale[:, :], spread[:, :], gamma[:, :], ALU.mult)
            dve.drain()
            dve.tensor_tensor(spread[:, :], moments[:, :, 0], k.bn_scale[:, :], ALU.mult)
            dve.drain()
            dve.tensor_tensor(k.bn_shift[:, :], beta[:, :], spread[:, :], ALU.subtract)
            dve.wait_ge(parts_ready, 1)
            for h in range(PARTS_C):
                dve.tensor_copy(k.w_graph[:, h, HE:NODE], part_ps[h][:, :])

        @block.scalar
        def _(act):
            act.wait_ge(var_ready, 1)
            act.activation(spread[:, :], spread[:, :], ACT.Sqrt).then_inc(root_ready, 1)

        @block.tensor
        def _(pe):
            pe.wait_ge(loaded, 96)
            pe.wait_ge(blocks_ready, 1)
            for h in range(PARTS_C):
                mm = pe.matmul(part_ps[h][:, :], gat_t[:, h * P:(h + 1) * P],
                               blocks[:, :, :].rearrange("p s h -> p (s h)"), start=True, stop=True)
            mm.then_inc(parts_ready, 1)


def guide_taps(nc, k):
    with ExitStack() as ctx:
        def sb(name, shape, dt):
            return ctx.enter_context(nc.sbuf_tensor(name, shape, dt))

        def sem(name):
            return ctx.enter_context(nc.semaphore(name))
        w_cat = sb("gt_w_cat", [P, PARTS_C, TAPS, GUIDES], F32)
        strip = [sb(f"gt_strip{u}", [P, PARTS_C, GROUP_ROWS + 2, W + 2], F32) for u in range(2)]
        guide = [sb(f"gt_guide{u}", [GUIDES, GPX], F32) for u in range(2)]
        SETS = 2
        SOFTMAXES = GROUP_ROWS * BRANCHES
        highest = sb("gt_highest", [W, SOFTMAXES], F32)
        total = sb("gt_total", [W, SOFTMAXES], F32)
        weight = [sb(f"gt_weight{u}", [W, SOFTMAXES, TAPS], F32) for u in range(2)]
        rest = sb("gt_rest", [W, GROUP_ROWS, GUIDES], F32)
        parts = [sb(f"gt_parts{u}", [W, GROUP_ROWS, SPLITS * GUIDES], BF16) for u in range(2)]
        left = [sb(f"gt_left{u}", [SPLITS * LEFT, GPX], BF16) for u in range(2)]
        right = [sb(f"gt_right{u}", [SPLITS * RIGHT, GPX], BF16) for u in range(2)]
        conv_ps = [ctx.enter_context(nc.psum_tensor(f"gt_conv{u}", [GUIDES, GPX], F32)) for u in range(2)]
        pixel_ps = [ctx.enter_context(nc.psum_tensor(f"gt_pixel{u}", [W, SOFTMAXES, TAPS], F32)) for u in range(2)]
        left_ps = [ctx.enter_context(nc.psum_tensor(f"gt_left_ps{u}", [SPLITS * LEFT, GPX], BF16)) for u in range(2)]
        right_ps = [ctx.enter_context(nc.psum_tensor(f"gt_right_ps{u}", [SPLITS * RIGHT, GPX], BF16))
                    for u in range(2)]
        w_in = sem("gt_w_in")
        strip_in = [sem(f"gt_strip_in{u}") for u in range(2)]
        left_out = [sem(f"gt_left_out{u}") for u in range(2)]
        right_out = [sem(f"gt_right_out{u}") for u in range(2)]
        edges_zero, conv_ready, guide_ready, pixel_ready, shifted, raised, parts_ready, taps_ready, taps_copied = (
            sem("gt_" + n) for n in ("edges_zero", "conv_ready", "guide_ready", "pixel_ready", "shifted", "raised",
                                     "parts_ready", "taps_ready", "taps_copied"))
        block = ctx.enter_context(nc.Block())

        @block.sync
        def _(sp):
            sp.dma_start(w_cat[:, :, :, :], k.w_cat_t.rearrange("(h p) t o -> p h t o", p=P)).then_inc(w_in, 16)
            sp.wait_ge(edges_zero, 1)

            def body(img, g, n, u):
                sp.wait_ge(conv_ready, n + 1)
                for h in range(PARTS_C):
                    sp.dma_start(strip[u % 2][:, h, :, 1:W + 1],
                                 k.xn_rows[h * P:(h + 1) * P, img, bass.ds(g * GROUP_ROWS, GROUP_ROWS + 2), :]
                                 ).then_inc(strip_in[u % 2], 16)
            over_tiles(sp, [(body, 0)])

        @block.tensor
        def _(pe):
            for freed in (conv_ready, pixel_ready, taps_ready):
                pe.sem_inc(freed, SETS)
            pe.wait_ge(w_in, 16)

            def conv(img, g, n, u):
                b = u % 2
                pe.wait_ge(strip_in[b], (n - b) * 16 + 32)
                pe.wait_ge(guide_ready, n + 1)
                step = 0
                for h in range(PARTS_C):
                    for t in range(TAPS):
                        dy, dx = t // 3, t % 3
                        mm = pe.matmul(conv_ps[b][:, :], w_cat[:, h, t, :],
                                       strip[b][:, h, dy:dy + GROUP_ROWS, dx:dx + W],
                                       start=(step == 0), stop=(step == PARTS_C * TAPS - 1))
                        step += 1
                mm.then_inc(conv_ready, 1)

            def to_pixels(img, g, n, u):
                b = u % 2
                pe.wait_ge(guide_ready, n + 1 + SETS)
                wait_alone(pe, shifted, n + 1, k.passed)
                for r in range(GROUP_ROWS):
                    mm = pe.transpose(pixel_ps[b][:, r * BRANCHES:(r + 1) * BRANCHES, :].rearrange("p a b -> p (a b)"),
                                      guide[b][:, r * W:(r + 1) * W], k.ident[0:GUIDES, 0:GUIDES])
                mm.then_inc(pixel_ready, 1)

            def to_rows(img, g, n, u):
                b = u % 2
                pe.wait_ge(parts_ready, n + 1)
                pe.wait_ge(taps_copied, n + 1)
                for r in range(GROUP_ROWS):
                    pe.transpose(left_ps[b][:, r * W:(r + 1) * W], parts[b][:, r, 0:SPLITS * LEFT], k.ident_b[0:W, 0:W])
                    mm = pe.transpose(right_ps[b][:, r * W:(r + 1) * W], parts[b][:, r, SPLITS * LEFT:],
                                      k.ident_b[0:W, 0:W])
                mm.then_inc(taps_ready, 1)
            over_tiles(pe, [(conv, 0), (to_pixels, 1), (to_rows, 2)])

        @block.scalar
        def _(act):
            act.sem_inc(guide_ready, SETS)
            act.sem_inc(taps_copied, SETS)
            for b in range(2):
                act.sem_inc(left_out[b], 1)
                act.sem_inc(right_out[b], 1)
            def copy_guide(img, g, n, u):
                b = u % 2
                act.wait_ge(conv_ready, n + 1 + SETS)
                act.wait_ge(pixel_ready, n + 1)
                act.activation(guide[b][:, :], conv_ps[b][:, :], ACT.Copy).then_inc(guide_ready, 1)

            def exponent(img, g, n, u):
                act.wait_ge(shifted, n + 1 + SETS)
                act.activation(weight[u % 2][:, :, :], weight[u % 2][:, :, :], ACT.Exp).then_inc(raised, 1)

            def copy_taps(img, g, n, u):
                b = u % 2
                act.wait_ge(taps_ready, n + 1 + SETS)
                act.wait_ge(left_out[b], (n - b) * 8 + 1)
                act.wait_ge(right_out[b], (n - b) * 8 + 1)
                act.activation(left[b][:, :], left_ps[b][:, :], ACT.Copy)
                act.activation(right[b][:, :], right_ps[b][:, :], ACT.Copy).then_inc(taps_copied, 1)
                act.wait_ge(taps_copied, n + 1 + SETS)
                act.dma_start(k.taps_left[:, bass.ds(g * GPX + img * PIX, GPX)], left[b][:, :]).then_inc(left_out[b], 16)
                act.dma_start(k.taps_right[:, bass.ds(g * GPX + img * PIX, GPX)],
                              right[b][:, :]).then_inc(right_out[b], 16)
            over_tiles(act, [(copy_guide, 0), (exponent, 1), (copy_taps, 2)])
            for b in range(2):
                act.wait_ge(left_out[b], IMGS * ROW_GROUPS * 8 + 1)
                act.wait_ge(right_out[b], IMGS * ROW_GROUPS * 8 + 1)

        @block.vector
        def _(dve):
            for b in range(2):
                dve.memset(strip[b][:, :, :, :], 0.0)
            dve.drain()
            dve.sem_inc(edges_zero, 1)
            dve.sem_inc(shifted, SETS)

            def body(img, g, n, u):
                b = u % 2
                dve.wait_ge(pixel_ready, n + 1 + SETS)
                dve.tensor_reduce(highest[:, :], pixel_ps[b][:, :, :], AX_X, ALU.max)
                dve.drain()
                dve.tensor_tensor(weight[b][:, :, :], pixel_ps[b][:, :, :],
                                  highest[:, :].unsqueeze(2).to_broadcast([W, SOFTMAXES, TAPS]),
                                  ALU.subtract).then_inc(shifted, 1)
                dve.wait_ge(raised, n + 1)
                dve.tensor_reduce(total[:, :], weight[b][:, :, :], AX_X, ALU.add)
                dve.drain()
                dve.reciprocal(total[:, :], total[:, :])
                dve.drain()
                dve.tensor_tensor(weight[b][:, :, :], weight[b][:, :, :],
                                  total[:, :].unsqueeze(2).to_broadcast([W, SOFTMAXES, TAPS]), ALU.mult)
                dve.drain()
                dve.wait_ge(taps_ready, n + 1)
                value = weight[b][:, :, :].rearrange("p (r i) t -> p r (i t)", i=BRANCHES)
                for s in range(SPLITS):
                    at = SPLITS * LEFT + s * RIGHT
                    lots = ((slice(0, LEFT), parts[b][:, :, s * LEFT:(s + 1) * LEFT]),
                            (slice(LEFT, GUIDES), parts[b][:, :, at:at + RIGHT]))
                    for lot, part in lots:
                        dve.tensor_copy(part, value[:, :, lot])
                    dve.drain()
                    if s < SPLITS - 1:
                        for lot, part in lots:
                            dve.tensor_tensor(rest[:, :, lot], value[:, :, lot], part, ALU.subtract)
                        dve.drain()
                        value = rest[:, :, :]
                dve.sem_inc(parts_ready, 1)
            over_tiles(dve, [(body, 0)])


CLASSES = 6
CLASS_ROWS = H // CLASSES
CLASS_GROUPS = CLASS_ROWS // GROUP_ROWS


def branch_masks(nc, k):
    with ExitStack() as ctx:
        zeroed = ctx.enter_context(nc.semaphore("bm_zeroed"))
        made = ctx.enter_context(nc.semaphore("bm_made"))
        wide = ctx.enter_context(nc.sbuf_tensor("bm_wide", [W, len(k.offsets), GPX], F32))
        block = ctx.enter_context(nc.Block())

        @block.gpsimd
        def _(pool):
            pool.memset(wide[:, :, :], 0.0)
            pool.memset(k.pick_left[:, :, :], 0.0)
            pool.memset(k.pick_right[:, :, :], 0.0).then_inc(zeroed, 1)
            pool.wait_ge(zeroed, 1)
            for n, dx in enumerate(k.offsets):
                v = wide[:, n, :].rearrange("p (r w) -> p r w", w=W)
                pool.affine_select(out=v, in_=v, compare_op=ALU.not_equal, fill=1.0, base=-dx,
                                   pattern=[[0, GROUP_ROWS], [-1, W]], channel_multiplier=1)
            for pick, taps in ((k.pick_left, LEFT), (k.pick_right, RIGHT)):
                for s in range(SPLITS):
                    pool.affine_select(out=pick[:, :, :], in_=pick[:, :, :], compare_op=ALU.not_equal, fill=1.0,
                                       base=-s * taps, pattern=[[-1, taps], [0, W]], channel_multiplier=1
                                       ).then_inc(made, 1)
                    pool.wait_ge(made, (s + 1) if taps == LEFT else SPLITS + s + 1)

        @block.vector
        def _(dve):
            dve.wait_ge(made, 1)
            dve.tensor_copy(k.masks[:, :, :], wide[:, :, :])


def dilated_branches(nc, k):
    SETS = 2
    PAIR = 2
    assert CLASSES % PAIR == 0
    with ExitStack() as ctx:
        def sb(name, shape, dt):
            return ctx.enter_context(nc.sbuf_tensor(name, shape, dt))

        def sem(name):
            return ctx.enter_context(nc.semaphore(name))
        w_scale = sb("db_w_scale", [P, (BRANCHES + 1) * PARTS_C, C], F32)
        own, above, below = ([sb(f"db_{name}{c}", [W, CLASS_ROWS, C], F32) for c in range(PAIR)]
                             for name in ("own", "above", "below"))
        rows = [sb(f"db_rows{c}", [P, PARTS_C, CLASS_ROWS, W], F32) for c in range(PAIR)]
        left = [sb(f"db_left{c}", [SPLITS * LEFT, CLASS_ROWS, W], BF16) for c in range(PAIR)]
        right = [sb(f"db_right{c}", [SPLITS * RIGHT, CLASS_ROWS, W], BF16) for c in range(PAIR)]
        diagonals = [sb(f"db_diagonals{i}", [W, 3, GPX], F32) for i in range(BRANCHES)]
        branch = [sb(f"db_branch{u}", [P, PARTS_C, GPX], F32) for u in range(SETS)]
        y = [sb(f"db_y{u}", [P, PARTS_C, GPX], F32) for u in range(SETS)]
        tap_ps = [ctx.enter_context(nc.psum_tensor(f"db_tap{u}", [W, GPX], F32)) for u in range(2)]
        branch_ps = [[ctx.enter_context(nc.psum_tensor(f"db_branch_ps{u}{h}", [P, GPX], F32))
                      for h in range(PARTS_C)] for u in range(2)]
        y_ps = [ctx.enter_context(nc.psum_tensor(f"db_y_ps{h}", [P, GPX], F32)) for h in range(PARTS_C)]
        w_in, y_copied, y_used = (sem("db_" + n) for n in ("w_in", "y_copied", "y_used"))
        class_in = [sem(f"db_class_in{c}") for c in range(PAIR)]
        zeroed, tap_ready, tap_placed, branch_ready, branch_copied, branch_used = (
            sem("db_" + n) for n in ("zeroed", "tap_ready", "tap_placed", "branch_ready", "branch_copied",
                                     "branch_used"))
        y_out = [sem(f"db_y_out{u}") for u in range(SETS)]
        LOADS = 3 + PARTS_C + 2
        CLASS_STEPS = CLASS_GROUPS * BRANCHES
        STEPS = PAIR * CLASS_STEPS
        GROUPS = PAIR * CLASS_GROUPS
        USED = CLASS_STEPS + SETS
        block = ctx.enter_context(nc.Block())

        def class_pairs(eng, body):
            for img in range(IMGS):
                with eng.Fori(0, CLASSES // PAIR) as i:
                    body(img, i, i + img * (CLASSES // PAIR))

        def place(step):
            group, b = divmod(step, BRANCHES)
            return group // CLASS_GROUPS, group % CLASS_GROUPS, b

        @block.sync
        def _(sp):
            sp.dma_start(w_scale[:, :, :], k.w_scale_t.rearrange("(c p) o -> p c o", p=P)).then_inc(w_in, 16)

            def body(img, i, n):
                for c in range(PAIR):
                    r = i * PAIR + c
                    wait_alone(sp, branch_used, n * STEPS + (USED + (c - 1) * CLASS_STEPS), k.passed)
                    pixels = k.xn_pixels[img, 0:H].rearrange("(k s) w c -> w s k c", s=CLASSES)
                    pixels_1 = k.xn_pixels[img, 1:H + 1].rearrange("(k s) w c -> w s k c", s=CLASSES)
                    pixels_2 = k.xn_pixels[img, 2:H + 2].rearrange("(k s) w c -> w s k c", s=CLASSES)
                    for tile, source in ((above[c], pixels), (own[c], pixels_1), (below[c], pixels_2)):
                        sp.dma_start(tile[:, :, :], source[:, bass.ds(r, 1), :, :].rearrange(
                            "w s k c -> w (s k) c")).then_inc(class_in[c], 16)
                    by_rows = k.xn_rows[:, img, 1:H + 1, :].rearrange("(h p) (k s) w -> p h s k w", p=P, s=CLASSES)
                    for h in range(PARTS_C):
                        sp.dma_start(rows[c][:, h, :, :], by_rows[:, h, bass.ds(r, 1), :, :].rearrange(
                            "p s k w -> p (s k) w")).then_inc(class_in[c], 16)
                    for tile, source in ((left[c], k.taps_left), (right[c], k.taps_right)):
                        v = source[:, img * PIX:(img + 1) * PIX].rearrange("t (k s w) -> t s k w", s=CLASSES, w=W)
                        sp.dma_start(tile[:, :, :], v[:, bass.ds(r, 1), :, :].rearrange("t s k w -> t (s k) w")
                                     ).then_inc(class_in[c], 16)
            class_pairs(sp, body)

        @block.tensor
        def _(pe):
            pe.wait_ge(w_in, 16)
            pe.wait_ge(zeroed, 1)
            pe.sem_inc(branch_used, USED)

            def body(img, i, n):
                def spread_tap(step, at):
                    c, q, b = place(step)
                    if step % CLASS_STEPS == 0 and at == 0:
                        pe.wait_ge(class_in[c], n * (16 * LOADS) + 16 * LOADS)
                    m = step * TAPS + at
                    t = at % 3 * 3 + at // 3
                    pick, taps, base = ((k.pick_left, left[c], b * TAPS) if b < LEFT_BRANCHES else
                                        (k.pick_right, right[c], (b - LEFT_BRANCHES) * TAPS))
                    pe.wait_ge(tap_placed, n * (STEPS * TAPS) + m + 1)
                    pe.matmul(tap_ps[m % 2][:, :], pick[:, base + t, :],
                              taps[:, q * GROUP_ROWS:(q + 1) * GROUP_ROWS, :],
                              start=True, stop=True).then_inc(tap_ready, 1)

                def gather_rows(step):
                    c, q, b = place(step)
                    jump = DILATIONS[b] // CLASSES
                    pe.wait_ge(branch_copied, n * STEPS + step + 1)
                    pe.wait_ge(tap_placed, n * (STEPS * TAPS) + (step + 1) * TAPS + 2)
                    spreads = TAPS if step + 1 < STEPS else 0
                    parts = PARTS_C * GROUP_ROWS
                    for h in range(PARTS_C):
                        for i in range(GROUP_ROWS):
                            row = q * GROUP_ROWS + i
                            if DILATIONS[b] == 1:
                                used = [(0, above[c], row), (1, own[c], row), (2, below[c], row)]
                            else:
                                used = [(dy, own[c], row + (dy - 1) * jump) for dy in range(3)
                                        if 0 <= row + (dy - 1) * jump < CLASS_ROWS]
                            for at, (dy, tile, source) in enumerate(used):
                                mm = pe.matmul(branch_ps[step % 2][h][:, i * W:(i + 1) * W],
                                               tile[:, source, h * P:(h + 1) * P],
                                               diagonals[b][:, dy, i * W:(i + 1) * W],
                                               start=(at == 0), stop=(at == len(used) - 1))
                            done = h * GROUP_ROWS + i
                            if done == parts - 1:
                                mm.then_inc(branch_ready, 1)
                            for at in range(spreads * done // parts, spreads * (done + 1) // parts):
                                spread_tap(step + 1, at)

                def scale(step):
                    c, q, b = place(step)
                    if b == 0:
                        pe.wait_ge(y_copied, n * GROUPS + (c * CLASS_GROUPS + q + 1))
                        for o in range(PARTS_C):
                            for h in range(PARTS_C):
                                pe.matmul(y_ps[o][:, :], w_scale[:, h, o * P:(o + 1) * P],
                                          rows[c][:, h, q * GROUP_ROWS:(q + 1) * GROUP_ROWS, :],
                                          start=(h == 0), stop=False)
                    pe.wait_ge(branch_copied, n * STEPS + step + 1 + SETS)
                    for o in range(PARTS_C):
                        for h in range(PARTS_C):
                            last = b == BRANCHES - 1 and h == PARTS_C - 1
                            mm = pe.matmul(y_ps[o][:, :], w_scale[:, (b + 1) * PARTS_C + h, o * P:(o + 1) * P],
                                           branch[step % 2][:, h, :], start=False, stop=last)
                    mm.then_inc(branch_used, 1)

                for at in range(TAPS):
                    spread_tap(0, at)
                for step in range(STEPS):
                    gather_rows(step)
                    if step >= 1:
                        scale(step - 1)
                scale(STEPS - 1)
            class_pairs(pe, body)

        @block.vector
        def _(dve):
            for b in range(BRANCHES):
                dve.memset(diagonals[b][:, :, :], 0.0)
            dve.drain()
            dve.sem_inc(zeroed, 1)
            dve.sem_inc(tap_placed, 2)

            def body(img, i, n):
                for step in range(STEPS):
                    c, q, b = place(step)
                    for at in range(TAPS):
                        dx, dy = divmod(at, 3)
                        m = step * TAPS + at
                        if dy == 0:
                            dve.drain()
                        mask = k.offsets.index((dx - 1) * DILATIONS[b])
                        wait_alone(dve, tap_ready, n * (STEPS * TAPS) + m + 1, k.passed)
                        dve.copy_predicated(diagonals[b][:, dy, :], k.masks[:, mask, :],
                                            tap_ps[m % 2][:, :]).then_inc(tap_placed, 1)
                    if b == 1 and step >= BRANCHES:
                        statistics(n, step // BRANCHES - 1)
                statistics(n, GROUPS - 1)

            def statistics(n, q):
                dve.wait_ge(y_copied, n * GROUPS + q + 2)
                for h in range(PARTS_C):
                    last = dve.bn_stats(k.y_stats[:, h, bass.ds(n * GROUPS + q, 1), :].rearrange(
                        "p a s -> p (a s)"), y[q % 2][:, h, :])
                last.then_inc(y_used, 1)
            class_pairs(dve, body)

        @block.scalar
        def _(act):
            act.sem_inc(y_used, 2)
            act.sem_inc(branch_copied, SETS)
            act.sem_inc(y_copied, 1)
            for u in range(SETS):
                act.sem_inc(y_out[u], 1)

            def body(img, i, n):
                for step in range(STEPS):
                    act.wait_ge(branch_ready, n * STEPS + step + 1)
                    act.wait_ge(branch_used, n * STEPS + (step + 1 + CLASS_STEPS))
                    for h in range(PARTS_C):
                        last = act.activation(branch[step % 2][:, h, :], branch_ps[step % 2][h][:, :], ACT.Copy)
                    last.then_inc(branch_copied, 1)
                    if step % BRANCHES == 0 and step >= BRANCHES:
                        copy_y(img, i, n, step // BRANCHES - 1)
                copy_y(img, i, n, GROUPS - 1)

            def copy_y(img, i, n, group):
                c, q = divmod(group, CLASS_GROUPS)
                act.wait_ge(branch_used, n * STEPS + ((group + 1) * BRANCHES + USED))
                act.wait_ge(y_used, n * GROUPS + group + 1)
                act.wait_ge(y_out[q % 2], n * (16 * PARTS_C * GROUPS // 2) + 16 * PARTS_C * (group // 2) + 1)
                for h in range(PARTS_C):
                    last = act.activation(y[q % 2][:, h, :], y_ps[h][:, :], ACT.Copy)
                last.then_inc(y_copied, 1)
                act.wait_ge(y_copied, n * GROUPS + group + 2)
                for h in range(PARTS_C):
                    v = k.conv_out[h * P:(h + 1) * P, img, :, :].rearrange("p (k s) w -> p s k w", s=CLASSES)
                    act.dma_start(v[:, bass.ds(i * PAIR + c, 1), q * GROUP_ROWS:(q + 1) * GROUP_ROWS, :].rearrange(
                        "p s k w -> p (s k) w"), y[q % 2][:, h, :].rearrange("p (k w) -> p k w", w=W)
                        ).then_inc(y_out[q % 2], 16)
            class_pairs(act, body)
            for u in range(2):
                act.wait_ge(y_out[u], IMGS * CLASSES * PARTS_C * CLASS_GROUPS // 2 * 16 + 1)


LEAK = 0.2
FAR = 1e30


def place_scores(nc, k):
    with ExitStack() as ctx:
        placed = ctx.enter_context(nc.semaphore("ps_placed"))
        scores = ctx.enter_context(nc.sbuf_tensor("ps_scores", [P, TILES, HEADS], F32))
        scores_ready = ctx.enter_context(nc.semaphore("ps_scores_ready"))
        block = ctx.enter_context(nc.Block())

        @block.vector
        def _(dve):
            dve.tensor_copy(scores[:, :, :], k.node[:, :, HE + HEADS:NODE]).then_inc(scores_ready, 1)

        @block.gpsimd
        def _(pool):
            pool.wait_ge(scores_ready, 1)
            for t in range(TILES):
                pool.indirect_dma_start(k.dst_scores[:, :],
                                        bass.IndirectOffsetOnAxis(k.first_place[:, t:t + 1], 0),
                                        scores[:, t, :], None, bounds_check=E - 1,
                                        oob_is_err=False).then_inc(placed, 16)
            pool.wait_ge(placed, 16 * TILES)


def edge_softmax(nc, k):
    SUMS = HE + HEADS
    with ExitStack() as ctx:
        def sb(name, shape, dt):
            return ctx.enter_context(nc.sbuf_tensor("es_" + name, shape, dt))

        def sem(name):
            return ctx.enter_context(nc.semaphore("es_" + name))

        def ps(name, shape):
            return ctx.enter_context(nc.psum_tensor("es_" + name, shape, F32))
        keys, before = sb("keys", [P, P], I32), sb("before", [P, P], I32)
        given = sb("given", [P, P, HEADS], F32)
        run, run_before = sb("run", [P, P], I32), sb("run_before", [P, P], I32)
        fetched = sb("fetched", [P, P, ROW], F32)
        same_next = sb("same_next", [P, P], F32)
        given_next = sb("given_next", [P, HEADS, P], F32)
        same = sb("same", [P, HEADS, P], F32)
        given_row = sb("given_row", [P, HEADS, P], F32)
        first = sb("first", [P, 4], F32)
        penalty = sb("penalty", [P, HEADS, P], F32)
        src_score = sb("src_score", [P, HEADS, P], F32)
        dst_score = sb("dst_score", [P, HEADS, P], F32)
        score = sb("score", [P, HEADS, P], F32)
        score_0 = sb("score_0", [P, HEADS], F32)
        peak = sb("peak", [P, HEADS, P], F32)
        peak_in = sb("peak_in", [P, HEADS], F32)
        powers = sb("powers", [P, 2 * HEADS * P + HEADS], F32)
        decay = powers[:, 0:HEADS * P].rearrange("p (h j) -> p h j", h=HEADS)
        weight = powers[:, HEADS * P:2 * HEADS * P].rearrange("p (h j) -> p h j", h=HEADS)
        decay_all = powers[:, 2 * HEADS * P:]
        decay_0 = sb("decay_0", [P, SUMS], F32)
        value = sb("value", [P, SUMS, P], F32)
        value_decay = sb("value_decay", [P, SUMS, P], F32)
        sums = sb("sums", [P, SUMS, P], F32)
        ends = sb("ends", [P, 2, SUMS], F32)
        rows_out = sb("rows_out", [P, P, NODE], F32)
        factor_row = sb("factor_row", [SUMS, P], F32)
        handed = [sb("handed_score", [HEADS, P + 1], F32), sb("handed_peak", [HEADS, P + 1], F32),
                  sb("handed_sums", [SUMS, P + 1], F32)]
        turned_ps = ps("turned_ps", [SUMS, 2, P])
        back_ps = ps("back_ps", [P, SUMS])
        (chunk_in, decoded, rows_in, rows_taken, ends_ready, ends_turned, handed_ready,
         handed_turned, powers_ready, raised, rows_ready, stored) = (sem(n) for n in (
             "chunk_in", "decoded", "rows_in", "rows_taken", "ends_ready", "ends_turned",
             "handed_ready", "handed_turned", "powers_ready", "raised", "rows_ready", "stored"))
        block = ctx.enter_context(nc.Block())

        def over_chunks(eng, body):
            own = eng.value_load(k.edge_counts[0:1, 0:1], min_val=1, max_val=E)
            with eng.Fori(0, CHUNKS) as c:
                with eng.If(c * CHUNK < own):
                    body(c, own)

        @block.sync
        def _(sp):
            def load(c):
                sp.dma_start(keys[:, :], k.sorted_keys[bass.ds(c * CHUNK + P, CHUNK)].rearrange(
                    "(p f) -> p f", p=P)).then_inc(chunk_in, 16)
                sp.dma_start(before[:, :], k.sorted_keys[bass.ds(c * CHUNK + (P - 1), CHUNK)].rearrange(
                    "(p f) -> p f", p=P)).then_inc(chunk_in, 16)
                sp.dma_start(given[:, :, :], k.dst_scores[bass.ds(c * CHUNK, CHUNK), :].rearrange(
                    "(p f) h -> p f h", p=P)).then_inc(chunk_in, 16)
            def load_rows(c):
                sp.dma_start(fetched[:, :, :].rearrange("p j v -> p (j v)"),
                             k.edge_rows[bass.ds(c, 1)].rearrange("a p v -> p (a v)")).then_inc(rows_in, 16)
            load(0)
            load_rows(0)
            sp.sem_inc(stored, 1)

            def body(c, own):
                wait_alone(sp, decoded, c + 1, k.passed)
                load(c + 1)
                wait_alone(sp, rows_taken, c + 1, k.passed)
                with sp.If((c + 1) * CHUNK < own):
                    load_rows(c + 1)
                wait_alone(sp, rows_ready, c + 1, k.passed)
                sp.dma_start(k.states[bass.ds(c * CHUNK, CHUNK), :].rearrange("(p f) r -> p f r", p=P),
                             rows_out[:, :, :]).then_inc(stored, 16)
                wait_alone(sp, stored, c * 16 + 17, k.passed)
            over_chunks(sp, body)
            sp.wait_ge(chunk_in, 48)

        @block.scalar
        def _(act):
            def body(c, own):
                act.wait_ge(powers_ready, c + 1)
                act.activation(powers[:, :], powers[:, :], ACT.Exp).then_inc(raised, 1)
            over_chunks(act, body)

        @block.tensor
        def _(pe):
            def body(c, own):
                for r, channels in enumerate((HEADS, HEADS, SUMS)):
                    wait_alone(pe, ends_ready, c * 3 + r + 1, k.passed)
                    for i in range(2):
                        mm = pe.transpose(turned_ps[0:channels, i, :], ends[:, i, 0:channels], k.ident[:, :])
                    mm.then_inc(ends_turned, 1)
                    wait_alone(pe, handed_ready, c * 3 + r + 1, k.passed)
                    pe.transpose(back_ps[:, 0:channels], handed[r][:, 0:P],
                                 k.ident[0:channels, 0:channels]).then_inc(handed_turned, 1)
            over_chunks(pe, body)

        @block.vector
        def _(dve):
            def flat(t):
                return t[:, :, :].rearrange("p c j -> p (c j)")

            def decode(c):
                dve.wait_ge(chunk_in, c * 48 + 48)
                dve.tensor_scalar(run[:, :], keys[:, :], SRC_BITS, None, ALU.logical_shift_right)
                dve.tensor_scalar(run_before[:, :], before[:, :], SRC_BITS, None, ALU.logical_shift_right)
                dve.tensor_copy(given_next[:, :, :], given[:, :, :].rearrange("p j h -> p h j"))
                dve.drain().then_inc(decoded, 1)
                dve.tensor_tensor(same_next[:, :], run[:, :], run_before[:, :], ALU.is_equal)
                dve.drain()

            def hand_on(c, r, channels, initial_op, op):
                dve.drain().then_inc(ends_ready, 1)
                dve.wait_ge(ends_turned, c * 3 + r + 1)
                dve.tensor_copy(factor_row[0:channels, :], turned_ps[0:channels, 1, :])
                dve.tensor_copy(handed[r][:, 0:1], handed[r][:, P:P + 1])
                dve.drain()
                dve.tensor_tensor_scan(handed[r][:, 1:P + 1], factor_row[0:channels, :], turned_ps[0:channels, 0, :],
                                       handed[r][:, 0:1], initial_op, op).then_inc(handed_ready, 1)
                dve.wait_ge(handed_turned, c * 3 + r + 1)

            for r, start in enumerate((0.0, -FAR, 0.0)):
                dve.memset(handed[r][:, :], start)
            dve.drain()
            decode(0)

            def body(c, own):
                wait_alone(dve, rows_in, c * 16 + 16, k.passed)
                dve.tensor_copy(value[:, 0:HE, :], fetched[:, :, 0:HE].rearrange("p j v -> p v j"))
                dve.tensor_copy(src_score[:, :, :], fetched[:, :, HE:ROW].rearrange("p j v -> p v j"))
                dve.tensor_copy(same[:, :, :], same_next[:, :].unsqueeze(1).to_broadcast([P, HEADS, P]))
                dve.tensor_copy(given_row[:, :, :], given_next[:, :, :])
                dve.tensor_copy(first[:, 0:1], same_next[:, 0:1])
                dve.tensor_reduce(first[:, 2:3], same_next[:, :], AX_X, ALU.min)
                dve.drain().then_inc(rows_taken, 1)
                decode(c + 1)
                dve.memset(same[:, :, 0:1], 0.0)
                for i in (0, 2):
                    dve.tensor_scalar(first[:, i + 1:i + 2], first[:, i:i + 1], -1.0, FAR, ALU.add, ALU.mult)
                dve.drain()

                dve.tensor_scalar(penalty[:, :, :], same[:, :, :], -1.0, FAR, ALU.add, ALU.mult)
                dve.tensor_tensor_scan(flat(dst_score), flat(same), flat(given_row), 0.0, ALU.mult, ALU.add)
                dve.drain()
                dve.tensor_copy(ends[:, 0, 0:HEADS], dst_score[:, :, P - 1])
                dve.tensor_copy(ends[:, 1, 0:HEADS], first[:, 2:3].to_broadcast([P, HEADS]))
                hand_on(c, 0, HEADS, ALU.mult, ALU.add)
                dve.scalar_tensor_tensor(given_row[:, :, 0], back_ps[:, 0:HEADS], first[:, 0:1], given_row[:, :, 0],
                                         ALU.mult, ALU.add)
                dve.drain()
                dve.tensor_tensor_scan(flat(dst_score), flat(same), flat(given_row), 0.0, ALU.mult, ALU.add)
                dve.drain()

                dve.tensor_tensor(dst_score[:, :, :], dst_score[:, :, :], src_score[:, :, :], ALU.add)
                dve.drain()
                dve.scalar_tensor_tensor(score[:, :, :], dst_score[:, :, :], LEAK, dst_score[:, :, :], ALU.mult,
                                         ALU.max)
                dve.drain()
                dve.tensor_tensor_scan(flat(peak), flat(penalty), flat(score), -FAR, ALU.add, ALU.max)
                dve.tensor_copy(score_0[:, :], score[:, :, 0])
                dve.drain()
                dve.tensor_copy(ends[:, 0, 0:HEADS], peak[:, :, P - 1])
                dve.tensor_copy(ends[:, 1, 0:HEADS], first[:, 3:4].to_broadcast([P, HEADS]))
                hand_on(c, 1, HEADS, ALU.add, ALU.max)
                dve.tensor_copy(peak_in[:, :], back_ps[:, 0:HEADS])
                dve.drain()
                dve.scalar_tensor_tensor(score[:, :, 0], peak_in[:, :], first[:, 1:2], score[:, :, 0], ALU.add,
                                         ALU.max)
                dve.drain()
                dve.tensor_tensor_scan(flat(peak), flat(penalty), flat(score), -FAR, ALU.add, ALU.max)
                dve.drain()

                dve.tensor_copy(score[:, :, 0], score_0[:, :])
                dve.tensor_tensor(decay[:, :, 1:P], peak[:, :, 0:P - 1], peak[:, :, 1:P], ALU.subtract)
                dve.tensor_tensor(decay[:, :, 0], peak_in[:, :], peak[:, :, 0], ALU.subtract)
                dve.tensor_tensor(decay_all, peak_in[:, :], peak[:, :, P - 1], ALU.subtract)
                dve.drain()
                dve.tensor_tensor(weight, score[:, :, :], peak[:, :, :], ALU.subtract)
                dve.drain()
                dve.tensor_scalar(powers[:, :], powers[:, :], 0.0, None, ALU.min).then_inc(powers_ready, 1)
                wait_alone(dve, raised, c + 1, k.passed)
                dve.tensor_scalar(decay_0[:, HE:SUMS], decay[:, :, 0], first[:, 0:1], None, ALU.mult)
                dve.tensor_scalar(ends[:, 1, HE:SUMS], decay_all, first[:, 2:3], None, ALU.mult)
                dve.tensor_tensor(value_decay[:, HE:SUMS, :], decay, same[:, :, :], ALU.mult)
                dve.tensor_copy(value[:, HE:SUMS, :], weight)
                dve.drain()
                for h in range(HEADS):
                    own = slice(h * EXPERTS, (h + 1) * EXPERTS)
                    one = slice(HE + h, HE + h + 1)
                    dve.tensor_copy(value_decay[:, own, :], value_decay[:, one, :].to_broadcast([P, EXPERTS, P]))
                    dve.tensor_tensor(value[:, own, :], value[:, own, :],
                                      value[:, one, :].to_broadcast([P, EXPERTS, P]), ALU.mult)
                    dve.tensor_copy(decay_0[:, own], decay_0[:, one].to_broadcast([P, EXPERTS]))
                    dve.tensor_copy(ends[:, 1, own], ends[:, 1, one].to_broadcast([P, EXPERTS]))
                dve.drain()
                dve.tensor_tensor_scan(flat(sums), flat(value_decay), flat(value), 0.0, ALU.mult, ALU.add)
                dve.drain()
                dve.tensor_copy(ends[:, 0, :], sums[:, :, P - 1])
                hand_on(c, 2, SUMS, ALU.mult, ALU.add)
                dve.tensor_tensor(decay_0[:, :], decay_0[:, :], back_ps[:, :], ALU.mult)
                dve.drain()
                dve.tensor_tensor(value[:, :, 0], value[:, :, 0], decay_0[:, :], ALU.add)
                dve.drain()
                dve.tensor_tensor_scan(flat(sums), flat(value_decay), flat(value), 0.0, ALU.mult, ALU.add)
                dve.drain()
                wait_alone(dve, stored, c * 16 + 1, k.passed)
                dve.tensor_copy(rows_out[:, :, 0:SUMS], sums[:, :, :].rearrange("p c j -> p j c"))
                dve.tensor_copy(rows_out[:, :, SUMS:NODE], peak[:, :, :].rearrange("p c j -> p j c"))
                dve.drain().then_inc(rows_ready, 1)
            over_chunks(dve, body)


def gates(nc, k):
    with ExitStack() as ctx:
        def sb(name, shape):
            return ctx.enter_context(nc.sbuf_tensor("ga_" + name, shape, F32))

        def sem(name):
            return ctx.enter_context(nc.semaphore("ga_" + name))
        state = sb("state", [P, TILES, NODE])
        last = sb("last", [P, ROW])
        b_gat, ln_gamma, ln_beta = sb("b_gat", [P, HE]), sb("ln_gamma", [P, HE]), sb("ln_beta", [P, HE])
        S4 = [P, TILES, HEADS]
        loop, late, own, peak, total, part = (sb(n, S4) for n in ("loop", "late", "own", "peak", "total", "part"))
        S16 = [P, TILES, HEADS, EXPERTS]
        agg, term = sb("agg", S16), sb("term", S16)
        mean, spread = sb("mean", [P, TILES]), sb("spread", [P, TILES])
        fetched, loaded, powers_ready, raised, var_ready, root_ready, gaps_ready, gaps_raised = (
            sem(n) for n in ("fetched", "loaded", "powers_ready", "raised", "var_ready", "root_ready",
                             "gaps_ready", "gaps_raised"))
        block = ctx.enter_context(nc.Block())

        @block.gpsimd
        def _(pool):
            for t in range(TILES):
                pool.indirect_dma_start(state[:, t, :], None, k.states[:, :],
                                        bass.IndirectOffsetOnAxis(k.last_place[:, t:t + 1], 0)).then_inc(fetched, 16)

        @block.sync
        def _(sp):
            sp.dma_start(last[:, :], k.table[TOK - 1:TOK, :].to_broadcast([P, ROW])).then_inc(loaded, 16)
            for tile, source in ((b_gat, k.b_gat), (ln_gamma, k.ln_gamma), (ln_beta, k.ln_beta)):
                sp.dma_start(tile[:, :], source.rearrange("(a n) -> a n", a=1).to_broadcast([P, HE])
                             ).then_inc(loaded, 16)

        @block.scalar
        def _(act):
            act.wait_ge(powers_ready, 1)
            for tile in (loop, late, own):
                mm = act.activation(tile[:, :, :], tile[:, :, :], ACT.Exp)
            mm.then_inc(raised, 1)
            act.wait_ge(var_ready, 1)
            act.activation(spread[:, :], spread[:, :], ACT.Sqrt).then_inc(root_ready, 1)
            act.wait_ge(gaps_ready, 1)
            act.activation(k.gate[:, :, :], k.gate[:, :, :], ACT.Exp).then_inc(gaps_raised, 1)

        @block.vector
        def _(dve):
            def tt(out, a, b, op):
                dve.tensor_tensor(out, a, b, op)
                dve.drain()

            def ts(out, a, s1, s2, op0, op1=ALU.bypass):
                dve.tensor_scalar(out, a, s1, s2, op0, op1)
                dve.drain()

            def by_tile(t, n):
                return t[:, :].unsqueeze(2).to_broadcast([P, TILES, n])

            def over_experts(t):
                return t.unsqueeze(3).to_broadcast(S16)

            def vector(v):
                return v.rearrange("p (h e) -> p h e", h=HEADS).unsqueeze(1).to_broadcast(S16)

            def masked(t, flag):
                dve.tensor_scalar(part[:, :, :], by_tile(flag, HEADS), -1.0, FAR, ALU.add, ALU.mult)
                tt(t[:, :, :], t[:, :, :], by_tile(flag, HEADS), ALU.mult)
                tt(t[:, :, :], t[:, :, :], part[:, :, :], ALU.add)

            def leaky(t):
                dve.scalar_tensor_tensor(t[:, :, :], t[:, :, :], LEAK, t[:, :, :], ALU.mult, ALU.max)
                dve.drain()
            to_score = k.node[:, :, HE + HEADS:NODE]
            dve.wait_ge(loaded, 64)
            tt(loop[:, :, :], k.node[:, :, HE:HE + HEADS], to_score, ALU.add)
            tt(late[:, :, :], last[:, HE:ROW].unsqueeze(1).to_broadcast(S4), to_score, ALU.add)
            leaky(loop)
            leaky(late)
            masked(late, k.has_last)
            dve.wait_ge(fetched, 16 * TILES)
            dve.tensor_copy(own[:, :, :], state[:, :, ROW:NODE])
            dve.drain()
            masked(own, k.has_own)
            tt(peak[:, :, :], loop[:, :, :], late[:, :, :], ALU.max)
            tt(peak[:, :, :], peak[:, :, :], own[:, :, :], ALU.max)
            for t in (loop, late, own):
                dve.tensor_tensor(t[:, :, :], t[:, :, :], peak[:, :, :], ALU.subtract)
            dve.drain().then_inc(powers_ready, 1)
            dve.wait_ge(raised, 1)
            tt(late[:, :, :], late[:, :, :], by_tile(k.count_last, HEADS), ALU.mult)
            tt(total[:, :, :], own[:, :, :], state[:, :, HE:ROW], ALU.mult)
            tt(total[:, :, :], total[:, :, :], loop[:, :, :], ALU.add)
            tt(total[:, :, :], total[:, :, :], late[:, :, :], ALU.add)
            ts(total[:, :, :], total[:, :, :], 1e-16, None, ALU.add)
            dve.reciprocal(total[:, :, :], total[:, :, :])

            def heads(t):
                return t.rearrange("p t (h e) -> p t h e", h=HEADS)
            tt(agg[:, :, :, :], heads(state[:, :, 0:HE]), over_experts(own[:, :, :]), ALU.mult)
            tt(term[:, :, :, :], heads(k.node[:, :, 0:HE]), over_experts(loop[:, :, :]), ALU.mult)
            tt(agg[:, :, :, :], agg[:, :, :, :], term[:, :, :, :], ALU.add)
            tt(term[:, :, :, :], vector(last[:, 0:HE]), over_experts(late[:, :, :]), ALU.mult)
            tt(agg[:, :, :, :], agg[:, :, :, :], term[:, :, :, :], ALU.add)
            tt(agg[:, :, :, :], agg[:, :, :, :], over_experts(total[:, :, :]), ALU.mult)
            tt(agg[:, :, :, :], agg[:, :, :, :], vector(b_gat[:, :]), ALU.add)

            rows, term_rows = (t[:, :, :, :].rearrange("p t h e -> p t (h e)") for t in (agg, term))
            dve.tensor_reduce(mean[:, :], rows, AX_X, ALU.add)
            dve.drain()
            ts(mean[:, :], mean[:, :], 1.0 / HE, None, ALU.mult)
            tt(rows, rows, by_tile(mean, HE), ALU.subtract)
            tt(term_rows, rows, rows, ALU.mult)
            dve.tensor_reduce(spread[:, :], term_rows, AX_X, ALU.add)
            dve.drain()
            dve.tensor_scalar(spread[:, :], spread[:, :], 1.0 / HE, LN_T_EPS, ALU.mult, ALU.add).then_inc(var_ready, 1)
            dve.wait_ge(root_ready, 1)
            dve.reciprocal(spread[:, :], spread[:, :])
            dve.drain()
            tt(rows, rows, by_tile(spread, HE), ALU.mult)
            tt(agg[:, :, :, :], agg[:, :, :, :], vector(ln_gamma[:, :]), ALU.mult)
            tt(agg[:, :, :, :], agg[:, :, :, :], vector(ln_beta[:, :]), ALU.add)
            score = part
            dve.tensor_reduce(score[:, :, :], agg[:, :, :, :].rearrange("p t h e -> p t e h"), AX_X, ALU.add)
            dve.drain()
            ts(score[:, :, :], score[:, :, :], 1.0 / HEADS, None, ALU.mult)

            rank, ahead = total, loop
            dve.memset(rank[:, :, :], 0.0)
            dve.drain()
            for a in range(EXPERTS):
                for b in range(a + 1, EXPERTS):
                    tt(ahead[:, :, 0], score[:, :, a], score[:, :, b], ALU.is_ge)
                    ts(ahead[:, :, 1], ahead[:, :, 0], -1.0, 1.0, ALU.mult, ALU.add)
                    dve.tensor_tensor(rank[:, :, b], rank[:, :, b], ahead[:, :, 0], ALU.add)
                    tt(rank[:, :, a], rank[:, :, a], ahead[:, :, 1], ALU.add)
            dve.tensor_reduce(mean[:, :], score[:, :, :], AX_X, ALU.max)
            dve.drain()
            dve.tensor_tensor(k.gate[:, :, :], score[:, :, :], by_tile(mean, EXPERTS),
                              ALU.subtract).then_inc(gaps_ready, 1)
            ts(rank[:, :, :], rank[:, :, :], 1.5, None, ALU.is_lt)
            dve.wait_ge(gaps_raised, 1)
            tt(k.gate[:, :, :], k.gate[:, :, :], rank[:, :, :], ALU.mult)
            dve.tensor_reduce(mean[:, :], k.gate[:, :, :], AX_X, ALU.add)
            dve.drain()
            dve.reciprocal(mean[:, :], mean[:, :])
            dve.drain()
            tt(k.gate[:, :, :], k.gate[:, :, :], by_tile(mean, EXPERTS), ALU.mult)


def feed_forward(nc, k, out):
    HID = k.w1.shape[2]
    HID_C = HID // P
    STEPS = EXPERTS * HID_C
    T = GPX // P
    HIDDEN_BUFS, GELU_BUFS, TILE_BUFS = 2, 4, 2
    LEAD = STEPS
    out_tiles = out.rearrange("b (h p) y w -> b p h (y w)", p=P)
    ln_tiles = k.ln_rows.rearrange("(h p) b y w -> b p h (y w)", p=P)

    def over_steps(eng, stages):
        for img in range(IMGS):
            with eng.Fori(0, ROW_GROUPS // UNROLL) as i:
                for step in range(UNROLL * STEPS + max(lag for _, lag, _ in stages)):
                    for body, lag, own in stages:
                        u, j = divmod(step - lag, STEPS)
                        if 0 <= u < UNROLL and j in own:
                            body(img, i * UNROLL + u, i * UNROLL + (img * ROW_GROUPS + u), u, j)

    with ExitStack() as ctx:
        def sb(name, shape, dt=F32):
            return ctx.enter_context(nc.sbuf_tensor("ff_" + name, shape, dt))

        def sem(name):
            return ctx.enter_context(nc.semaphore("ff_" + name))

        def ps(name, shape):
            return ctx.enter_context(nc.psum_tensor("ff_" + name, shape, F32))
        w1 = sb("w1", [P, EXPERTS, PARTS_C, HID])
        w2 = sb("w2", [P, STEPS, C])
        b1 = sb("b1", [P, STEPS])
        b1_rows = sb("b1_rows", [STEPS, P])
        b2 = sb("b2", [EXPERTS, C])
        pick = sb("pick", [EXPERTS, EXPERTS, P])
        x = [sb(f"x{b}", [P, PARTS_C, GPX]) for b in range(TILE_BUFS)]
        res = [sb(f"res{b}", [P, PARTS_C, GPX]) for b in range(TILE_BUFS)]
        hidden = [sb(f"hidden{b}", [P, GPX]) for b in range(GELU_BUFS)]
        gate_column = [sb(f"gate_column{b}", [P, T, EXPERTS]) for b in range(2)]
        gate_row = [sb(f"gate_row{b}", [EXPERTS, GPX]) for b in range(2)]
        gate_all = [sb(f"gate_all{b}", [P, EXPERTS, GPX]) for b in range(2)]
        hidden_ps = [ps(f"hidden_ps{b}", [P, GPX]) for b in range(HIDDEN_BUFS)]
        acc_ps = [[ps(f"acc_ps{b}_{h}", [P, GPX]) for h in range(PARTS_C)] for b in range(2)]
        row_ps = ps("row_ps", [P, GPX])
        all_ps = ps("all_ps", [P, GPX])
        x_in = [sem(f"x_in{b}") for b in range(TILE_BUFS)]
        res_in = [sem(f"res_in{b}") for b in range(TILE_BUFS)]
        stored = [sem(f"stored{b}") for b in range(TILE_BUFS)]
        weights_in, pick_ready = sem("weights_in"), sem("pick_ready")
        b1_turned, b1_ready = sem("b1_turned"), sem("b1_ready")
        multiplied, gelu_done, gated, summed, tile_ready, row_taken, all_taken = (sem(n) for n in (
            "multiplied", "gelu_done", "gated", "summed", "tile_ready", "row_taken", "all_taken"))
        column_ready, row_turned, all_ready = sem("column_ready"), sem("row_turned"), sem("all_ready")
        block = ctx.enter_context(nc.Block())
        WEIGHT_LOADS = 4
        TAKE_ROW = 2
        SPREADS = (4, 7, 10, 13)
        assert len(SPREADS) == EXPERTS
        ALL = range(STEPS)

        @block.sync
        def _(sp):
            sp.dma_start(w1[:, :, :, :], k.w1.rearrange("e (h p) n -> p e h n", p=P)).then_inc(weights_in, 16)
            sp.dma_start(w2[:, :, :], k.w2.rearrange("e (c p) o -> p (e c) o", p=P)).then_inc(weights_in, 16)
            sp.dma_start(b1_rows[:, :], k.b1.rearrange("e (c p) -> (e c) p", p=P)).then_inc(weights_in, 16)
            sp.dma_start(b2[:, :], k.b2).then_inc(weights_in, 16)

            def load(img, g, n, u):
                b = u % TILE_BUFS
                wait_alone(sp, multiplied, n * STEPS + 1, k.passed)
                sp.dma_start(x[b][:, :, :], ln_tiles[img, :, :, bass.ds(g * GPX, GPX)]).then_inc(x_in[b], 16)
                wait_alone(sp, stored[b], (n - b) * (16 // TILE_BUFS) + 1, k.passed)
                sp.dma_start(res[b][:, :, :],
                             k.residual[img, :, :, bass.ds(g * GPX, GPX)]).then_inc(res_in[b], 16)

            def store(img, g, n, u):
                b = u % TILE_BUFS
                wait_alone(sp, tile_ready, n + 3, k.passed)
                sp.dma_start(out_tiles[img, :, :, bass.ds(g * GPX, GPX)], res[b][:, :, :]).then_inc(stored[b], 16)
            for b in range(TILE_BUFS):
                sp.sem_inc(stored[b], 1)
            over_tiles(sp, [(load, 0), (store, 1)])
            for b in range(TILE_BUFS):
                sp.wait_ge(stored[b], 16 * IMGS * ROW_GROUPS // TILE_BUFS + 1)

        @block.tensor
        def _(pe):
            pe.sem_inc(multiplied, STEPS + 1)
            pe.sem_inc(summed, GELU_BUFS)
            pe.wait_ge(weights_in, 16 * WEIGHT_LOADS)
            pe.wait_ge(pick_ready, 2)
            pe.transpose(all_ps[:, 0:STEPS], b1_rows[:, :], k.ident[0:STEPS, 0:STEPS]).then_inc(b1_turned, 1)
            pe.wait_ge(b1_ready, 1)

            def turn_gates(img, g, n, u, j):
                pe.wait_ge(column_ready, n + 1)
                pe.wait_ge(row_taken, n + 1)
                for t in range(T):
                    mm = pe.transpose(row_ps[0:EXPERTS, t * P:(t + 1) * P], gate_column[u % 2][:, t, :], k.ident[:, :])
                mm.then_inc(row_turned, 1)

            def spread_gate(img, g, n, u, j):
                e = SPREADS.index(j)
                pe.wait_ge(row_taken, n + 2)
                pe.wait_ge(all_taken, n * EXPERTS + (e + 1))
                pe.matmul(all_ps[:, :], pick[:, e, :], gate_row[u % 2][:, :], start=True,
                          stop=True).then_inc(all_ready, 1)

            def first_product(img, g, n, u, j):
                b, e = u % TILE_BUFS, j // HID_C
                if j == 0:
                    pe.wait_ge(x_in[b], (n - b) * (16 // TILE_BUFS) + 16)
                pe.wait_ge(gelu_done, n * STEPS + (j + 1))
                part = slice(j % HID_C * P, (j % HID_C + 1) * P)
                for h in range(PARTS_C):
                    mm = pe.matmul(hidden_ps[j % HIDDEN_BUFS][:, :], w1[:, e, h, part], x[b][:, h, :],
                                   start=(h == 0), stop=(h == PARTS_C - 1))
                mm.then_inc(multiplied, 1)

            def second_product(img, g, n, u, j):
                acc = acc_ps[u % 2]
                if j == 0:
                    pe.wait_ge(tile_ready, n + 1)
                    for h in range(PARTS_C):
                        pe.matmul(acc[h][:, :], b2[:, h * P:(h + 1) * P], gate_row[u % 2][:, :], start=True,
                                  stop=False)
                pe.wait_ge(gated, n * STEPS + (j + 2 + STEPS))
                for h in range(PARTS_C):
                    mm = pe.matmul(acc[h][:, :], w2[:, j, h * P:(h + 1) * P], hidden[j % GELU_BUFS][:, :],
                                   start=False, stop=(j == STEPS - 1))
                mm.then_inc(summed, 1)
            over_steps(pe, [(turn_gates, 0, (0,)), (spread_gate, 0, SPREADS), (first_product, LEAD, ALL),
                            (second_product, LEAD + 2, ALL)])

        @block.scalar
        def _(act):
            act.sem_inc(gelu_done, HIDDEN_BUFS)
            act.sem_inc(all_taken, 1)
            act.wait_ge(b1_turned, 1)
            act.activation(b1[:, :], all_ps[:, 0:STEPS], ACT.Copy).then_inc(b1_ready, 1)
            act.wait_ge(b1_ready, 1)

            def take_gate(img, g, n, u, j):
                e = SPREADS.index(j)
                act.wait_ge(gated, n * STEPS + 1)
                act.wait_ge(all_ready, n * EXPERTS + (e + 1))
                act.activation(gate_all[u % 2][:, e, :], all_ps[:, :], ACT.Copy).then_inc(all_taken, 1)

            def gelu(img, g, n, u, j):
                act.wait_ge(multiplied, n * STEPS + (j + 2 + STEPS))
                act.wait_ge(summed, n * STEPS + (j + 1))
                act.activation(hidden[j % GELU_BUFS][:, :], hidden_ps[j % HIDDEN_BUFS][:, :], ACT.Gelu,
                               bias=b1[:, j:j + 1]).then_inc(gelu_done, 1)
            over_steps(act, [(take_gate, 0, SPREADS), (gelu, LEAD, ALL)])

        @block.vector
        def _(dve):
            dve.sem_inc(gated, STEPS + 1)
            dve.sem_inc(tile_ready, 2)
            dve.sem_inc(row_taken, 1)

            def gate_columns(img, g, n, u, j):
                dve.tensor_copy(gate_column[u % 2][:, :, :],
                                k.gate[:, bass.ds(n * T, T), :]).then_inc(column_ready, 1)

            def take_row(img, g, n, u, j):
                dve.wait_ge(row_turned, n + 1)
                dve.tensor_copy(gate_row[u % 2][:, :], row_ps[0:EXPERTS, :]).then_inc(row_taken, 1)

            def times_gate(img, g, n, u, j):
                e = j // HID_C
                if j % HID_C == 0:
                    dve.wait_ge(all_taken, n * EXPERTS + (e + 2))
                dve.wait_ge(gelu_done, n * STEPS + (j + 1 + HIDDEN_BUFS))
                x = hidden[j % GELU_BUFS]
                dve.tensor_tensor(x[:, :], x[:, :], gate_all[u % 2][:, e, :], ALU.mult).then_inc(gated, 1)

            def add_residual(img, g, n, u, j):
                b = u % TILE_BUFS
                dve.wait_ge(res_in[b], (n - b) * (16 // TILE_BUFS) + 16)
                dve.wait_ge(summed, n * STEPS + (STEPS + GELU_BUFS))
                for h in range(PARTS_C):
                    last = dve.tensor_tensor(res[b][:, h, :], res[b][:, h, :], acc_ps[u % 2][h][:, :], ALU.add)
                last.then_inc(tile_ready, 1)
            over_steps(dve, [(gate_columns, 0, (0,)), (take_row, 0, (TAKE_ROW,)), (times_gate, LEAD, ALL),
                             (add_residual, LEAD + 3, (STEPS - 1,))])

        @block.gpsimd
        def _(pool):
            pool.memset(pick[:, :, :], 1.0).then_inc(pick_ready, 1)
            pool.wait_ge(pick_ready, 1)
            pool.affine_select(out=pick[:, :, :], in_=pick[:, :, :], compare_op=ALU.is_equal, fill=0.0, base=0,
                               pattern=[[-1, EXPERTS], [0, P]], channel_multiplier=1).then_inc(pick_ready, 1)


def mix_experts(nc, k, out):
    T = GPX // P
    TILE_BUFS = 2
    TILES_ALL = IMGS * ROW_GROUPS
    out_tiles = out.rearrange("b (h p) y w -> b p h (y w)", p=P)
    with ExitStack() as ctx:
        def sb(name, shape):
            return ctx.enter_context(nc.sbuf_tensor("me_" + name, shape, F32))

        def sem(name):
            return ctx.enter_context(nc.semaphore("me_" + name))

        def ps(name, shape):
            return ctx.enter_context(nc.psum_tensor("me_" + name, shape, F32))
        pick = sb("pick", [EXPERTS, EXPERTS, P])
        given = [sb(f"given{b}", [P, EXPERTS, PARTS_C, GPX]) for b in range(TILE_BUFS)]
        res = [sb(f"res{b}", [P, PARTS_C, GPX]) for b in range(TILE_BUFS)]
        gate_column = [sb(f"gate_column{b}", [P, T, EXPERTS]) for b in range(2)]
        gate_row = [sb(f"gate_row{b}", [EXPERTS, GPX]) for b in range(2)]
        row_ps = ps("row_ps", [EXPERTS, GPX])
        gate_ps = [ps(f"gate_ps{e}", [P, GPX]) for e in range(EXPERTS)]
        given_in = [sem(f"given_in{b}") for b in range(TILE_BUFS)]
        res_in = [sem(f"res_in{b}") for b in range(TILE_BUFS)]
        stored = [sem(f"stored{b}") for b in range(TILE_BUFS)]
        pick_ready, column_ready, row_turned, gate_ready = (
            sem(n) for n in ("pick_ready", "column_ready", "row_turned", "gate_ready"))
        row_taken, gate_used, mixed = sem("row_taken"), sem("gate_used"), sem("mixed")
        block = ctx.enter_context(nc.Block())

        @block.gpsimd
        def _(pool):
            pool.memset(pick[:, :, :], 1.0).then_inc(pick_ready, 1)
            pool.wait_ge(pick_ready, 1)
            pool.affine_select(out=pick[:, :, :], in_=pick[:, :, :], compare_op=ALU.is_equal, fill=0.0, base=0,
                               pattern=[[-1, EXPERTS], [0, P]], channel_multiplier=1).then_inc(pick_ready, 1)

        @block.sync
        def _(sp):
            for b in range(TILE_BUFS):
                sp.sem_inc(stored[b], 1)

            def load(img, g, n, u):
                b = u % TILE_BUFS
                wait_alone(sp, mixed, n + 1, k.passed)
                sp.dma_start(given[b][:, :, :, :].rearrange("p e h t -> p (e h t)"),
                             k.expert_out[bass.ds(n, 1)].rearrange("a p v -> p (a v)")).then_inc(given_in[b], 16)
                wait_alone(sp, stored[b], (n - b) * (16 // TILE_BUFS) + 1, k.passed)
                sp.dma_start(res[b][:, :, :],
                             k.residual[img, :, :, bass.ds(g * GPX, GPX)]).then_inc(res_in[b], 16)
            over_tiles(sp, [(load, 0)])

        @block.tensor
        def _(pe):
            pe.wait_ge(pick_ready, 2)

            def turn_gates(img, g, n, u):
                pe.wait_ge(column_ready, n + 1)
                pe.wait_ge(row_taken, n + 1)
                for t in range(T):
                    mm = pe.transpose(row_ps[:, t * P:(t + 1) * P], gate_column[u % 2][:, t, :], k.ident[:, :])
                mm.then_inc(row_turned, 1)

            def spread_gates(img, g, n, u):
                pe.wait_ge(row_taken, n + 2)
                for e in range(EXPERTS):
                    pe.wait_ge(gate_used, n * EXPERTS + (e + 1))
                    pe.matmul(gate_ps[e][:, :], pick[:, e, :], gate_row[u % 2][:, :], start=True,
                              stop=True).then_inc(gate_ready, 1)
            over_tiles(pe, [(turn_gates, 0), (spread_gates, 1)])

        @block.scalar
        def _(act):
            act.sem_inc(row_taken, 1)

            def take_column(img, g, n, u):
                act.wait_ge(row_taken, n + 1)
                act.activation(gate_column[u % 2][:, :, :], k.gate[:, bass.ds(n * T, T), :],
                               ACT.Copy).then_inc(column_ready, 1)

            def take_row(img, g, n, u):
                act.wait_ge(row_turned, n + 1)
                act.wait_ge(gate_used, n * EXPERTS + 1)
                act.activation(gate_row[u % 2][:, :], row_ps[:, :], ACT.Copy).then_inc(row_taken, 1)

            def store(img, g, n, u):
                b = u % TILE_BUFS
                act.wait_ge(mixed, n + 1 + TILE_BUFS)
                act.dma_start(out_tiles[img, :, :, bass.ds(g * GPX, GPX)], res[b][:, :, :]).then_inc(stored[b], 16)
            over_tiles(act, [(take_column, 0), (take_row, 0), (store, 2)])
            for b in range(TILE_BUFS):
                act.wait_ge(stored[b], 16 * TILES_ALL // TILE_BUFS + 1)

        @block.vector
        def _(dve):
            dve.sem_inc(gate_used, EXPERTS)
            dve.sem_inc(mixed, TILE_BUFS)

            def mix(img, g, n, u):
                b = u % TILE_BUFS
                v = given[b]
                dve.wait_ge(given_in[b], (n - b) * (16 // TILE_BUFS) + 16)
                for e in range(EXPERTS):
                    dve.wait_ge(gate_ready, n * EXPERTS + (e + 1))
                    dve.tensor_tensor(v[:, e, :, :], v[:, e, :, :],
                                      gate_ps[e][:, :].unsqueeze(1).to_broadcast([P, PARTS_C, GPX]),
                                      ALU.mult).then_inc(gate_used, 1)
                dve.drain()
                half = EXPERTS // 2
                dve.tensor_tensor(v[:, 0:half, :, :], v[:, 0:half, :, :], v[:, half:, :, :], ALU.add)
                dve.drain()
                dve.tensor_tensor(v[:, 0, :, :], v[:, 0, :, :], v[:, 1, :, :], ALU.add)
                dve.drain()
                dve.wait_ge(res_in[b], (n - b) * (16 // TILE_BUFS) + 16)
                dve.tensor_tensor(res[b][:, :, :], res[b][:, :, :], v[:, 0, :, :], ALU.add).then_inc(mixed, 1)
            over_tiles(dve, [(mix, 0)])


def constants(nc, k):
    with ExitStack() as ctx:
        zeroed = ctx.enter_context(nc.semaphore("co_zeroed"))
        block = ctx.enter_context(nc.Block())

        @block.gpsimd
        def _(pool):
            pool.memset(k.ident[:, :], 0.0).then_inc(zeroed, 1)
            pool.memset(k.ones_f[:, :], 1.0)
            pool.wait_ge(zeroed, 1)
            pool.affine_select(out=k.ident[:, :], in_=k.ident[:, :], compare_op=ALU.not_equal, fill=1.0, base=0,
                               pattern=[[-1, P]], channel_multiplier=1).then_inc(zeroed, 1)
            pool.memset(k.mean_c[:, :], 1.0 / C)
            pool.memset(k.eps_c[:, :], LN_C_EPS)
            pool.memset(k.eps_t[:, :], LN_T_EPS)
            pool.wait_ge(zeroed, 2)
            pool.tensor_copy(k.ident_b[:, :], k.ident[:, :])


ARGS = ("x", "w_cat_t", "w_scale_t", "gamma", "beta", "w_gat", "att_src", "att_dst", "b_gat", "ln_gamma",
        "ln_beta", "w1", "b1", "w2", "b2", "edge_index")


def build(nc, args, out):
    k = Ctx()
    (k.x, k.w_cat_t, k.w_scale_t, k.gamma, k.beta, k.w_gat, k.att_src, k.att_dst, k.b_gat, k.ln_gamma, k.ln_beta,
     k.w1, k.b1, k.w2, k.b2, k.edge_index) = (args[name] for name in ARGS)
    declare_scratch(nc, k)
    with ExitStack() as ctx:
        def sb(name, shape, dt):
            return ctx.enter_context(nc.sbuf_tensor(name, shape, dt))
        k.passed = ctx.enter_context(nc.semaphore("passed"))
        k.ident = sb("ident", [P, P], F32)
        k.ones_f = sb("ones_f", [P, P], F32)
        k.mean_c = sb("mean_c", [P, P], F32)
        k.eps_c = sb("eps_c", [P, 1], F32)
        k.eps_t = sb("eps_t", [P, 1], F32)
        k.ident_b = sb("ident_b", [P, P], BF16)
        k.edge_counts = sb("edge_counts", [P, 2], I32)
        constants(nc, k)
        layer_norm_tiles(nc, k, tokens=False)
        guide_taps(nc, k)
        k.y_stats = sb("y_stats", [P, PARTS_C, TOK // GPX, 6], F32)
        with ExitStack() as conv_ctx:
            k.offsets = [0] + [sign * d for d in DILATIONS for sign in (-1, 1)]
            k.masks = conv_ctx.enter_context(nc.sbuf_tensor("masks", [W, len(k.offsets), GPX], U16))
            k.pick_left = conv_ctx.enter_context(nc.sbuf_tensor("pick_left", [SPLITS * LEFT, LEFT, W], BF16))
            k.pick_right = conv_ctx.enter_context(nc.sbuf_tensor("pick_right", [SPLITS * RIGHT, RIGHT, W], BF16))
            branch_masks(nc, k)
            dilated_branches(nc, k)
        k.bn_scale, k.bn_shift = sb("bn_scale", [P, PARTS_C], F32), sb("bn_shift", [P, PARTS_C], F32)
        k.w_graph = sb("w_graph", [P, PARTS_C, NODE], F32)
        k.node = sb("node", [P, TILES, NODE], F32)
        token_constants(nc, k)
        layer_norm_tiles(nc, k, tokens=True)
        with ExitStack() as sort_ctx:
            k.keys_a = sort_ctx.enter_context(nc.sbuf_tensor("keys_a", [P, LANE], F32))
            k.keys_b = sort_ctx.enter_context(nc.sbuf_tensor("keys_b", [P, LANE], F32))
            edge_keys(nc, k)
            sort_and_experts(nc, k)
            store_sorted(nc, k)
        k.first_place = sb("first_place", [P, TILES], U32)
        k.last_place = sb("last_place", [P, TILES], U32)
        k.has_own = sb("has_own", [P, TILES], F32)
        k.has_last = sb("has_last", [P, TILES], F32)
        k.count_last = sb("count_last", [P, TILES], F32)
        count_edges(nc, k)
        place_scores(nc, k)
        edge_softmax(nc, k)
        k.gate = sb("gate", [P, TILES, EXPERTS], F32)
        gates(nc, k)
        mix_experts(nc, k, out)


def kernel(**inputs):
    import numpy as np
    import concourse.bacc as bacc
    from concourse.bass_utils import run_bass_kernel_spmd

    conv, ffn = "L0_conv_", "L0_ffn_"
    given = {name: np.asarray(a) for name, a in inputs.items()}
    arrays = {
        "x": given["x"],
        "w_cat_t": given[conv + "W_cat"].transpose(1, 2, 3, 0).reshape(C, TAPS, GUIDES),
        "w_scale_t": given[conv + "W_scale"].reshape(C, (BRANCHES + 1) * C).T,
        "gamma": given[conv + "gamma"], "beta": given[conv + "beta"],
        "w_gat": given[ffn + "W_gat"], "att_src": given[ffn + "att_src"], "att_dst": given[ffn + "att_dst"],
        "b_gat": given[ffn + "b_gat"], "ln_gamma": given[ffn + "ln_gamma"], "ln_beta": given[ffn + "ln_beta"],
        "w1": given[ffn + "W1"], "b1": given[ffn + "b1"], "w2": given[ffn + "W2"], "b2": given[ffn + "b2"],
        "edge_index": given[ffn + "edge_index"],
    }
    arrays = {"in_" + name: np.ascontiguousarray(a) for name, a in arrays.items()}
    nc = bacc.Bacc("TRN2", target_bir_lowering=False, num_devices=1)
    args = {name: nc.dram_tensor("in_" + name, arrays["in_" + name].shape,
                                 mybir.dt.from_np(arrays["in_" + name].dtype), kind="ExternalInput").ap()
            for name in ARGS}
    out = nc.dram_tensor("out", (IMGS, C, H, W), F32, kind="ExternalOutput").ap()
    build(nc, args, out)
    return run_bass_kernel_spmd(nc, [arrays], core_ids=[0]).results[0]["out"]
```

```python
from contextlib import ExitStack

import concourse.bass as bass
from concourse import mybir

P = 128
ALU = mybir.AluOpType
ACT = mybir.ActivationFunctionType
AX_X = mybir.AxisListType.X
F32 = mybir.dt.float32
BF16 = mybir.dt.bfloat16
F16 = mybir.dt.float16
I32 = mybir.dt.int32
U32 = mybir.dt.uint32
U16 = mybir.dt.uint16

IMGS, C, H, W = 2, 256, 96, 96
PIX = H * W
TOK = IMGS * PIX
TILES = TOK // P
E = 1048576
HEADS, EXPERTS = 4, 4
HE = HEADS * EXPERTS

SRC_BITS = 15
SRC_MASK = (1 << SRC_BITS) - 1
KEY_BASE = 256
KEY_LAST = 1 << 15
KEY_DROP = 0xFE00
LANE = E // P
CHUNK = P * P
CHUNKS = E // CHUNK
NODE = HE + 2 * HEADS
ROW = HE + HEADS


ZEROED_EARLY = 24
ZERO_COLS = 1040 * HEADS
assert (E + CHUNK) % (P * (ZERO_COLS // HEADS)) == 0


class Ctx:
    pass


def declare_scratch(nc, k):
    k.xn_rows = nc.dram_tensor("xn_rows", (C, IMGS, H + 2, W), F32, kind="Internal").ap()
    k.xn_pixels = nc.dram_tensor("xn_pixels", (IMGS, H + 2, W, C), F32, kind="Internal").ap()
    k.taps_left = nc.dram_tensor("taps_left", (SPLITS * LEFT, TOK), BF16, kind="Internal").ap()
    k.taps_right = nc.dram_tensor("taps_right", (SPLITS * RIGHT, TOK), BF16, kind="Internal").ap()
    k.conv_out = nc.dram_tensor("conv_out", (C, IMGS, H, W), F32, kind="Internal").ap()
    k.ln_tiles = nc.dram_tensor("ln_tiles", (TOK // GPX, P, PARTS_C, GPX), F32, kind="Internal").ap()
    k.residual = nc.dram_tensor("residual", (TOK // GPX, P, PARTS_C, GPX), F32, kind="Internal").ap()
    k.table = nc.dram_tensor("table", (TOK, ROW), F32, kind="Internal").ap()
    k.dst_scores = nc.dram_tensor("dst_scores", (E + CHUNK, HEADS), F32, kind="Internal").ap()
    k.states = nc.dram_tensor("states", (E, NODE), F32, kind="Internal").ap()
    k.expert_out = nc.dram_tensor("expert_out", (IMGS * ROW_GROUPS, P, EXPERTS * PARTS_C * GPX), F32,
                                  kind="Internal").ap()
    k.edge_rows = nc.dram_tensor("edge_rows", (CHUNKS + 1, P, P * ROW), F32, kind="Internal").ap()
    k.sorted_keys = nc.dram_tensor("sorted_keys", (P + E + CHUNK,), I32, kind="Internal").ap()


GROUP_ROWS = 4
GPX = GROUP_ROWS * W
ROW_GROUPS = H // GROUP_ROWS
PARTS_C = C // P
DILATIONS = (1, 6, 12, 24, 36)
BRANCHES = len(DILATIONS)
TAPS = 9
GUIDES = BRANCHES * TAPS
LN_C_EPS, LN_T_EPS, BN_EPS = 1e-6, 1e-5, 1e-5
SPLITS = 3
LEFT_BRANCHES = 3
LEFT = LEFT_BRANCHES * TAPS
RIGHT = GUIDES - LEFT


HID_C = 4
STEPS = EXPERTS * HID_C
BIASES = EXPERTS * PARTS_C
EXPERT_TILES = TOK // GPX
HIDDEN_BANKS, HIDDEN_BUFS, ACC_BANKS, EXPERT_BUFS = 2, 4, 2, 2
LAST_OF_EXPERT = range(HID_C - 1, STEPS, HID_C)


def expert_buffers(nc, k, ctx):
    def sb(name, shape):
        return ctx.enter_context(nc.sbuf_tensor("ex_" + name, shape, F32))

    def sem(name):
        return ctx.enter_context(nc.semaphore("ex_" + name))

    def ps(name):
        return ctx.enter_context(nc.psum_tensor("ex_" + name, [P, GPX], F32))
    x = k.experts = Ctx()
    x.w1 = sb("w1", [P, EXPERTS, PARTS_C, HID_C * P])
    x.w2 = sb("w2", [P, STEPS, C])
    x.b1, x.b2 = sb("b1", [P, STEPS]), sb("b2", [P, BIASES])
    x.tile = [sb(f"tile{b}", [P, PARTS_C, GPX]) for b in range(EXPERT_BUFS)]
    x.hidden = [sb(f"hidden{b}", [P, GPX]) for b in range(HIDDEN_BUFS)]
    x.given = [sb(f"given{b}", [P, EXPERTS, PARTS_C, GPX]) for b in range(EXPERT_BUFS)]
    x.hidden_ps = [ps(f"hidden_ps{b}") for b in range(HIDDEN_BANKS)]
    x.acc_ps = [[ps(f"acc_ps{b}_{h}") for h in range(PARTS_C)] for b in range(ACC_BANKS)]
    x.tile_in = [sem(f"tile_in{b}") for b in range(EXPERT_BUFS)]
    x.stored = [sem(f"stored{b}") for b in range(EXPERT_BUFS)]
    x.multiplied, x.gelu_done, x.summed, x.copied = (sem(n) for n in ("multiplied", "gelu_done", "summed", "copied"))


def load_tile(k, sp, n, u):
    x, b = k.experts, u % EXPERT_BUFS
    wait_alone(sp, x.multiplied, n * STEPS + 1, k.passed)
    sp.dma_start(x.tile[b][:, :, :], k.ln_tiles[bass.ds(n, 1)].rearrange("a p h t -> p (a h) t")
                 ).then_inc(x.tile_in[b], 16)


def store_tile(k, sp, n, u):
    x, b = k.experts, u % EXPERT_BUFS
    wait_alone(sp, x.copied, n * EXPERTS + (EXPERTS + ACC_BANKS), k.passed)
    sp.dma_start(k.expert_out[bass.ds(n, 1)].rearrange("a p v -> p (a v)"),
                 x.given[b][:, :, :, :].rearrange("p e h t -> p (e h t)")).then_inc(x.stored[b], 16)


def first_product(k, pe, n, u, j):
    x, b, e = k.experts, u % EXPERT_BUFS, j // HID_C
    if j == 0:
        pe.wait_ge(x.tile_in[b], (n - b) * (16 // EXPERT_BUFS) + 16)
    pe.wait_ge(x.gelu_done, n * STEPS + (j + 1))
    part = slice(j % HID_C * P, (j % HID_C + 1) * P)
    for h in range(PARTS_C):
        mm = pe.matmul(x.hidden_ps[j % HIDDEN_BANKS][:, :], x.w1[:, e, h, part], x.tile[b][:, h, :],
                       start=(h == 0), stop=(h == PARTS_C - 1))
    mm.then_inc(x.multiplied, 1)


def second_product(k, pe, n, u, j):
    x = k.experts
    e, c = divmod(j, HID_C)
    if c == 0:
        pe.wait_ge(x.copied, n * EXPERTS + (e + 1))
    pe.wait_ge(x.gelu_done, n * STEPS + (j + 1 + HIDDEN_BANKS))
    for h in range(PARTS_C):
        mm = pe.matmul(x.acc_ps[e % ACC_BANKS][h][:, :], x.w2[:, j, h * P:(h + 1) * P],
                       x.hidden[j % HIDDEN_BUFS][:, :], start=(c == 0), stop=(c == HID_C - 1))
    mm.then_inc(x.summed, 1)


def gelu(k, act, n, u, j):
    x = k.experts
    act.wait_ge(x.multiplied, n * STEPS + (j + 2 + STEPS))
    act.wait_ge(x.summed, n * STEPS + (j + 1))
    act.activation(x.hidden[j % HIDDEN_BUFS][:, :], x.hidden_ps[j % HIDDEN_BANKS][:, :], ACT.Gelu,
                   bias=x.b1[:, j:j + 1]).then_inc(x.gelu_done, 1)


def copy_expert(k, act, n, u, j):
    x, b, e = k.experts, u % EXPERT_BUFS, j // HID_C
    if e == 0:
        act.wait_ge(x.stored[b], (n - b) * (16 // EXPERT_BUFS) + 1)
    act.wait_ge(x.summed, n * STEPS + (j + 1 + HIDDEN_BUFS))
    for h in range(PARTS_C):
        last = act.activation(x.given[b][:, e, h, :], x.acc_ps[e % ACC_BANKS][h][:, :], ACT.Identity,
                              bias=x.b2[:, e * PARTS_C + h:e * PARTS_C + h + 1])
    last.then_inc(x.copied, 1)


PE_STAGES = ((first_product, 0, range(STEPS)), (second_product, 2, range(STEPS)))
ACT_STAGES = ((gelu, 0, range(STEPS)), (copy_expert, 3, LAST_OF_EXPERT))


def expert_steps(k, eng, stages, tile, tiles, beside=None):
    for step in range(tiles * STEPS + max(lag for _, lag, _ in stages)):
        if beside is not None:
            beside(step)
        for stage, lag, own in stages:
            u, j = divmod(step - lag, STEPS)
            if 0 <= u < tiles and j in own:
                stage(k, eng, tile(u), u, j)


def expert_share(nc, k, block, first, count, unroll, beside_loads=None):
    assert count % unroll == 0 and unroll % EXPERT_BUFS == 0 and first % EXPERT_BUFS == 0

    def loop(eng, body):
        with eng.Fori(0, count // unroll) as i:
            body(lambda u: i * unroll + (first + u))

    @block.sync
    def _(sp):
        def body(tile):
            for u in range(unroll + 1):
                if u < unroll:
                    load_tile(k, sp, tile(u), u)
                if u > 0:
                    store_tile(k, sp, tile(u - 1), u - 1)
                    if beside_loads is not None:
                        beside_loads(sp, tile(u - 1))
        loop(sp, body)
        for b in range(EXPERT_BUFS):
            sp.wait_ge(k.experts.stored[b], (first + count) * (16 // EXPERT_BUFS) + 1)

    @block.tensor
    def _(pe):
        loop(pe, lambda tile: expert_steps(k, pe, PE_STAGES, tile, unroll))

    @block.scalar
    def _(act):
        loop(act, lambda tile: expert_steps(k, act, ACT_STAGES, tile, unroll))


def expert_constants(nc, k):
    x = k.experts
    with ExitStack() as ctx:
        b1_rows = ctx.enter_context(nc.sbuf_tensor("ec_b1_rows", [STEPS, P], F32))
        b2_rows = ctx.enter_context(nc.sbuf_tensor("ec_b2_rows", [BIASES, P], F32))
        weights_in, turned = (ctx.enter_context(nc.semaphore("ec_" + n)) for n in ("weights_in", "turned"))
        block = ctx.enter_context(nc.Block())

        @block.sync
        def _(sp):
            sp.dma_start(b1_rows[:, :], k.b1.rearrange("e (c p) -> (e c) p", p=P)).then_inc(weights_in, 16)
            sp.dma_start(b2_rows[:, :], k.b2.rearrange("e (h p) -> (e h) p", p=P)).then_inc(weights_in, 16)
            sp.dma_start(x.w1[:, :, :, :], k.w1.rearrange("e (h p) n -> p e h n", p=P)).then_inc(weights_in, 16)
            sp.dma_start(x.w2[:, :, :], k.w2.rearrange("e (c p) o -> p (e c) o", p=P)).then_inc(weights_in, 16)
            for b in range(EXPERT_BUFS):
                sp.sem_inc(x.stored[b], 1)
            sp.wait_ge(weights_in, 64)

        @block.tensor
        def _(pe):
            pe.sem_inc(x.multiplied, STEPS + 1)
            pe.sem_inc(x.summed, HIDDEN_BUFS)
            pe.wait_ge(weights_in, 64)
            pe.transpose(x.hidden_ps[0][:, 0:STEPS], b1_rows[:, :], k.ident[0:STEPS, 0:STEPS])
            pe.transpose(x.hidden_ps[1][:, 0:BIASES], b2_rows[:, :], k.ident[0:BIASES, 0:BIASES]).then_inc(turned, 1)

        @block.scalar
        def _(act):
            act.sem_inc(x.gelu_done, HIDDEN_BANKS)
            act.sem_inc(x.copied, ACC_BANKS)
            act.wait_ge(turned, 1)
            act.activation(x.b1[:, :], x.hidden_ps[0][:, 0:STEPS], ACT.Copy)
            act.activation(x.b2[:, :], x.hidden_ps[1][:, 0:BIASES], ACT.Copy)


BESIDE_KEYS, BESIDE_SORT, BESIDE_COUNT, BESIDE_PLACES, BESIDE_GATES = SHARES = (8, 20, 12, 4, 4)
assert sum(SHARES) == EXPERT_TILES
FIRST_SORT, FIRST_COUNT, FIRST_PLACES, FIRST_GATES = (sum(SHARES[:n]) for n in range(1, 5))


def edge_keys(nc, k):
    PART = 1024
    PARTS = LANE // PART
    edges = k.edge_index.rearrange("two (p f) -> two p f", p=P)
    with ExitStack() as ctx:
        src = [ctx.enter_context(nc.sbuf_tensor(f"ek_src{i}", [P, PART], I32)) for i in range(2)]
        dst = [ctx.enter_context(nc.sbuf_tensor(f"ek_dst{i}", [P, PART], I32)) for i in range(2)]
        t1 = ctx.enter_context(nc.sbuf_tensor("ek_t1", [P, PART], I32))
        t2 = ctx.enter_context(nc.sbuf_tensor("ek_t2", [P, PART], I32))
        t3 = ctx.enter_context(nc.sbuf_tensor("ek_t3", [P, PART], I32))
        part_count = ctx.enter_context(nc.sbuf_tensor("ek_part_count", [P, 2, PARTS], F32))
        boundary = ctx.enter_context(nc.sbuf_tensor("ek_boundary", [P, LANE // P], F32))
        counted = ctx.enter_context(nc.sbuf_tensor("ek_counted", [P, 3], F32))
        totals = ctx.enter_context(nc.psum_tensor("ek_totals", [P, 3], F32))
        src_in = [ctx.enter_context(nc.semaphore(f"ek_src_in{i}")) for i in range(2)]
        dst_in = [ctx.enter_context(nc.semaphore(f"ek_dst_in{i}")) for i in range(2)]
        part_done = ctx.enter_context(nc.semaphore("ek_part_done"))
        lane_counted = ctx.enter_context(nc.semaphore("ek_lane_counted"))
        totals_ready = ctx.enter_context(nc.semaphore("ek_totals_ready"))
        block = ctx.enter_context(nc.Block())

        @block.gpsimd
        def _(pool):
            for c in range(PARTS):
                if c >= 2:
                    pool.wait_ge(part_done, c - 1)
                pool.dma_start(src[c % 2][:, :], edges[0, :, c * PART:(c + 1) * PART]).then_inc(src_in[c % 2], 16)
                pool.dma_start(dst[c % 2][:, :], edges[1, :, c * PART:(c + 1) * PART]).then_inc(dst_in[c % 2], 16)

        @block.vector
        def _(dve):
            for c in range(PARTS):
                s, d = src[c % 2], dst[c % 2]
                dve.wait_ge(src_in[c % 2], 16 * (c // 2 + 1))
                dve.wait_ge(dst_in[c % 2], 16 * (c // 2 + 1))
                dve.tensor_scalar(t1[:, :], s[:, :], float(TOK - 1), float(KEY_LAST), ALU.is_ge, ALU.mult)
                dve.tensor_scalar(t2[:, :], d[:, :], float(TOK), float(KEY_BASE), ALU.min, ALU.add)
                dve.tensor_scalar(t3[:, :], d[:, :], float(TOK), float(KEY_DROP), ALU.is_ge, ALU.mult)
                dve.tensor_scalar(s[:, :], s[:, :], float(TOK - 1), 0.0, ALU.min, ALU.max)
                dve.drain()
                dve.tensor_tensor(t2[:, :], t2[:, :], t1[:, :], ALU.add)
                dve.drain()
                dve.tensor_tensor(t2[:, :], t2[:, :], t3[:, :], ALU.max)
                dve.drain()
                dve.tensor_scalar(t1[:, :], t2[:, :], float(KEY_LAST), 0.0, ALU.is_ge, ALU.add,
                                  accum_out=part_count[:, 0, c:c + 1])
                dve.tensor_scalar(t3[:, :], t2[:, :], float(KEY_DROP), 0.0, ALU.is_ge, ALU.add,
                                  accum_out=part_count[:, 1, c:c + 1])
                dve.scalar_tensor_tensor(k.keys_a[:, c * PART:(c + 1) * PART].bitcast(I32), t2[:, :], SRC_BITS,
                                         s[:, :], ALU.logical_shift_left, ALU.bitwise_or).then_inc(part_done, 1)
                dve.drain()
            dve.tensor_reduce(counted[:, 0:2], part_count[:, :, :], AX_X, ALU.add)
            dve.drain()
            bufs = [k.keys_a[:, :], k.keys_b[:, :]]
            end, _ = sort_levels(dve, bufs, range(1, PRUNE_LEVEL + 1), FREE)
            assert end == 0
            dve.tensor_copy(k.keys_b[:, :], k.keys_a[:, :])
            dve.drain()
            half = P // 2
            blocks = k.keys_b[:, :].rearrange("p (a two c) -> p a two c", two=2, c=P)
            halves = k.keys_a[:, 0:LANE // 2].rearrange("p (a two c) -> p a two c", two=2, c=half)
            dve.tensor_copy(halves[:, :, 0, :], blocks[:, :, 0, 0:half])
            dve.tensor_copy(halves[:, :, 1, :], blocks[:, :, 1, half:P])
            nearest = boundary[:, :].rearrange("p (two a) -> p two a", two=2)
            dve.tensor_copy(nearest[:, 0, :], blocks[:, :, 0, half])
            dve.tensor_scalar(nearest[:, 1, :], blocks[:, :, 1, half - 1], -1.0, None, ALU.mult)
            dve.drain()
            dve.tensor_scalar(boundary[:, :].bitcast(I32), boundary[:, :].bitcast(I32), SRC_BITS, None,
                              ALU.logical_shift_right)
            dve.drain()
            dve.tensor_scalar(boundary[:, :], boundary[:, :].bitcast(I32), float(KEY_DROP), 0.0, ALU.is_lt, ALU.add,
                              accum_out=counted[:, 2:3])
            dve.drain()
            dve.sem_inc(lane_counted, 1)
            dve.wait_ge(totals_ready, 1)
            dve.tensor_scalar(k.edge_counts[:, 0:2], totals[:, 0:2], -1.0, float(E), ALU.mult, ALU.add)
            dve.tensor_copy(k.edge_counts[:, 2:3], totals[:, 2:3])
            dve.drain()
            dve.tensor_scalar(k.edge_counts[:, 0:2], k.edge_counts[:, 0:2], 1.0, None, ALU.max)

        expert_share(nc, k, block, 0, BESIDE_KEYS, 8)

        @block.tensor
        def _(pe):
            pe.wait_ge(lane_counted, 1)
            pe.matmul(totals[:, :], k.ones_f[:, :], counted[:, :], start=True, stop=True).then_inc(totals_ready, 1)


def sort_views(buf, j, q):
    if q is None:
        v = buf.rearrange("p (a two c) -> p a two c", two=2, c=1 << j)
        return {0: (v[:, :, 0, :], v[:, :, 1, :])}
    hi, lo = max(j, q), min(j, q)
    v = buf.rearrange("p (a h b l c) -> p a h b l c", h=2, l=2, b=1 << (hi - lo - 1), c=1 << lo)
    out = {}
    for d in range(2):
        pair = []
        for side in range(2):
            h, l = (side, d) if j > q else (d, side)
            x = v[:, :, h, :, l, :]
            pair.append(x[:, :, 0, :] if hi - lo == 1 else x[:, 0, :, :])
        out[d] = tuple(pair)
    return out


FREE = 13
PRUNED_FREE = FREE - 1
PRUNE_LEVEL = 7
QUARTERS = 4


def sort_levels(dve, bufs, levels, free, to_swap=None, swapped=None, sign=None):
    quarter, top = free + 5, free + 7
    cur, swap_sources = 0, []

    def index_bit(bit, layout):
        return {"plain": bit, "turned": bit if bit < free else bit - free, "swapped": bit - quarter + free - 2}[layout]

    def run(level, bits, layout, split=True):
        nonlocal cur
        for bit in bits:
            first = bit == level - 1
            q = index_bit(level, layout) if first and split else None
            s, d = bufs[cur], bufs[1 - cur]
            sv, dv = (sort_views(t, index_bit(bit, layout), q) for t in (s, d))
            for direction, (low, high) in sv.items():
                for out, op, other in zip(dv[direction], (ALU.min, ALU.max), (ALU.max, ALU.min)):
                    if not first:
                        dve.tensor_tensor(out, low, high, op)
                    elif level == 1:
                        dve.tensor_tensor(out, low, high, op if direction == 0 else other)
                    elif direction == 0:
                        dve.scalar_tensor_tensor(out, high, -1.0, low, ALU.mult, op)
                    else:
                        dve.scalar_tensor_tensor(out, low, -1.0, high, ALU.mult, op)
            dve.drain()
            if level == 1:
                for side in sort_views(d, 0, 1)[1]:
                    dve.tensor_scalar(side, side, -1.0, None, ALU.mult)
                dve.drain()
            cur = 1 - cur

    def turn():
        nonlocal cur
        dve.transpose(bufs[1 - cur], bufs[cur])
        dve.drain()
        cur = 1 - cur

    def swap():
        nonlocal cur
        swap_sources.append(cur)
        dve.sem_inc(to_swap, 1)
        dve.wait_ge(swapped, 16 * QUARTERS * QUARTERS * len(swap_sources))
        cur = 1 - cur

    def down(first, last):
        return range(first, last - 1, -1)
    for level in levels:
        if level < free:
            run(level, down(level - 1, 0), "plain")
            continue
        if level == quarter:
            dve.tensor_scalar(bufs[cur], bufs[cur], sign, None, ALU.mult)
            dve.drain()
        if level > quarter:
            swap()
            run(level, down(level - 1, quarter), "swapped", split=level < top)
            swap()
        turn()
        run(level, down(min(level, quarter) - 1, 5), "turned", split=level != quarter)
        turn()
        run(level, down(4, 0), "plain")
    return cur, swap_sources


def swap_quarters(pool, bufs, sources, to_swap, swapped):
    span, rows = bufs[0].shape[1] // QUARTERS, P // QUARTERS
    for n, source in enumerate(sources):
        pool.wait_ge(to_swap, n + 1)
        s, d = bufs[source], bufs[1 - source]
        for i in range(QUARTERS):
            for j in range(QUARTERS):
                pool.dma_start(d[i * rows:(i + 1) * rows, j * span:(j + 1) * span],
                               s[j * rows:(j + 1) * rows, i * span:(i + 1) * span]).then_inc(swapped, 16)


def pruned_buffers(k):
    return [k.keys_a[:, 0:LANE // 2], k.keys_a[:, LANE // 2:LANE]]


def sort_pruned(nc, k):
    with ExitStack() as ctx:
        to_swap = ctx.enter_context(nc.semaphore("sp_to_swap"))
        swapped = ctx.enter_context(nc.semaphore("sp_swapped"))
        zero_ready = ctx.enter_context(nc.semaphore("sp_zero_ready"))
        zero_out = ctx.enter_context(nc.semaphore("sp_zero_out"))
        zeros = ctx.enter_context(nc.sbuf_tensor("sp_zeros", [P, P * NODE], F32))
        block = ctx.enter_context(nc.Block())
        bufs, sources = pruned_buffers(k), []
        states = k.states.rearrange("(c p r) v -> c p (r v)", p=P, r=P)
        EACH = (CHUNKS - ZEROED_EARLY) // BESIDE_SORT
        assert EACH * BESIDE_SORT == CHUNKS - ZEROED_EARLY

        @block.vector
        def _(dve):
            dve.memset(zeros[:, :], 0.0).then_inc(zero_ready, 1)
            end, found = sort_levels(dve, bufs, range(PRUNE_LEVEL, PRUNED_FREE + 8), PRUNED_FREE, to_swap, swapped,
                                     k.sign[:, 0:1])
            k.pruned_sorted = bufs[end]
            sources.extend(found)

        @block.gpsimd
        def _(pool):
            swap_quarters(pool, bufs, sources, to_swap, swapped)

        def zero_states(sp, n):
            if n is None:
                return
            for i in range(EACH):
                chunk = (n - FIRST_SORT) * EACH + (ZEROED_EARLY + i)
                sp.wait_ge(zero_ready, 1)
                sp.dma_start(states[bass.ds(chunk, 1)].rearrange("a p v -> p (a v)"), zeros[:, :]
                             ).then_inc(zero_out, 16)
        expert_share(nc, k, block, FIRST_SORT, BESIDE_SORT, 4, zero_states)

        @block.gpsimd
        def _(pool):
            pool.wait_ge(zero_out, 16 * EACH * BESIDE_SORT)


def sort_all(nc, k):
    with ExitStack() as ctx:
        to_swap = ctx.enter_context(nc.semaphore("sa_to_swap"))
        swapped = ctx.enter_context(nc.semaphore("sa_swapped"))
        block = ctx.enter_context(nc.Block())
        bufs, sources = [k.keys_b[:, :], k.keys_a[:, :]], []

        @block.vector
        def _(dve):
            above = dve.value_load(k.edge_counts[0:1, 2:3], min_val=0, max_val=E)
            with dve.If(0 < above):
                end, found = sort_levels(dve, bufs, range(PRUNE_LEVEL + 1, FREE + 8), FREE, to_swap, swapped,
                                         k.sign[:, 0:1])
            k.sorted_buf = bufs[end]
            sources.extend(found)

        @block.gpsimd
        def _(pool):
            above = pool.value_load(k.edge_counts[0:1, 2:3], min_val=0, max_val=E)
            with pool.If(0 < above):
                swap_quarters(pool, bufs, sources, to_swap, swapped)


def store_sorted(nc, k):
    with ExitStack() as ctx:
        front = ctx.enter_context(nc.sbuf_tensor("ss_front", [1, P], I32))
        tail = ctx.enter_context(nc.sbuf_tensor("ss_tail", [P, P], I32))
        zero = ctx.enter_context(nc.semaphore("ss_zero"))
        keys_out = ctx.enter_context(nc.semaphore("ss_keys_out"))
        block = ctx.enter_context(nc.Block())

        @block.vector
        def _(dve):
            dve.memset(tail[:, :], 0)
            dve.memset(front[:, :], 0).then_inc(zero, 1)

        def store(eng, keys, count):
            eng.wait_ge(zero, 1)
            eng.dma_start(k.sorted_keys[P:P + count].rearrange("(p f) -> p f", p=P),
                          keys.bitcast(I32)).then_inc(keys_out, 16)
            eng.dma_start(k.sorted_keys[P + count:P + count + CHUNK].rearrange("(p f) -> p f", p=P),
                          tail[:, :]).then_inc(keys_out, 16)
            eng.dma_start(k.sorted_keys[0:P].rearrange("(a f) -> a f", a=1), front[:, :]).then_inc(keys_out, 16)
            eng.wait_ge(keys_out, 3 * 16)

        @block.sync
        def _(sp):
            above = sp.value_load(k.edge_counts[0:1, 2:3], min_val=0, max_val=E)
            with sp.If(above < 1):
                store(sp, k.pruned_sorted, E // 2)

        @block.scalar
        def _(act):
            above = act.value_load(k.edge_counts[0:1, 2:3], min_val=0, max_val=E)
            with act.If(0 < above):
                store(act, k.sorted_buf, E)


def count_edges(nc, k):
    KINDS = 2 * TILES
    RING, GROUP = 32, 4
    GROUPS = P // GROUP
    TURN_CHUNKS = 3
    BESIDE_CHUNKS = BESIDE_COUNT // EXPERT_BUFS * TURN_CHUNKS
    assert TURN_CHUNKS * GROUPS % (EXPERT_BUFS * STEPS) == 0
    with ExitStack() as ctx:
        def sb(name, shape, dt):
            return ctx.enter_context(nc.sbuf_tensor(name, shape, dt))

        def sem(name):
            return ctx.enter_context(nc.semaphore(name))
        keys = sb("ce_keys", [P, P], I32)
        token = sb("ce_token", [P, P], I32)
        high = sb("ce_high", [P, P], F32)
        low = sb("ce_low", [P, P], F32)
        high_i = sb("ce_high_i", [P, P], I32)
        low_i = sb("ce_low_i", [P, P], I32)
        hot_high = sb("ce_hot_high", [P, RING, KINDS], BF16)
        hot_low = sb("ce_hot_low", [P, RING, P], BF16)
        iota_high = sb("ce_iota_high", [P, KINDS], F16)
        iota_low = sb("ce_iota_low", [P, P], F16)
        before = sb("ce_before", [P, P], F32)
        counts = sb("ce_counts", [P, KINDS], F32)
        running = sb("ce_running", [P, TILES], F32)
        column = sb("ce_column", [P, TILES], F32)
        first = sb("ce_first", [P, TILES], F32)
        none = sb("ce_none", [P, TILES], F32)
        sums_ps = ctx.enter_context(nc.psum_tensor("ce_sums_ps", [P, KINDS + TILES], F32))
        counts_ps, within_ps = sums_ps[:, 0:KINDS], sums_ps[:, KINDS:]
        column_ps = ctx.enter_context(nc.psum_tensor("ce_column_ps", [P, TILES], F32))
        source_i = sb("ce_source_i", [P, P], I32)
        sources = sb("ce_sources", [P, LANE], U32)
        source = sb("ce_source", [P, P], U32)
        fetched = sb("ce_fetched", [P, P, ROW], F32)
        source_ready, source_taken, rows_fetched, rows_stored = (sem("ce_" + x) for x in (
            "source_ready", "source_taken", "rows_fetched", "rows_stored"))
        iota_ready, before_ready, keys_in, keys_read = (sem("ce_" + x) for x in (
            "iota_ready", "before_ready", "keys_in", "keys_read"))
        hot_ready, hot_free, chunk_added = (sem("ce_" + x) for x in (
            "hot_ready", "hot_free", "chunk_added"))
        sums_ready = sem("ce_sums_ready")
        counts_whole = sem("ce_counts_whole")
        block = ctx.enter_context(nc.Block())

        @block.gpsimd
        def _(pool):
            pool.memset(before[:, :], 1.0).then_inc(before_ready, 1)
            pool.iota(iota_high[:, :].rearrange("p (a b) -> p a b", a=2), [[KEY_LAST // P, 2], [1, TILES]], base=0,
                      channel_multiplier=0, allow_small_or_imprecise_dtypes=True)
            pool.iota(iota_low[:, :], [[1, P]], base=0, channel_multiplier=0,
                      allow_small_or_imprecise_dtypes=True).then_inc(iota_ready, 1)
            pool.wait_ge(before_ready, 1)
            pool.affine_select(out=before[:, :], in_=before[:, :], compare_op=ALU.is_gt, fill=0.0, base=0,
                               pattern=[[1, P]], channel_multiplier=-1).then_inc(before_ready, 1)
            own = pool.value_load(k.edge_counts[0:1, 0:1], min_val=1, max_val=E)
            with pool.Fori(0, CHUNKS) as c:
                with pool.If(c * CHUNK < own):
                    wait_alone(pool, source_ready, c + 1, k.passed)
                    pool.tensor_copy(source[:, :], sources[:, bass.ds(c * P, P)]).then_inc(source_taken, 1)
                    wait_alone(pool, source_taken, c + 1, k.passed)
                    for j in range(P):
                        pool.indirect_dma_start(fetched[:, j, :], None, k.table[:, :],
                                                bass.IndirectOffsetOnAxis(source[:, j:j + 1], 0)
                                                ).then_inc(rows_fetched, 16)
                    wait_alone(pool, rows_fetched, c * (16 * P) + 16 * P, k.passed)
                    pool.dma_start(k.edge_rows[bass.ds(c, 1)].rearrange("a p v -> p (a v)"),
                                   fetched[:, :, :].rearrange("p j v -> p (j v)")).then_inc(rows_stored, 16)
                    wait_alone(pool, rows_stored, c * 16 + 16, k.passed)

        @block.sync
        def _(sp):
            kept = sp.value_load(k.edge_counts[0:1, 1:2], min_val=1, max_val=E)

            def load_keys(c):
                with sp.If(c * CHUNK < kept):
                    wait_alone(sp, keys_read, c + 1, k.passed)
                    sp.dma_start(keys[:, :], k.sorted_keys[bass.ds(c * CHUNK + P, CHUNK)].rearrange(
                        "(p f) -> p f", p=P)).then_inc(keys_in, 16)
            load_keys(0)
            with sp.Fori(0, BESIDE_COUNT // EXPERT_BUFS) as i:
                for u in range(EXPERT_BUFS):
                    load_tile(k, sp, i * EXPERT_BUFS + (FIRST_COUNT + u), u)
                load_keys(i * TURN_CHUNKS + 1)
                store_tile(k, sp, i * EXPERT_BUFS + FIRST_COUNT, 0)
                load_keys(i * TURN_CHUNKS + 2)
                load_keys(i * TURN_CHUNKS + 3)
                store_tile(k, sp, i * EXPERT_BUFS + (FIRST_COUNT + 1), 1)
            with sp.Fori(1, CHUNKS - BESIDE_CHUNKS) as i:
                load_keys(i + BESIDE_CHUNKS)
            for b in range(EXPERT_BUFS):
                sp.wait_ge(k.experts.stored[b], (FIRST_COUNT + BESIDE_COUNT) * (16 // EXPERT_BUFS) + 1)

        @block.scalar
        def _(act):
            with act.Fori(0, BESIDE_COUNT // EXPERT_BUFS) as i:
                expert_steps(k, act, ACT_STAGES, lambda u: i * EXPERT_BUFS + (FIRST_COUNT + u), EXPERT_BUFS)

        @block.vector
        def _(dve):
            dve.memset(counts[:, :], 0.0)
            dve.sem_inc(keys_read, 1)
            dve.sem_inc(chunk_added, 1)
            dve.wait_ge(iota_ready, 1)
            own_edges = dve.value_load(k.edge_counts[0:1, 0:1], min_val=1, max_val=E)
            kept = dve.value_load(k.edge_counts[0:1, 1:2], min_val=1, max_val=E)
            with dve.Fori(0, CHUNKS) as c:
                with dve.If(c * CHUNK < kept):
                    wait_alone(dve, keys_in, c * 16 + 16, k.passed)
                    with dve.If(c * CHUNK < own_edges):
                        dve.tensor_scalar(source_i[:, :], keys[:, :], SRC_MASK, None, ALU.bitwise_and)
                        dve.drain()
                        dve.tensor_scalar(sources[:, bass.ds(c * P, P)], source_i[:, :], float(TOK - 1), None,
                                          ALU.min).then_inc(source_ready, 1)
                    dve.tensor_scalar(token[:, :], keys[:, :], SRC_BITS, None,
                                      ALU.logical_shift_right).then_inc(keys_read, 1)
                    dve.drain()
                    dve.tensor_scalar(token[:, :], token[:, :], float(KEY_BASE), None, ALU.subtract)
                    dve.drain()
                    dve.tensor_scalar(high_i[:, :], token[:, :], 7, None, ALU.logical_shift_right)
                    dve.tensor_scalar(low_i[:, :], token[:, :], P - 1, None, ALU.bitwise_and)
                    dve.drain()
                    dve.tensor_copy(high[:, :], high_i[:, :])
                    dve.tensor_copy(low[:, :], low_i[:, :])
                    dve.drain()
                    for g in range(GROUPS):
                        dve.wait_ge(hot_free, c * GROUPS + g + 1)
                        for i in range(GROUP):
                            j = GROUP * g + i
                            dve.tensor_scalar(hot_high[:, j % RING, :], iota_high[:, :], high[:, j:j + 1], None,
                                              ALU.is_equal)
                            last = dve.tensor_scalar(hot_low[:, j % RING, :], iota_low[:, :], low[:, j:j + 1],
                                                     None, ALU.is_equal)
                        last.then_inc(hot_ready, 1)
                    dve.wait_ge(hot_free, c * GROUPS + GROUPS + RING // GROUP)
                    dve.tensor_tensor(counts[:, :], counts[:, :], counts_ps, ALU.add).then_inc(chunk_added, 1)
                    dve.drain()
            dve.sem_inc(counts_whole, 1)
            own = counts[:, 0:TILES]
            dve.wait_ge(sums_ready, 1)
            dve.tensor_copy(column[:, :], column_ps[:, :])
            dve.drain()
            dve.tensor_tensor_scan(running[:, :], column[:, :], column[:, :], 0.0, ALU.add, ALU.bypass)
            dve.tensor_scalar(none[:, :], own, 0.5, float(2 * E), ALU.is_lt, ALU.mult)
            dve.drain()
            dve.tensor_tensor(first[:, :], running[:, :], column[:, :], ALU.subtract)
            dve.tensor_scalar(k.has_own[:, :], own, 0.5, None, ALU.is_gt)
            dve.tensor_scalar(k.has_last[:, :], counts[:, TILES:KINDS], 0.5, None, ALU.is_gt)
            dve.tensor_copy(k.count_last[:, :], counts[:, TILES:KINDS])
            dve.drain()
            dve.tensor_tensor(first[:, :], first[:, :], within_ps, ALU.add)
            dve.drain()
            dve.tensor_tensor(k.first_place[:, :], first[:, :], none[:, :], ALU.add)
            dve.tensor_tensor(running[:, :], first[:, :], own, ALU.add)
            dve.drain()
            dve.scalar_tensor_tensor(k.last_place[:, :], running[:, :], 1.0, k.has_own[:, :], ALU.subtract, ALU.mult)

        @block.tensor
        def _(pe):
            pe.sem_inc(hot_free, RING // GROUP)
            kept = pe.value_load(k.edge_counts[0:1, 1:2], min_val=1, max_val=E)

            def add_group(c, g):
                if g == 0:
                    pe.wait_ge(chunk_added, c + 1)
                pe.wait_ge(hot_ready, c * GROUPS + g + 1)
                for i in range(GROUP):
                    j = GROUP * g + i
                    mm = pe.matmul(counts_ps, hot_low[:, j % RING, :], hot_high[:, j % RING, :],
                                   start=(j == 0), stop=(j == P - 1))
                mm.then_inc(hot_free, 1)

            with pe.Fori(0, BESIDE_COUNT // EXPERT_BUFS) as i:
                def beside(step):
                    each = TURN_CHUNKS * GROUPS // (EXPERT_BUFS * STEPS)
                    c, g = divmod(step * each, GROUPS)
                    if c < TURN_CHUNKS:
                        for first, last in ((g, min(g + each, GROUPS)), (0, g + each - GROUPS)):
                            if first < last:
                                chunk = i * TURN_CHUNKS + c
                                with pe.If(chunk * CHUNK < kept):
                                    for group in range(first, last):
                                        add_group(chunk, group)
                            c += 1
                expert_steps(k, pe, PE_STAGES, lambda u: i * EXPERT_BUFS + (FIRST_COUNT + u), EXPERT_BUFS, beside)
            with pe.Fori(BESIDE_CHUNKS, CHUNKS) as c:
                with pe.If(c * CHUNK < kept):
                    for g in range(GROUPS):
                        add_group(c, g)
            pe.wait_ge(counts_whole, 1)
            pe.wait_ge(before_ready, 2)
            pe.matmul(within_ps, before[:, :], counts[:, 0:TILES], start=True, stop=True)
            pe.matmul(column_ps[:, :], k.ones_f[:, :], counts[:, 0:TILES], start=True,
                      stop=True).then_inc(sums_ready, 1)


def wait_alone(eng, sem, value, passed):
    eng.wait_ge(sem, value)
    eng.sem_inc(passed, 1)


UNROLL = 8


def over_tiles(eng, stages, unroll=UNROLL):
    for img in range(IMGS):
        with eng.Fori(0, ROW_GROUPS // unroll) as i:
            for step in range(unroll + max(lag for _, lag in stages)):
                for body, lag in stages:
                    u = step - lag
                    if 0 <= u < unroll:
                        body(img, i * unroll + u, i * unroll + (img * ROW_GROUPS + u), u)


def through_tiles(eng, stages):
    tiles = IMGS * ROW_GROUPS
    for step in range(UNROLL):
        for body, lag in stages:
            if step >= lag:
                body(None, None, step - lag, step - lag)
    with eng.Fori(1, tiles // UNROLL) as i:
        for step in range(UNROLL):
            for body, lag in stages:
                body(None, None, i * UNROLL + (step - lag), (step - lag) % UNROLL)
    for step in range(max(lag for _, lag in stages)):
        for body, lag in stages:
            if step < lag:
                body(None, None, tiles + step - lag, (step - lag) % UNROLL)


def layer_norm_tiles(nc, k, tokens):
    x_tiles = k.x.rearrange("b (h p) y w -> b p h (y w)", p=P)
    y_tiles = k.conv_out.rearrange("(h p) b y w -> b p h (y w)", p=P)
    BUFS, CREDIT = 4, 2
    tag = "lt_" if tokens else "lc_"
    TILE_TOKENS = GPX // P
    with ExitStack() as ctx:
        def sb(name, shape, dt):
            return ctx.enter_context(nc.sbuf_tensor(tag + name, shape, dt))

        def sem(name):
            return ctx.enter_context(nc.semaphore(tag + name))

        def ps(name, shape):
            return ctx.enter_context(nc.psum_tensor(tag + name, shape, F32))
        x = [sb(f"x{b}", [P, PARTS_C, GPX], F32) for b in range(BUFS)]
        y = [sb(f"y{b}", [P, PARTS_C, GPX], F32) for b in range(BUFS)] if tokens else x
        square = [sb(f"square{c}", [P, PARTS_C, GPX], F32) for c in range(2)]
        spread = [sb(f"spread{c}", [P, GPX], F32) for c in range(2)]
        pixels = [sb(f"pixels{c}", [W, GROUP_ROWS, C], F32) for c in range(2)]
        zeros = sb("zeros", [P, C], F32)
        mean_ps = [ps(f"mean{c}", [P, GPX]) for c in range(2)]
        var_ps = [ps(f"var{c}", [P, GPX]) for c in range(2)]
        post_ps = [ps(f"post{c}", [P, TILE_TOKENS, NODE] if tokens else [W, GROUP_ROWS, C]) for c in range(2)]
        x_in = [sem(f"x_in{b}") for b in range(BUFS)]
        rows_out = [sem(f"rows_out{b}") for b in range(BUFS)]
        sums_out = [sem(f"sums_out{b}") for b in range(BUFS)] if tokens else None
        pixels_out = None if tokens else [sem(f"pixels_out{c}") for c in range(2)]
        summed, mean_ready, squared = sem("summed") if tokens else None, sem("mean_ready"), sem("squared")
        centred, var_ready, spread_ready, normed, copied, posted = (
            sem(n) for n in ("centred", "var_ready", "spread_ready", "normed", "copied", "posted"))
        zero_ready, zero_out, table_out = (None, None, sem("table_out")) if tokens else (
            sem("zero_ready"), sem("zero_out"), None)
        block = ctx.enter_context(nc.Block())
        eps = k.eps_t if tokens else k.eps_c
        TILES_ALL = IMGS * ROW_GROUPS
        LOADED = 32 if tokens else 16
        ROW_STORES = 1 if tokens else PARTS_C

        def run(eng, stages):
            if tokens:
                through_tiles(eng, stages)
            else:
                over_tiles(eng, stages, 3 * BUFS)

        @block.sync
        def _(sp):
            def load(img, g, n, u):
                b = u % BUFS
                wait_alone(sp, posted, n + 1, k.passed)
                wait_alone(sp, rows_out[b], (n - b) * (16 * ROW_STORES // BUFS) + 1, k.passed)
                if tokens:
                    sp.wait_ge(sums_out[b], (n - b) * (16 // BUFS) + 1)
                    sp.dma_start(y[b][:, :, :], y_tiles[img, :, :, bass.ds(g * GPX, GPX)]).then_inc(x_in[b], 16)
                sp.dma_start(x[b][:, :, :], x_tiles[img, :, :, bass.ds(g * GPX, GPX)]).then_inc(x_in[b], 16)
            if not tokens:
                sp.wait_ge(zero_ready, 1)
                for img in range(IMGS):
                    for row in (0, H + 1):
                        for h in range(PARTS_C):
                            sp.dma_start(k.xn_rows[h * P:(h + 1) * P, img, row, :],
                                         zeros[:, 0:W]).then_inc(zero_out, 16)
                        sp.dma_start(k.xn_pixels[img, row], zeros[0:W, :]).then_inc(zero_out, 16)
            over_tiles(sp, [(load, 0)])
            if tokens:
                sp.wait_ge(copied, TILES_ALL + CREDIT)
                sp.dma_start(k.table.rearrange("(t p) r -> p t r", p=P), k.node[:, :, 0:ROW]).then_inc(table_out, 16)
                sp.wait_ge(table_out, 16)
            else:
                sp.wait_ge(zero_out, 16 * IMGS * 2 * (PARTS_C + 1))

        if not tokens:
            @block.gpsimd
            def _(pool):
                pool.memset(zeros[:, :], 0.0).then_inc(zero_ready, 1)

        @block.tensor
        def _(pe):
            pe.sem_inc(var_ready, CREDIT)
            pe.sem_inc(posted, BUFS)

            def mean(img, g, n, u):
                b, c = u % BUFS, u % 2
                if tokens:
                    pe.wait_ge(summed, n + 1)
                else:
                    pe.wait_ge(x_in[b], (n - b) * (LOADED // BUFS) + LOADED)
                pe.wait_ge(centred, n + 1)
                for h in range(PARTS_C):
                    mm = pe.matmul(mean_ps[c][:, :], k.mean_c[:, :], x[b][:, h, :], start=(h == 0), stop=(h == 1))
                mm.then_inc(mean_ready, 1)

            def variance(img, g, n, u):
                c = u % 2
                pe.wait_ge(squared, n + 1)
                pe.wait_ge(spread_ready, n + 1)
                for h in range(PARTS_C):
                    mm = pe.matmul(var_ps[c][:, :], k.mean_c[:, :], square[c][:, h, :], start=(h == 0),
                                   stop=(h == 1))
                mm.then_inc(var_ready, 1)

            def post(img, g, n, u):
                b, c = u % BUFS, u % 2
                pe.wait_ge(normed, n + 1 + CREDIT)
                pe.wait_ge(copied, n + 1)
                if tokens:
                    for t in range(TILE_TOKENS):
                        for h in range(PARTS_C):
                            mm = pe.matmul(post_ps[c][:, t, :], y[b][:, h, t * P:(t + 1) * P],
                                           k.w_graph[:, h, :], start=(h == 0), stop=(h == 1))
                else:
                    for r in range(GROUP_ROWS):
                        for h in range(PARTS_C):
                            mm = pe.transpose(post_ps[c][:, r, h * P:(h + 1) * P], x[b][:, h, r * W:(r + 1) * W],
                                              k.ident[:, :])
                mm.then_inc(posted, 1)
            run(pe, [(mean, 0), (variance, 1), (post, 2)])

        @block.vector
        def _(dve):
            dve.sem_inc(centred, CREDIT)
            dve.sem_inc(normed, CREDIT)

            def add_conv(img, g, n, u):
                b = u % BUFS
                dve.wait_ge(x_in[b], (n - b) * (LOADED // BUFS) + LOADED)
                for h in range(PARTS_C):
                    dve.tensor_scalar(y[b][:, h, :], y[b][:, h, :], k.bn_scale[:, h:h + 1], k.bn_shift[:, h:h + 1],
                                      ALU.mult, ALU.add)
                dve.drain()
                dve.tensor_tensor(x[b][:, :, :], x[b][:, :, :], y[b][:, :, :], ALU.add).then_inc(summed, 1)

            def centre(img, g, n, u):
                b, c = u % BUFS, u % 2
                dve.wait_ge(mean_ready, n + 1)
                dve.tensor_tensor(y[b][:, :, :], x[b][:, :, :],
                                  mean_ps[c][:, :].unsqueeze(1).to_broadcast([P, PARTS_C, GPX]),
                                  ALU.subtract).then_inc(centred, 1)

            def normalise(img, g, n, u):
                b, c = u % BUFS, u % 2
                dve.wait_ge(spread_ready, n + 1 + CREDIT)
                dve.reciprocal(spread[c][:, :], spread[c][:, :])
                dve.drain()
                dve.tensor_tensor(y[b][:, :, :], y[b][:, :, :],
                                  spread[c][:, :].unsqueeze(1).to_broadcast([P, PARTS_C, GPX]),
                                  ALU.mult).then_inc(normed, 1)
            run(dve, ([(add_conv, 0)] if tokens else []) + [(centre, 1), (normalise, 2)])

        @block.scalar
        def _(act):
            act.sem_inc(spread_ready, CREDIT)
            act.sem_inc(copied, CREDIT)
            for b in range(BUFS):
                act.sem_inc(rows_out[b], 1)
                if tokens:
                    act.sem_inc(sums_out[b], 1)
            if not tokens:
                for c in range(2):
                    act.sem_inc(pixels_out[c], 1)

            def squares(img, g, n, u):
                b, c = u % BUFS, u % 2
                act.wait_ge(centred, n + 1 + CREDIT)
                act.wait_ge(var_ready, n + 1)
                act.activation(square[c][:, :, :], y[b][:, :, :], ACT.Square).then_inc(squared, 1)
                if tokens:
                    act.dma_start(k.residual[bass.ds(n, 1)].rearrange("a p h t -> p (a h) t"), x[b][:, :, :]
                                  ).then_inc(sums_out[b], 16)

            def root(img, g, n, u):
                c = u % 2
                act.wait_ge(var_ready, n + 1 + CREDIT)
                act.wait_ge(normed, n + 1)
                act.activation(spread[c][:, :], var_ps[c][:, :], ACT.Sqrt, bias=eps[:, :]).then_inc(spread_ready, 1)

            def store(img, g, n, u):
                b, c = u % BUFS, u % 2
                act.wait_ge(normed, n + 1 + CREDIT)
                if tokens:
                    act.dma_start(k.ln_tiles[bass.ds(n, 1)].rearrange("a p h t -> p (a h) t"), y[b][:, :, :]
                                  ).then_inc(rows_out[b], 16)
                else:
                    for h in range(PARTS_C):
                        act.dma_start(k.xn_rows[h * P:(h + 1) * P, img, bass.ds(g * GROUP_ROWS + 1, GROUP_ROWS), :],
                                      y[b][:, h, :].rearrange("p (r w) -> p r w", w=W)).then_inc(rows_out[b], 16)

            def copy_out(img, g, n, u):
                b, c = u % BUFS, u % 2
                act.wait_ge(posted, n + 1 + BUFS)
                if tokens:
                    act.activation(k.node[:, bass.ds(n * TILE_TOKENS, TILE_TOKENS), :], post_ps[c][:, :, :],
                                   ACT.Copy).then_inc(copied, 1)
                else:
                    act.wait_ge(pixels_out[c], (n - c) * (16 // 2) + 1)
                    act.activation(pixels[c][:, :, :], post_ps[c][:, :, :], ACT.Copy).then_inc(copied, 1)
                    act.wait_ge(copied, n + 1 + CREDIT)
                    act.dma_start(k.xn_pixels[img, bass.ds(g * GROUP_ROWS + 1, GROUP_ROWS)].rearrange(
                        "r w c -> w r c"), pixels[c][:, :, :]).then_inc(pixels_out[c], 16)
            run(act, [(root, 2), (squares, 1)] + ([(copy_out, 3), (store, 2)] if tokens else [(store, 3), (copy_out, 3)]))
            for b in range(BUFS):
                act.wait_ge(rows_out[b], TILES_ALL // BUFS * 16 * ROW_STORES + 1)
                if tokens:
                    act.wait_ge(sums_out[b], TILES_ALL // BUFS * 16 + 1)
            if not tokens:
                for c in range(2):
                    act.wait_ge(pixels_out[c], TILES_ALL // 2 * 16 + 1)


def token_constants(nc, k):
    with ExitStack() as ctx:
        def sb(name, shape, dt):
            return ctx.enter_context(nc.sbuf_tensor("tc_" + name, shape, dt))

        def sem(name):
            return ctx.enter_context(nc.semaphore("tc_" + name))
        gamma, beta = sb("gamma", [P, PARTS_C], F32), sb("beta", [P, PARTS_C], F32)
        moments = sb("moments", [P, PARTS_C, 2], F32)
        spread = sb("spread", [P, PARTS_C], F32)
        gat_t = sb("gat_t", [HE, C], F32)
        attention = sb("attention", [HE, 2], F32)
        blocks = sb("blocks", [HE, 2, HEADS], F32)
        part_ps = [ctx.enter_context(nc.psum_tensor(f"tc_part{h}", [P, 2 * HEADS], F32)) for h in range(PARTS_C)]
        loaded, var_ready, root_ready, ones_ready, blocks_made, blocks_ready, parts_ready = (
            sem(n) for n in ("loaded", "var_ready", "root_ready", "ones_ready", "blocks_made", "blocks_ready",
                             "parts_ready"))
        block = ctx.enter_context(nc.Block())

        @block.sync
        def _(sp):
            with nc.allow_non_contiguous_dma(reason="a few hundred parameters"):
                sp.dma_start(gamma[:, :], k.gamma.rearrange("(h p) -> p h", p=P)).then_inc(loaded, 16)
                sp.dma_start(beta[:, :], k.beta.rearrange("(h p) -> p h", p=P)).then_inc(loaded, 16)
                sp.dma_start(gat_t[:, :], k.w_gat.rearrange("c o -> o c")).then_inc(loaded, 16)
                sp.dma_start(attention[:, 0:1], k.att_src.rearrange("h (e a) -> (h e) a", a=1)).then_inc(loaded, 16)
                sp.dma_start(attention[:, 1:2], k.att_dst.rearrange("h (e a) -> (h e) a", a=1)).then_inc(loaded, 16)
                sp.dma_start(k.w_graph[:, :, 0:HE], k.w_gat.rearrange("(h p) o -> p h o", p=P)).then_inc(loaded, 16)

        @block.gpsimd
        def _(pool):
            pool.memset(blocks[:, :, :], 1.0).then_inc(ones_ready, 1)
            pool.wait_ge(ones_ready, 1)
            pool.affine_select(out=blocks[:, :, :], in_=blocks[:, :, :], compare_op=ALU.is_ge, fill=0.0, base=0,
                               pattern=[[0, 2], [-EXPERTS, HEADS]], channel_multiplier=1).then_inc(blocks_made, 1)
            pool.wait_ge(blocks_made, 1)
            pool.affine_select(out=blocks[:, :, :], in_=blocks[:, :, :], compare_op=ALU.is_ge, fill=0.0,
                               base=EXPERTS - 1, pattern=[[0, 2], [EXPERTS, HEADS]],
                               channel_multiplier=-1).then_inc(blocks_made, 1)

        @block.vector
        def _(dve):
            for h in range(PARTS_C):
                dve.bn_aggr(moments[:, h, :], k.y_stats[:, h, :, :].rearrange("p n s -> p (n s)"))
            dve.wait_ge(loaded, 96)
            dve.wait_ge(blocks_made, 2)
            for s in range(2):
                last = dve.tensor_scalar(blocks[:, s, :], blocks[:, s, :], attention[:, s:s + 1], None, ALU.mult)
            last.then_inc(blocks_ready, 1)
            dve.drain()
            dve.tensor_scalar(spread[:, :], moments[:, :, 1], BN_EPS, None, ALU.add).then_inc(var_ready, 1)
            dve.wait_ge(root_ready, 1)
            dve.reciprocal(spread[:, :], spread[:, :])
            dve.drain()
            dve.tensor_tensor(k.bn_scale[:, :], spread[:, :], gamma[:, :], ALU.mult)
            dve.drain()
            dve.tensor_tensor(spread[:, :], moments[:, :, 0], k.bn_scale[:, :], ALU.mult)
            dve.drain()
            dve.tensor_tensor(k.bn_shift[:, :], beta[:, :], spread[:, :], ALU.subtract)
            dve.wait_ge(parts_ready, 1)
            for h in range(PARTS_C):
                dve.tensor_copy(k.w_graph[:, h, HE:NODE], part_ps[h][:, :])

        @block.scalar
        def _(act):
            act.wait_ge(var_ready, 1)
            act.activation(spread[:, :], spread[:, :], ACT.Sqrt).then_inc(root_ready, 1)

        @block.tensor
        def _(pe):
            pe.wait_ge(loaded, 96)
            pe.wait_ge(blocks_ready, 1)
            for h in range(PARTS_C):
                mm = pe.matmul(part_ps[h][:, :], gat_t[:, h * P:(h + 1) * P],
                               blocks[:, :, :].rearrange("p s h -> p (s h)"), start=True, stop=True)
            mm.then_inc(parts_ready, 1)


def guide_taps(nc, k):
    with ExitStack() as ctx:
        def sb(name, shape, dt):
            return ctx.enter_context(nc.sbuf_tensor(name, shape, dt))

        def sem(name):
            return ctx.enter_context(nc.semaphore(name))
        w_cat = sb("gt_w_cat", [P, PARTS_C, TAPS, GUIDES], F32)
        strip = [sb(f"gt_strip{u}", [P, PARTS_C, GROUP_ROWS + 2, W + 2], F32) for u in range(2)]
        guide = [sb(f"gt_guide{u}", [GUIDES, GPX], F32) for u in range(2)]
        SETS = 2
        SOFTMAXES = GROUP_ROWS * BRANCHES
        highest = sb("gt_highest", [W, SOFTMAXES], F32)
        total = sb("gt_total", [W, SOFTMAXES], F32)
        weight = [sb(f"gt_weight{u}", [W, SOFTMAXES, TAPS], F32) for u in range(2)]
        rest = sb("gt_rest", [W, GROUP_ROWS, GUIDES], F32)
        parts = [sb(f"gt_parts{u}", [W, GROUP_ROWS, SPLITS * GUIDES], BF16) for u in range(2)]
        left = [sb(f"gt_left{u}", [SPLITS * LEFT, GPX], BF16) for u in range(2)]
        right = [sb(f"gt_right{u}", [SPLITS * RIGHT, GPX], BF16) for u in range(2)]
        conv_ps = [ctx.enter_context(nc.psum_tensor(f"gt_conv{u}", [GUIDES, GPX], F32)) for u in range(2)]
        pixel_ps = [ctx.enter_context(nc.psum_tensor(f"gt_pixel{u}", [W, SOFTMAXES, TAPS], F32)) for u in range(2)]
        left_ps = [ctx.enter_context(nc.psum_tensor(f"gt_left_ps{u}", [SPLITS * LEFT, GPX], BF16)) for u in range(2)]
        right_ps = [ctx.enter_context(nc.psum_tensor(f"gt_right_ps{u}", [SPLITS * RIGHT, GPX], BF16))
                    for u in range(2)]
        w_in = sem("gt_w_in")
        strip_in = [sem(f"gt_strip_in{u}") for u in range(2)]
        left_out = [sem(f"gt_left_out{u}") for u in range(2)]
        right_out = [sem(f"gt_right_out{u}") for u in range(2)]
        edges_zero, conv_ready, guide_ready, pixel_ready, shifted, raised, parts_ready, taps_ready, taps_copied = (
            sem("gt_" + n) for n in ("edges_zero", "conv_ready", "guide_ready", "pixel_ready", "shifted", "raised",
                                     "parts_ready", "taps_ready", "taps_copied"))
        block = ctx.enter_context(nc.Block())

        zeros = sb("gt_zeros", [P, ZERO_COLS], F32)
        zero_ready, zero_out = sem("gt_zero_ready"), sem("gt_zero_out")

        @block.gpsimd
        def _(pool):
            pool.memset(zeros[:, :], 0.0).then_inc(zero_ready, 1)
            pool.wait_ge(zero_ready, 1)
            states = k.states.rearrange("(c p r) v -> c p (r v)", p=P, r=P)
            scores = k.dst_scores.rearrange("(n p r) h -> n p (r h)", p=P, r=ZERO_COLS // HEADS)
            parts = ([(scores[n], zeros[:, :]) for n in range(scores.shape[0])]
                     + [(states[c], zeros[:, 0:P * NODE]) for c in range(ZEROED_EARLY)])
            for n, (target, source) in enumerate(parts):
                pool.wait_ge(conv_ready, SETS + n + 1)
                pool.dma_start(target, source).then_inc(zero_out, 16)
            pool.wait_ge(zero_out, 16 * len(parts))

        @block.sync
        def _(sp):
            sp.dma_start(w_cat[:, :, :, :], k.w_cat_t.rearrange("(h p) t o -> p h t o", p=P)).then_inc(w_in, 16)
            sp.wait_ge(edges_zero, 1)

            def body(img, g, n, u):
                sp.wait_ge(conv_ready, n + 1)
                for h in range(PARTS_C):
                    sp.dma_start(strip[u % 2][:, h, :, 1:W + 1],
                                 k.xn_rows[h * P:(h + 1) * P, img, bass.ds(g * GROUP_ROWS, GROUP_ROWS + 2), :]
                                 ).then_inc(strip_in[u % 2], 16)
            over_tiles(sp, [(body, 0)])

        @block.tensor
        def _(pe):
            for freed in (conv_ready, pixel_ready, taps_ready):
                pe.sem_inc(freed, SETS)
            pe.wait_ge(w_in, 16)

            def conv(img, g, n, u):
                b = u % 2
                pe.wait_ge(strip_in[b], (n - b) * 16 + 32)
                pe.wait_ge(guide_ready, n + 1)
                step = 0
                for h in range(PARTS_C):
                    for t in range(TAPS):
                        dy, dx = t // 3, t % 3
                        mm = pe.matmul(conv_ps[b][:, :], w_cat[:, h, t, :],
                                       strip[b][:, h, dy:dy + GROUP_ROWS, dx:dx + W],
                                       start=(step == 0), stop=(step == PARTS_C * TAPS - 1))
                        step += 1
                mm.then_inc(conv_ready, 1)

            def to_pixels(img, g, n, u):
                b = u % 2
                pe.wait_ge(guide_ready, n + 1 + SETS)
                wait_alone(pe, shifted, n + 1, k.passed)
                for r in range(GROUP_ROWS):
                    mm = pe.transpose(pixel_ps[b][:, r * BRANCHES:(r + 1) * BRANCHES, :].rearrange("p a b -> p (a b)"),
                                      guide[b][:, r * W:(r + 1) * W], k.ident[0:GUIDES, 0:GUIDES])
                mm.then_inc(pixel_ready, 1)

            def to_rows(img, g, n, u):
                b = u % 2
                pe.wait_ge(parts_ready, n + 1)
                pe.wait_ge(taps_copied, n + 1)
                for r in range(GROUP_ROWS):
                    pe.transpose(left_ps[b][:, r * W:(r + 1) * W], parts[b][:, r, 0:SPLITS * LEFT], k.ident_b[0:W, 0:W])
                    mm = pe.transpose(right_ps[b][:, r * W:(r + 1) * W], parts[b][:, r, SPLITS * LEFT:],
                                      k.ident_b[0:W, 0:W])
                mm.then_inc(taps_ready, 1)
            through_tiles(pe, [(conv, 0), (to_pixels, 1), (to_rows, 2)])

        @block.scalar
        def _(act):
            act.sem_inc(guide_ready, SETS)
            act.sem_inc(taps_copied, SETS)
            for b in range(2):
                act.sem_inc(left_out[b], 1)
                act.sem_inc(right_out[b], 1)
            def copy_guide(img, g, n, u):
                b = u % 2
                act.wait_ge(conv_ready, n + 1 + SETS)
                act.wait_ge(pixel_ready, n + 1)
                act.activation(guide[b][:, :], conv_ps[b][:, :], ACT.Copy).then_inc(guide_ready, 1)

            def exponent(img, g, n, u):
                act.wait_ge(shifted, n + 1 + SETS)
                act.activation(weight[u % 2][:, :, :], weight[u % 2][:, :, :], ACT.Exp).then_inc(raised, 1)

            def copy_taps(img, g, n, u):
                b = u % 2
                act.wait_ge(taps_ready, n + 1 + SETS)
                act.wait_ge(left_out[b], (n - b) * 8 + 1)
                act.wait_ge(right_out[b], (n - b) * 8 + 1)
                act.activation(left[b][:, :], left_ps[b][:, :], ACT.Copy)
                act.activation(right[b][:, :], right_ps[b][:, :], ACT.Copy).then_inc(taps_copied, 1)
                act.wait_ge(taps_copied, n + 1 + SETS)
                act.dma_start(k.taps_left[:, bass.ds(n * GPX, GPX)], left[b][:, :]).then_inc(left_out[b], 16)
                act.dma_start(k.taps_right[:, bass.ds(n * GPX, GPX)],
                              right[b][:, :]).then_inc(right_out[b], 16)
            through_tiles(act, [(copy_guide, 0), (exponent, 1), (copy_taps, 2)])
            for b in range(2):
                act.wait_ge(left_out[b], IMGS * ROW_GROUPS * 8 + 1)
                act.wait_ge(right_out[b], IMGS * ROW_GROUPS * 8 + 1)

        @block.vector
        def _(dve):
            for b in range(2):
                dve.memset(strip[b][:, :, :, :], 0.0)
            dve.drain()
            dve.sem_inc(edges_zero, 1)
            dve.sem_inc(shifted, SETS)

            def body(img, g, n, u):
                b = u % 2
                dve.wait_ge(pixel_ready, n + 1 + SETS)
                dve.tensor_reduce(highest[:, :], pixel_ps[b][:, :, :], AX_X, ALU.max)
                dve.drain()
                dve.tensor_tensor(weight[b][:, :, :], pixel_ps[b][:, :, :],
                                  highest[:, :].unsqueeze(2).to_broadcast([W, SOFTMAXES, TAPS]),
                                  ALU.subtract).then_inc(shifted, 1)
                dve.wait_ge(raised, n + 1)
                dve.tensor_reduce(total[:, :], weight[b][:, :, :], AX_X, ALU.add)
                dve.drain()
                dve.reciprocal(total[:, :], total[:, :])
                dve.drain()
                dve.tensor_tensor(weight[b][:, :, :], weight[b][:, :, :],
                                  total[:, :].unsqueeze(2).to_broadcast([W, SOFTMAXES, TAPS]), ALU.mult)
                dve.drain()
                dve.wait_ge(taps_ready, n + 1)
                value = weight[b][:, :, :].rearrange("p (r i) t -> p r (i t)", i=BRANCHES)
                for s in range(SPLITS):
                    at = SPLITS * LEFT + s * RIGHT
                    lots = ((slice(0, LEFT), parts[b][:, :, s * LEFT:(s + 1) * LEFT]),
                            (slice(LEFT, GUIDES), parts[b][:, :, at:at + RIGHT]))
                    for lot, part in lots:
                        dve.tensor_copy(part, value[:, :, lot])
                    dve.drain()
                    if s < SPLITS - 1:
                        for lot, part in lots:
                            dve.tensor_tensor(rest[:, :, lot], value[:, :, lot], part, ALU.subtract)
                        dve.drain()
                        value = rest[:, :, :]
                dve.sem_inc(parts_ready, 1)
            through_tiles(dve, [(body, 0)])


CLASSES = 6
CLASS_ROWS = H // CLASSES
CLASS_GROUPS = CLASS_ROWS // GROUP_ROWS


def branch_masks(nc, k):
    with ExitStack() as ctx:
        zeroed = ctx.enter_context(nc.semaphore("bm_zeroed"))
        made = ctx.enter_context(nc.semaphore("bm_made"))
        wide = ctx.enter_context(nc.sbuf_tensor("bm_wide", [W, len(k.offsets), GPX], F32))
        block = ctx.enter_context(nc.Block())

        @block.gpsimd
        def _(pool):
            pool.memset(wide[:, :, :], 0.0)
            pool.memset(k.pick_left[:, :, :], 0.0)
            pool.memset(k.pick_right[:, :, :], 0.0).then_inc(zeroed, 1)
            pool.wait_ge(zeroed, 1)
            for n, dx in enumerate(k.offsets):
                v = wide[:, n, :].rearrange("p (r w) -> p r w", w=W)
                pool.affine_select(out=v, in_=v, compare_op=ALU.not_equal, fill=1.0, base=-dx,
                                   pattern=[[0, GROUP_ROWS], [-1, W]], channel_multiplier=1)
            for pick, taps in ((k.pick_left, LEFT), (k.pick_right, RIGHT)):
                for s in range(SPLITS):
                    pool.affine_select(out=pick[:, :, :], in_=pick[:, :, :], compare_op=ALU.not_equal, fill=1.0,
                                       base=-s * taps, pattern=[[-1, taps], [0, W]], channel_multiplier=1
                                       ).then_inc(made, 1)
                    pool.wait_ge(made, (s + 1) if taps == LEFT else SPLITS + s + 1)

        @block.vector
        def _(dve):
            dve.wait_ge(made, 1)
            dve.tensor_copy(k.masks[:, :, :], wide[:, :, :])


def dilated_branches(nc, k):
    SETS = 2
    PAIR = 2
    assert CLASSES % PAIR == 0
    with ExitStack() as ctx:
        def sb(name, shape, dt):
            return ctx.enter_context(nc.sbuf_tensor(name, shape, dt))

        def sem(name):
            return ctx.enter_context(nc.semaphore(name))
        w_scale = sb("db_w_scale", [P, (BRANCHES + 1) * PARTS_C, C], F32)
        own, above, below = ([sb(f"db_{name}{c}", [W, CLASS_ROWS, C], F32) for c in range(PAIR)]
                             for name in ("own", "above", "below"))
        rows = [sb(f"db_rows{c}", [P, PARTS_C, CLASS_ROWS, W], F32) for c in range(PAIR)]
        left = [sb(f"db_left{c}", [SPLITS * LEFT, CLASS_ROWS, W], BF16) for c in range(PAIR)]
        right = [sb(f"db_right{c}", [SPLITS * RIGHT, CLASS_ROWS, W], BF16) for c in range(PAIR)]
        diagonals = [sb(f"db_diagonals{i}", [W, 3, GPX], F32) for i in range(BRANCHES)]
        branch = [sb(f"db_branch{u}", [P, PARTS_C, GPX], F32) for u in range(SETS)]
        y = [sb(f"db_y{u}", [P, PARTS_C, GPX], F32) for u in range(SETS)]
        tap_ps = [ctx.enter_context(nc.psum_tensor(f"db_tap{u}", [W, GPX], F32)) for u in range(2)]
        branch_ps = [[ctx.enter_context(nc.psum_tensor(f"db_branch_ps{u}{h}", [P, GPX], F32))
                      for h in range(PARTS_C)] for u in range(2)]
        y_ps = [ctx.enter_context(nc.psum_tensor(f"db_y_ps{h}", [P, GPX], F32)) for h in range(PARTS_C)]
        w_in, y_copied, y_used = (sem("db_" + n) for n in ("w_in", "y_copied", "y_used"))
        class_in = [sem(f"db_class_in{c}") for c in range(PAIR)]
        zeroed, tap_ready, tap_placed, branch_ready, branch_copied, branch_used = (
            sem("db_" + n) for n in ("zeroed", "tap_ready", "tap_placed", "branch_ready", "branch_copied",
                                     "branch_used"))
        y_out = [sem(f"db_y_out{u}") for u in range(SETS)]
        LOADS = 3 + PARTS_C + 2
        CLASS_STEPS = CLASS_GROUPS * BRANCHES
        STEPS = PAIR * CLASS_STEPS
        GROUPS = PAIR * CLASS_GROUPS
        GATHER_SPREADS = TAPS - 3
        USED = CLASS_STEPS + SETS
        block = ctx.enter_context(nc.Block())

        def class_pairs(eng, body):
            for img in range(IMGS):
                with eng.Fori(0, CLASSES // PAIR) as i:
                    body(img, i, i + img * (CLASSES // PAIR))

        def place(step):
            group, b = divmod(step, BRANCHES)
            return group // CLASS_GROUPS, group % CLASS_GROUPS, b

        @block.sync
        def _(sp):
            sp.dma_start(w_scale[:, :, :], k.w_scale_t.rearrange("(c p) o -> p c o", p=P)).then_inc(w_in, 16)

            def body(img, i, n):
                for c in range(PAIR):
                    r = i * PAIR + c
                    wait_alone(sp, branch_used, n * STEPS + (USED + (c - 1) * CLASS_STEPS), k.passed)
                    pixels = k.xn_pixels[img, 0:H].rearrange("(k s) w c -> w s k c", s=CLASSES)
                    pixels_1 = k.xn_pixels[img, 1:H + 1].rearrange("(k s) w c -> w s k c", s=CLASSES)
                    pixels_2 = k.xn_pixels[img, 2:H + 2].rearrange("(k s) w c -> w s k c", s=CLASSES)
                    for tile, source in ((above[c], pixels), (own[c], pixels_1), (below[c], pixels_2)):
                        sp.dma_start(tile[:, :, :], source[:, bass.ds(r, 1), :, :].rearrange(
                            "w s k c -> w (s k) c")).then_inc(class_in[c], 16)
                    by_rows = k.xn_rows[:, img, 1:H + 1, :].rearrange("(h p) (k s) w -> p h s k w", p=P, s=CLASSES)
                    for h in range(PARTS_C):
                        sp.dma_start(rows[c][:, h, :, :], by_rows[:, h, bass.ds(r, 1), :, :].rearrange(
                            "p s k w -> p (s k) w")).then_inc(class_in[c], 16)
                    for tile, source in ((left[c], k.taps_left), (right[c], k.taps_right)):
                        v = source[:, img * PIX:(img + 1) * PIX].rearrange("t (k s w) -> t s k w", s=CLASSES, w=W)
                        sp.dma_start(tile[:, :, :], v[:, bass.ds(r, 1), :, :].rearrange("t s k w -> t (s k) w")
                                     ).then_inc(class_in[c], 16)
            class_pairs(sp, body)

        @block.tensor
        def _(pe):
            pe.wait_ge(w_in, 16)
            pe.wait_ge(zeroed, 1)
            pe.sem_inc(branch_used, USED)

            def body(img, i, n):
                def spread_tap(step, at):
                    c, q, b = place(step)
                    if step % CLASS_STEPS == 0 and at == 0:
                        pe.wait_ge(class_in[c], n * (16 * LOADS) + 16 * LOADS)
                    m = step * TAPS + at
                    t = at % 3 * 3 + at // 3
                    pick, taps, base = ((k.pick_left, left[c], b * TAPS) if b < LEFT_BRANCHES else
                                        (k.pick_right, right[c], (b - LEFT_BRANCHES) * TAPS))
                    pe.wait_ge(tap_placed, n * (STEPS * TAPS) + m + 1)
                    pe.matmul(tap_ps[m % 2][:, :], pick[:, base + t, :],
                              taps[:, q * GROUP_ROWS:(q + 1) * GROUP_ROWS, :],
                              start=True, stop=True).then_inc(tap_ready, 1)

                def gather_rows(step):
                    c, q, b = place(step)
                    jump = DILATIONS[b] // CLASSES
                    pe.wait_ge(branch_copied, n * STEPS + step + 1)
                    pe.wait_ge(tap_placed, n * (STEPS * TAPS) + (step + 1) * TAPS + 2)
                    spreads = 0 if step + 1 == STEPS else GATHER_SPREADS if step >= 1 else TAPS
                    parts = PARTS_C * GROUP_ROWS
                    for h in range(PARTS_C):
                        for i in range(GROUP_ROWS):
                            row = q * GROUP_ROWS + i
                            if DILATIONS[b] == 1:
                                used = [(0, above[c], row), (1, own[c], row), (2, below[c], row)]
                            else:
                                used = [(dy, own[c], row + (dy - 1) * jump) for dy in range(3)
                                        if 0 <= row + (dy - 1) * jump < CLASS_ROWS]
                            for at, (dy, tile, source) in enumerate(used):
                                mm = pe.matmul(branch_ps[step % 2][h][:, i * W:(i + 1) * W],
                                               tile[:, source, h * P:(h + 1) * P],
                                               diagonals[b][:, dy, i * W:(i + 1) * W],
                                               start=(at == 0), stop=(at == len(used) - 1))
                            done = h * GROUP_ROWS + i
                            if done == parts - 1:
                                mm.then_inc(branch_ready, 1)
                            for at in range(spreads * done // parts, spreads * (done + 1) // parts):
                                spread_tap(step + 1, at)

                def scale(step):
                    c, q, b = place(step)
                    left_over = list(range(GATHER_SPREADS, TAPS)) if step + 2 < STEPS else []
                    if b == 0:
                        pe.wait_ge(y_copied, n * GROUPS + (c * CLASS_GROUPS + q + 1))
                        for o in range(PARTS_C):
                            for h in range(PARTS_C):
                                pe.matmul(y_ps[o][:, :], w_scale[:, h, o * P:(o + 1) * P],
                                          rows[c][:, h, q * GROUP_ROWS:(q + 1) * GROUP_ROWS, :],
                                          start=(h == 0), stop=False)
                    pe.wait_ge(branch_copied, n * STEPS + step + 1 + SETS)
                    for o in range(PARTS_C):
                        for h in range(PARTS_C):
                            if left_over:
                                spread_tap(step + 2, left_over.pop(0))
                            last = b == BRANCHES - 1 and h == PARTS_C - 1
                            mm = pe.matmul(y_ps[o][:, :], w_scale[:, (b + 1) * PARTS_C + h, o * P:(o + 1) * P],
                                           branch[step % 2][:, h, :], start=False, stop=last)
                            if o * PARTS_C + h == PARTS_C * PARTS_C - 1:
                                mm.then_inc(branch_used, 1)

                for at in range(TAPS):
                    spread_tap(0, at)
                for step in range(STEPS):
                    gather_rows(step)
                    if step >= 1:
                        scale(step - 1)
                scale(STEPS - 1)
            class_pairs(pe, body)

        @block.vector
        def _(dve):
            for b in range(BRANCHES):
                dve.memset(diagonals[b][:, :, :], 0.0)
            dve.drain()
            dve.sem_inc(zeroed, 1)
            dve.sem_inc(tap_placed, 2)

            def body(img, i, n):
                for step in range(STEPS):
                    c, q, b = place(step)
                    for at in range(TAPS):
                        dx, dy = divmod(at, 3)
                        m = step * TAPS + at
                        if dy == 0:
                            dve.drain()
                        mask = k.offsets.index((dx - 1) * DILATIONS[b])
                        wait_alone(dve, tap_ready, n * (STEPS * TAPS) + m + 1, k.passed)
                        dve.copy_predicated(diagonals[b][:, dy, :], k.masks[:, mask, :],
                                            tap_ps[m % 2][:, :]).then_inc(tap_placed, 1)
                    if b == 1 and step >= BRANCHES:
                        statistics(n, step // BRANCHES - 1)
                statistics(n, GROUPS - 1)

            def statistics(n, q):
                dve.wait_ge(y_copied, n * GROUPS + q + 2)
                for h in range(PARTS_C):
                    last = dve.bn_stats(k.y_stats[:, h, bass.ds(n * GROUPS + q, 1), :].rearrange(
                        "p a s -> p (a s)"), y[q % 2][:, h, :])
                last.then_inc(y_used, 1)
            class_pairs(dve, body)

        @block.scalar
        def _(act):
            act.sem_inc(y_used, 2)
            act.sem_inc(branch_copied, SETS)
            act.sem_inc(y_copied, 1)
            for u in range(SETS):
                act.sem_inc(y_out[u], 1)

            def body(img, i, n):
                for step in range(STEPS):
                    act.wait_ge(branch_ready, n * STEPS + step + 1)
                    act.wait_ge(branch_used, n * STEPS + (step + 1 + CLASS_STEPS))
                    for h in range(PARTS_C):
                        last = act.activation(branch[step % 2][:, h, :], branch_ps[step % 2][h][:, :], ACT.Copy)
                    last.then_inc(branch_copied, 1)
                    if step % BRANCHES == 0 and step >= BRANCHES:
                        copy_y(img, i, n, step // BRANCHES - 1)
                copy_y(img, i, n, GROUPS - 1)

            def copy_y(img, i, n, group):
                c, q = divmod(group, CLASS_GROUPS)
                act.wait_ge(branch_used, n * STEPS + ((group + 1) * BRANCHES + USED))
                act.wait_ge(y_used, n * GROUPS + group + 1)
                act.wait_ge(y_out[q % 2], n * (16 * PARTS_C * GROUPS // 2) + 16 * PARTS_C * (group // 2) + 1)
                for h in range(PARTS_C):
                    last = act.activation(y[q % 2][:, h, :], y_ps[h][:, :], ACT.Copy)
                last.then_inc(y_copied, 1)
                act.wait_ge(y_copied, n * GROUPS + group + 2)
                for h in range(PARTS_C):
                    v = k.conv_out[h * P:(h + 1) * P, img, :, :].rearrange("p (k s) w -> p s k w", s=CLASSES)
                    act.dma_start(v[:, bass.ds(i * PAIR + c, 1), q * GROUP_ROWS:(q + 1) * GROUP_ROWS, :].rearrange(
                        "p s k w -> p (s k) w"), y[q % 2][:, h, :].rearrange("p (k w) -> p k w", w=W)
                        ).then_inc(y_out[q % 2], 16)
            class_pairs(act, body)
            for u in range(2):
                act.wait_ge(y_out[u], IMGS * CLASSES * PARTS_C * CLASS_GROUPS // 2 * 16 + 1)


LEAK = 0.2
FAR = 1e30


def place_scores(nc, k):
    with ExitStack() as ctx:
        placed = ctx.enter_context(nc.semaphore("ps_placed"))
        scores = ctx.enter_context(nc.sbuf_tensor("ps_scores", [P, TILES, HEADS], F32))
        scores_ready = ctx.enter_context(nc.semaphore("ps_scores_ready"))
        block = ctx.enter_context(nc.Block())

        @block.vector
        def _(dve):
            dve.tensor_copy(scores[:, :, :], k.node[:, :, HE + HEADS:NODE]).then_inc(scores_ready, 1)

        @block.gpsimd
        def _(pool):
            pool.wait_ge(scores_ready, 1)
            for t in range(TILES):
                pool.indirect_dma_start(k.dst_scores[:, :],
                                        bass.IndirectOffsetOnAxis(k.first_place[:, t:t + 1], 0),
                                        scores[:, t, :], None, bounds_check=E - 1,
                                        oob_is_err=False).then_inc(placed, 16)
            pool.wait_ge(placed, 16 * TILES)

        expert_share(nc, k, block, FIRST_PLACES, BESIDE_PLACES, 4)


def edge_softmax(nc, k):
    SUMS = HE + HEADS
    with ExitStack() as ctx:
        def sb(name, shape, dt):
            return ctx.enter_context(nc.sbuf_tensor("es_" + name, shape, dt))

        def sem(name):
            return ctx.enter_context(nc.semaphore("es_" + name))

        def ps(name, shape):
            return ctx.enter_context(nc.psum_tensor("es_" + name, shape, F32))
        keys, before = sb("keys", [P, P], I32), sb("before", [P, P], I32)
        given = sb("given", [P, P, HEADS], F32)
        run, run_before = sb("run", [P, P], I32), sb("run_before", [P, P], I32)
        fetched = sb("fetched", [P, P, ROW], F32)
        same_next = sb("same_next", [P, P], F32)
        given_next = sb("given_next", [P, HEADS, P], F32)
        same = sb("same", [P, HEADS, P], F32)
        given_row = sb("given_row", [P, HEADS, P], F32)
        first = sb("first", [P, 4], F32)
        penalty = sb("penalty", [P, HEADS, P], F32)
        src_score = sb("src_score", [P, HEADS, P], F32)
        dst_score = sb("dst_score", [P, HEADS, P], F32)
        score = sb("score", [P, HEADS, P], F32)
        score_0 = sb("score_0", [P, HEADS], F32)
        peak = sb("peak", [P, HEADS, P], F32)
        peak_in = sb("peak_in", [P, HEADS], F32)
        powers = sb("powers", [P, 2 * HEADS * P + HEADS], F32)
        decay = powers[:, 0:HEADS * P].rearrange("p (h j) -> p h j", h=HEADS)
        weight = powers[:, HEADS * P:2 * HEADS * P].rearrange("p (h j) -> p h j", h=HEADS)
        decay_all = powers[:, 2 * HEADS * P:]
        decay_0 = sb("decay_0", [P, SUMS], F32)
        value = sb("value", [P, SUMS, P], F32)
        value_decay = sb("value_decay", [P, SUMS, P], F32)
        sums = sb("sums", [P, SUMS, P], F32)
        ends = sb("ends", [P, 2, SUMS], F32)
        rows_out = sb("rows_out", [P, P, NODE], F32)
        factor_row = sb("factor_row", [SUMS, P], F32)
        handed = [sb("handed_score", [HEADS, P + 1], F32), sb("handed_peak", [HEADS, P + 1], F32),
                  sb("handed_sums", [SUMS, P + 1], F32)]
        turned_ps = ps("turned_ps", [SUMS, 2, P])
        back_ps = ps("back_ps", [P, SUMS])
        (chunk_in, decoded, rows_in, rows_taken, ends_ready, ends_turned, handed_ready,
         handed_turned, powers_ready, raised, rows_ready, stored) = (sem(n) for n in (
             "chunk_in", "decoded", "rows_in", "rows_taken", "ends_ready", "ends_turned",
             "handed_ready", "handed_turned", "powers_ready", "raised", "rows_ready", "stored"))
        block = ctx.enter_context(nc.Block())

        def over_chunks(eng, body):
            own = eng.value_load(k.edge_counts[0:1, 0:1], min_val=1, max_val=E)
            with eng.Fori(0, CHUNKS) as c:
                with eng.If(c * CHUNK < own):
                    body(c, own)

        @block.sync
        def _(sp):
            def load(c):
                sp.dma_start(keys[:, :], k.sorted_keys[bass.ds(c * CHUNK + P, CHUNK)].rearrange(
                    "(p f) -> p f", p=P)).then_inc(chunk_in, 16)
                sp.dma_start(before[:, :], k.sorted_keys[bass.ds(c * CHUNK + (P - 1), CHUNK)].rearrange(
                    "(p f) -> p f", p=P)).then_inc(chunk_in, 16)
                sp.dma_start(given[:, :, :], k.dst_scores[bass.ds(c * CHUNK, CHUNK), :].rearrange(
                    "(p f) h -> p f h", p=P)).then_inc(chunk_in, 16)
            def load_rows(c):
                sp.dma_start(fetched[:, :, :].rearrange("p j v -> p (j v)"),
                             k.edge_rows[bass.ds(c, 1)].rearrange("a p v -> p (a v)")).then_inc(rows_in, 16)
            load(0)
            load_rows(0)
            sp.sem_inc(stored, 1)

            def body(c, own):
                wait_alone(sp, decoded, c + 1, k.passed)
                load(c + 1)
                wait_alone(sp, rows_taken, c + 1, k.passed)
                with sp.If((c + 1) * CHUNK < own):
                    load_rows(c + 1)
                wait_alone(sp, rows_ready, c + 1, k.passed)
                sp.dma_start(k.states[bass.ds(c * CHUNK, CHUNK), :].rearrange("(p f) r -> p f r", p=P),
                             rows_out[:, :, :]).then_inc(stored, 16)
                wait_alone(sp, stored, c * 16 + 17, k.passed)
            over_chunks(sp, body)
            sp.wait_ge(chunk_in, 48)

        @block.scalar
        def _(act):
            def body(c, own):
                act.wait_ge(powers_ready, c + 1)
                act.activation(powers[:, :], powers[:, :], ACT.Exp).then_inc(raised, 1)
            over_chunks(act, body)

        @block.tensor
        def _(pe):
            def body(c, own):
                for r, channels in enumerate((HEADS, HEADS, SUMS)):
                    wait_alone(pe, ends_ready, c * 3 + r + 1, k.passed)
                    for i in range(2):
                        mm = pe.transpose(turned_ps[0:channels, i, :], ends[:, i, 0:channels], k.ident[:, :])
                    mm.then_inc(ends_turned, 1)
                    wait_alone(pe, handed_ready, c * 3 + r + 1, k.passed)
                    pe.transpose(back_ps[:, 0:channels], handed[r][:, 0:P],
                                 k.ident[0:channels, 0:channels]).then_inc(handed_turned, 1)
            over_chunks(pe, body)

        @block.vector
        def _(dve):
            def flat(t):
                return t[:, :, :].rearrange("p c j -> p (c j)")

            def decode(c):
                dve.wait_ge(chunk_in, c * 48 + 48)
                dve.tensor_scalar(run[:, :], keys[:, :], SRC_BITS, None, ALU.logical_shift_right)
                dve.tensor_scalar(run_before[:, :], before[:, :], SRC_BITS, None, ALU.logical_shift_right)
                dve.tensor_copy(given_next[:, :, :], given[:, :, :].rearrange("p j h -> p h j"))
                dve.drain().then_inc(decoded, 1)
                dve.tensor_tensor(same_next[:, :], run[:, :], run_before[:, :], ALU.is_equal)
                dve.drain()

            def hand_on(c, r, channels, initial_op, op):
                dve.drain().then_inc(ends_ready, 1)
                dve.wait_ge(ends_turned, c * 3 + r + 1)
                dve.tensor_copy(factor_row[0:channels, :], turned_ps[0:channels, 1, :])
                dve.tensor_copy(handed[r][:, 0:1], handed[r][:, P:P + 1])
                dve.drain()
                dve.tensor_tensor_scan(handed[r][:, 1:P + 1], factor_row[0:channels, :], turned_ps[0:channels, 0, :],
                                       handed[r][:, 0:1], initial_op, op).then_inc(handed_ready, 1)
                dve.wait_ge(handed_turned, c * 3 + r + 1)

            for r, start in enumerate((0.0, -FAR, 0.0)):
                dve.memset(handed[r][:, :], start)
            dve.drain()
            decode(0)

            def body(c, own):
                wait_alone(dve, rows_in, c * 16 + 16, k.passed)
                dve.tensor_copy(value[:, 0:HE, :], fetched[:, :, 0:HE].rearrange("p j v -> p v j"))
                dve.tensor_copy(src_score[:, :, :], fetched[:, :, HE:ROW].rearrange("p j v -> p v j"))
                dve.tensor_copy(same[:, :, :], same_next[:, :].unsqueeze(1).to_broadcast([P, HEADS, P]))
                dve.tensor_copy(given_row[:, :, :], given_next[:, :, :])
                dve.tensor_copy(first[:, 0:1], same_next[:, 0:1])
                dve.tensor_reduce(first[:, 2:3], same_next[:, :], AX_X, ALU.min)
                dve.drain().then_inc(rows_taken, 1)
                decode(c + 1)
                dve.memset(same[:, :, 0:1], 0.0)
                for i in (0, 2):
                    dve.tensor_scalar(first[:, i + 1:i + 2], first[:, i:i + 1], -1.0, FAR, ALU.add, ALU.mult)
                dve.drain()

                dve.tensor_scalar(penalty[:, :, :], same[:, :, :], -1.0, FAR, ALU.add, ALU.mult)
                dve.tensor_tensor_scan(flat(dst_score), flat(same), flat(given_row), 0.0, ALU.mult, ALU.add)
                dve.drain()
                dve.tensor_copy(ends[:, 0, 0:HEADS], dst_score[:, :, P - 1])
                dve.tensor_copy(ends[:, 1, 0:HEADS], first[:, 2:3].to_broadcast([P, HEADS]))
                hand_on(c, 0, HEADS, ALU.mult, ALU.add)
                dve.scalar_tensor_tensor(given_row[:, :, 0], back_ps[:, 0:HEADS], first[:, 0:1], given_row[:, :, 0],
                                         ALU.mult, ALU.add)
                dve.drain()
                dve.tensor_tensor_scan(flat(dst_score), flat(same), flat(given_row), 0.0, ALU.mult, ALU.add)
                dve.drain()

                dve.tensor_tensor(dst_score[:, :, :], dst_score[:, :, :], src_score[:, :, :], ALU.add)
                dve.drain()
                dve.scalar_tensor_tensor(score[:, :, :], dst_score[:, :, :], LEAK, dst_score[:, :, :], ALU.mult,
                                         ALU.max)
                dve.drain()
                dve.tensor_tensor_scan(flat(peak), flat(penalty), flat(score), -FAR, ALU.add, ALU.max)
                dve.tensor_copy(score_0[:, :], score[:, :, 0])
                dve.drain()
                dve.tensor_copy(ends[:, 0, 0:HEADS], peak[:, :, P - 1])
                dve.tensor_copy(ends[:, 1, 0:HEADS], first[:, 3:4].to_broadcast([P, HEADS]))
                hand_on(c, 1, HEADS, ALU.add, ALU.max)
                dve.tensor_copy(peak_in[:, :], back_ps[:, 0:HEADS])
                dve.drain()
                dve.scalar_tensor_tensor(score[:, :, 0], peak_in[:, :], first[:, 1:2], score[:, :, 0], ALU.add,
                                         ALU.max)
                dve.drain()
                dve.tensor_tensor_scan(flat(peak), flat(penalty), flat(score), -FAR, ALU.add, ALU.max)
                dve.drain()

                dve.tensor_copy(score[:, :, 0], score_0[:, :])
                dve.tensor_tensor(decay[:, :, 1:P], peak[:, :, 0:P - 1], peak[:, :, 1:P], ALU.subtract)
                dve.tensor_tensor(decay[:, :, 0], peak_in[:, :], peak[:, :, 0], ALU.subtract)
                dve.tensor_tensor(decay_all, peak_in[:, :], peak[:, :, P - 1], ALU.subtract)
                dve.drain()
                dve.tensor_tensor(weight, score[:, :, :], peak[:, :, :], ALU.subtract)
                dve.drain()
                dve.tensor_scalar(powers[:, :], powers[:, :], 0.0, None, ALU.min).then_inc(powers_ready, 1)
                wait_alone(dve, raised, c + 1, k.passed)
                dve.tensor_scalar(decay_0[:, HE:SUMS], decay[:, :, 0], first[:, 0:1], None, ALU.mult)
                dve.tensor_scalar(ends[:, 1, HE:SUMS], decay_all, first[:, 2:3], None, ALU.mult)
                dve.tensor_tensor(value_decay[:, HE:SUMS, :], decay, same[:, :, :], ALU.mult)
                dve.tensor_copy(value[:, HE:SUMS, :], weight)
                dve.drain()
                for h in range(HEADS):
                    own = slice(h * EXPERTS, (h + 1) * EXPERTS)
                    one = slice(HE + h, HE + h + 1)
                    dve.tensor_copy(value_decay[:, own, :], value_decay[:, one, :].to_broadcast([P, EXPERTS, P]))
                    dve.tensor_tensor(value[:, own, :], value[:, own, :],
                                      value[:, one, :].to_broadcast([P, EXPERTS, P]), ALU.mult)
                    dve.tensor_copy(decay_0[:, own], decay_0[:, one].to_broadcast([P, EXPERTS]))
                    dve.tensor_copy(ends[:, 1, own], ends[:, 1, one].to_broadcast([P, EXPERTS]))
                dve.drain()
                dve.tensor_tensor_scan(flat(sums), flat(value_decay), flat(value), 0.0, ALU.mult, ALU.add)
                dve.drain()
                dve.tensor_copy(ends[:, 0, :], sums[:, :, P - 1])
                hand_on(c, 2, SUMS, ALU.mult, ALU.add)
                dve.tensor_tensor(decay_0[:, :], decay_0[:, :], back_ps[:, :], ALU.mult)
                dve.drain()
                dve.tensor_tensor(value[:, :, 0], value[:, :, 0], decay_0[:, :], ALU.add)
                dve.drain()
                dve.tensor_tensor_scan(flat(sums), flat(value_decay), flat(value), 0.0, ALU.mult, ALU.add)
                dve.drain()
                wait_alone(dve, stored, c * 16 + 1, k.passed)
                dve.tensor_copy(rows_out[:, :, 0:SUMS], sums[:, :, :].rearrange("p c j -> p j c"))
                dve.tensor_copy(rows_out[:, :, SUMS:NODE], peak[:, :, :].rearrange("p c j -> p j c"))
                dve.drain().then_inc(rows_ready, 1)
            over_chunks(dve, body)


def gates(nc, k):
    with ExitStack() as ctx:
        def sb(name, shape):
            return ctx.enter_context(nc.sbuf_tensor("ga_" + name, shape, F32))

        def sem(name):
            return ctx.enter_context(nc.semaphore("ga_" + name))
        state = sb("state", [P, TILES, NODE])
        last = sb("last", [P, ROW])
        b_gat, ln_gamma, ln_beta = sb("b_gat", [P, HE]), sb("ln_gamma", [P, HE]), sb("ln_beta", [P, HE])
        S4 = [P, TILES, HEADS]
        loop, late, own, peak, total, part = (sb(n, S4) for n in ("loop", "late", "own", "peak", "total", "part"))
        S16 = [P, TILES, HEADS, EXPERTS]
        agg, term = sb("agg", S16), sb("term", S16)
        mean, spread = sb("mean", [P, TILES]), sb("spread", [P, TILES])
        fetched, loaded, powers_ready, raised, var_ready, root_ready, gaps_ready, gaps_raised = (
            sem(n) for n in ("fetched", "loaded", "powers_ready", "raised", "var_ready", "root_ready",
                             "gaps_ready", "gaps_raised"))
        block = ctx.enter_context(nc.Block())

        @block.gpsimd
        def _(pool):
            for t in range(TILES):
                pool.indirect_dma_start(state[:, t, :], None, k.states[:, :],
                                        bass.IndirectOffsetOnAxis(k.last_place[:, t:t + 1], 0)).then_inc(fetched, 16)

        expert_share(nc, k, block, FIRST_GATES, BESIDE_GATES, 4)

        @block.sync
        def _(sp):
            sp.dma_start(last[:, :], k.table[TOK - 1:TOK, :].to_broadcast([P, ROW])).then_inc(loaded, 16)
            for tile, source in ((b_gat, k.b_gat), (ln_gamma, k.ln_gamma), (ln_beta, k.ln_beta)):
                sp.dma_start(tile[:, :], source.rearrange("(a n) -> a n", a=1).to_broadcast([P, HE])
                             ).then_inc(loaded, 16)

        @block.scalar
        def _(act):
            act.wait_ge(powers_ready, 1)
            for tile in (loop, late, own):
                mm = act.activation(tile[:, :, :], tile[:, :, :], ACT.Exp)
            mm.then_inc(raised, 1)
            act.wait_ge(var_ready, 1)
            act.activation(spread[:, :], spread[:, :], ACT.Sqrt).then_inc(root_ready, 1)
            act.wait_ge(gaps_ready, 1)
            act.activation(k.gate[:, :, :], k.gate[:, :, :], ACT.Exp).then_inc(gaps_raised, 1)

        @block.vector
        def _(dve):
            def tt(out, a, b, op):
                dve.tensor_tensor(out, a, b, op)
                dve.drain()

            def ts(out, a, s1, s2, op0, op1=ALU.bypass):
                dve.tensor_scalar(out, a, s1, s2, op0, op1)
                dve.drain()

            def by_tile(t, n):
                return t[:, :].unsqueeze(2).to_broadcast([P, TILES, n])

            def over_experts(t):
                return t.unsqueeze(3).to_broadcast(S16)

            def vector(v):
                return v.rearrange("p (h e) -> p h e", h=HEADS).unsqueeze(1).to_broadcast(S16)

            def masked(t, flag):
                dve.tensor_scalar(part[:, :, :], by_tile(flag, HEADS), -1.0, FAR, ALU.add, ALU.mult)
                tt(t[:, :, :], t[:, :, :], by_tile(flag, HEADS), ALU.mult)
                tt(t[:, :, :], t[:, :, :], part[:, :, :], ALU.add)

            def leaky(t):
                dve.scalar_tensor_tensor(t[:, :, :], t[:, :, :], LEAK, t[:, :, :], ALU.mult, ALU.max)
                dve.drain()
            to_score = k.node[:, :, HE + HEADS:NODE]
            dve.wait_ge(loaded, 64)
            tt(loop[:, :, :], k.node[:, :, HE:HE + HEADS], to_score, ALU.add)
            tt(late[:, :, :], last[:, HE:ROW].unsqueeze(1).to_broadcast(S4), to_score, ALU.add)
            leaky(loop)
            leaky(late)
            masked(late, k.has_last)
            dve.wait_ge(fetched, 16 * TILES)
            dve.tensor_copy(own[:, :, :], state[:, :, ROW:NODE])
            dve.drain()
            masked(own, k.has_own)
            tt(peak[:, :, :], loop[:, :, :], late[:, :, :], ALU.max)
            tt(peak[:, :, :], peak[:, :, :], own[:, :, :], ALU.max)
            for t in (loop, late, own):
                dve.tensor_tensor(t[:, :, :], t[:, :, :], peak[:, :, :], ALU.subtract)
            dve.drain().then_inc(powers_ready, 1)
            dve.wait_ge(raised, 1)
            tt(late[:, :, :], late[:, :, :], by_tile(k.count_last, HEADS), ALU.mult)
            tt(total[:, :, :], own[:, :, :], state[:, :, HE:ROW], ALU.mult)
            tt(total[:, :, :], total[:, :, :], loop[:, :, :], ALU.add)
            tt(total[:, :, :], total[:, :, :], late[:, :, :], ALU.add)
            ts(total[:, :, :], total[:, :, :], 1e-16, None, ALU.add)
            dve.reciprocal(total[:, :, :], total[:, :, :])

            def heads(t):
                return t.rearrange("p t (h e) -> p t h e", h=HEADS)
            tt(agg[:, :, :, :], heads(state[:, :, 0:HE]), over_experts(own[:, :, :]), ALU.mult)
            tt(term[:, :, :, :], heads(k.node[:, :, 0:HE]), over_experts(loop[:, :, :]), ALU.mult)
            tt(agg[:, :, :, :], agg[:, :, :, :], term[:, :, :, :], ALU.add)
            tt(term[:, :, :, :], vector(last[:, 0:HE]), over_experts(late[:, :, :]), ALU.mult)
            tt(agg[:, :, :, :], agg[:, :, :, :], term[:, :, :, :], ALU.add)
            tt(agg[:, :, :, :], agg[:, :, :, :], over_experts(total[:, :, :]), ALU.mult)
            tt(agg[:, :, :, :], agg[:, :, :, :], vector(b_gat[:, :]), ALU.add)

            rows, term_rows = (t[:, :, :, :].rearrange("p t h e -> p t (h e)") for t in (agg, term))
            dve.tensor_reduce(mean[:, :], rows, AX_X, ALU.add)
            dve.drain()
            ts(mean[:, :], mean[:, :], 1.0 / HE, None, ALU.mult)
            tt(rows, rows, by_tile(mean, HE), ALU.subtract)
            tt(term_rows, rows, rows, ALU.mult)
            dve.tensor_reduce(spread[:, :], term_rows, AX_X, ALU.add)
            dve.drain()
            dve.tensor_scalar(spread[:, :], spread[:, :], 1.0 / HE, LN_T_EPS, ALU.mult, ALU.add).then_inc(var_ready, 1)
            dve.wait_ge(root_ready, 1)
            dve.reciprocal(spread[:, :], spread[:, :])
            dve.drain()
            tt(rows, rows, by_tile(spread, HE), ALU.mult)
            tt(agg[:, :, :, :], agg[:, :, :, :], vector(ln_gamma[:, :]), ALU.mult)
            tt(agg[:, :, :, :], agg[:, :, :, :], vector(ln_beta[:, :]), ALU.add)
            score = part
            dve.tensor_reduce(score[:, :, :], agg[:, :, :, :].rearrange("p t h e -> p t e h"), AX_X, ALU.add)
            dve.drain()
            ts(score[:, :, :], score[:, :, :], 1.0 / HEADS, None, ALU.mult)

            rank, ahead = total, loop
            dve.memset(rank[:, :, :], 0.0)
            dve.drain()
            for a in range(EXPERTS):
                for b in range(a + 1, EXPERTS):
                    tt(ahead[:, :, 0], score[:, :, a], score[:, :, b], ALU.is_ge)
                    ts(ahead[:, :, 1], ahead[:, :, 0], -1.0, 1.0, ALU.mult, ALU.add)
                    dve.tensor_tensor(rank[:, :, b], rank[:, :, b], ahead[:, :, 0], ALU.add)
                    tt(rank[:, :, a], rank[:, :, a], ahead[:, :, 1], ALU.add)
            dve.tensor_reduce(mean[:, :], score[:, :, :], AX_X, ALU.max)
            dve.drain()
            dve.tensor_tensor(k.gate[:, :, :], score[:, :, :], by_tile(mean, EXPERTS),
                              ALU.subtract).then_inc(gaps_ready, 1)
            ts(rank[:, :, :], rank[:, :, :], 1.5, None, ALU.is_lt)
            dve.wait_ge(gaps_raised, 1)
            tt(k.gate[:, :, :], k.gate[:, :, :], rank[:, :, :], ALU.mult)
            dve.tensor_reduce(mean[:, :], k.gate[:, :, :], AX_X, ALU.add)
            dve.drain()
            dve.reciprocal(mean[:, :], mean[:, :])
            dve.drain()
            tt(k.gate[:, :, :], k.gate[:, :, :], by_tile(mean, EXPERTS), ALU.mult)


def mix_experts(nc, k, out):
    T = GPX // P
    TILE_BUFS = 2
    TILES_ALL = IMGS * ROW_GROUPS
    out_tiles = out.rearrange("b (h p) y w -> b p h (y w)", p=P)
    with ExitStack() as ctx:
        def sb(name, shape):
            return ctx.enter_context(nc.sbuf_tensor("me_" + name, shape, F32))

        def sem(name):
            return ctx.enter_context(nc.semaphore("me_" + name))

        def ps(name, shape):
            return ctx.enter_context(nc.psum_tensor("me_" + name, shape, F32))
        pick = sb("pick", [EXPERTS, EXPERTS, P])
        given = [sb(f"given{b}", [P, EXPERTS, PARTS_C, GPX]) for b in range(TILE_BUFS)]
        res = [sb(f"res{b}", [P, PARTS_C, GPX]) for b in range(TILE_BUFS)]
        gate_column = [sb(f"gate_column{b}", [P, T, EXPERTS]) for b in range(2)]
        gate_row = [sb(f"gate_row{b}", [EXPERTS, GPX]) for b in range(2)]
        row_ps = ps("row_ps", [EXPERTS, GPX])
        gate_ps = [ps(f"gate_ps{e}", [P, GPX]) for e in range(EXPERTS)]
        given_in = [sem(f"given_in{b}") for b in range(TILE_BUFS)]
        res_in = [sem(f"res_in{b}") for b in range(TILE_BUFS)]
        stored = [sem(f"stored{b}") for b in range(TILE_BUFS)]
        pick_ready, column_ready, row_turned, gate_ready = (
            sem(n) for n in ("pick_ready", "column_ready", "row_turned", "gate_ready"))
        row_taken, gate_used, mixed = sem("row_taken"), sem("gate_used"), sem("mixed")
        block = ctx.enter_context(nc.Block())

        @block.gpsimd
        def _(pool):
            pool.memset(pick[:, :, :], 1.0).then_inc(pick_ready, 1)
            pool.wait_ge(pick_ready, 1)
            pool.affine_select(out=pick[:, :, :], in_=pick[:, :, :], compare_op=ALU.is_equal, fill=0.0, base=0,
                               pattern=[[-1, EXPERTS], [0, P]], channel_multiplier=1).then_inc(pick_ready, 1)

            def store(img, g, n, u):
                b = u % TILE_BUFS
                wait_alone(pool, mixed, n + 1 + TILE_BUFS, k.passed)
                pool.dma_start(out_tiles[img, :, :, bass.ds(g * GPX, GPX)], res[b][:, :, :]).then_inc(stored[b], 16)
            over_tiles(pool, [(store, 0)])
            for b in range(TILE_BUFS):
                pool.wait_ge(stored[b], 16 * TILES_ALL // TILE_BUFS)

        @block.sync
        def _(sp):
            def load(img, g, n, u):
                b = u % TILE_BUFS
                wait_alone(sp, mixed, n + 1, k.passed)
                sp.dma_start(given[b][:, :, :, :].rearrange("p e h t -> p (e h t)"),
                             k.expert_out[bass.ds(n, 1)].rearrange("a p v -> p (a v)")).then_inc(given_in[b], 16)
                if not isinstance(n, int) or n >= TILE_BUFS:
                    wait_alone(sp, stored[b], (n - b) * (16 // TILE_BUFS), k.passed)
                sp.dma_start(res[b][:, :, :],
                             k.residual[bass.ds(n, 1)].rearrange("a p h t -> p (a h) t")).then_inc(res_in[b], 16)
            through_tiles(sp, [(load, 0)])

        @block.tensor
        def _(pe):
            pe.wait_ge(pick_ready, 2)

            def turn_gates(img, g, n, u):
                pe.wait_ge(column_ready, n + 1)
                pe.wait_ge(row_taken, n + 1)
                for t in range(T):
                    mm = pe.transpose(row_ps[:, t * P:(t + 1) * P], gate_column[u % 2][:, t, :], k.ident[:, :])
                mm.then_inc(row_turned, 1)

            def spread_gates(img, g, n, u):
                pe.wait_ge(row_taken, n + 2)
                for e in range(EXPERTS):
                    pe.wait_ge(gate_used, n * EXPERTS + (e + 1))
                    pe.matmul(gate_ps[e][:, :], pick[:, e, :], gate_row[u % 2][:, :], start=True,
                              stop=True).then_inc(gate_ready, 1)
            through_tiles(pe, [(turn_gates, 0), (spread_gates, 1)])

        @block.scalar
        def _(act):
            act.sem_inc(row_taken, 1)

            def take_column(img, g, n, u):
                act.wait_ge(row_taken, n + 1)
                act.activation(gate_column[u % 2][:, :, :], k.gate[:, bass.ds(n * T, T), :],
                               ACT.Copy).then_inc(column_ready, 1)

            def take_row(img, g, n, u):
                act.wait_ge(row_turned, n + 1)
                act.wait_ge(gate_used, n * EXPERTS + 1)
                act.activation(gate_row[u % 2][:, :], row_ps[:, :], ACT.Copy).then_inc(row_taken, 1)

            through_tiles(act, [(take_column, 0), (take_row, 0)])

        @block.vector
        def _(dve):
            dve.sem_inc(gate_used, EXPERTS)
            dve.sem_inc(mixed, TILE_BUFS)

            def mix(img, g, n, u):
                b = u % TILE_BUFS
                v = given[b]
                dve.wait_ge(given_in[b], (n - b) * (16 // TILE_BUFS) + 16)
                for e in range(EXPERTS):
                    dve.wait_ge(gate_ready, n * EXPERTS + (e + 1))
                    dve.tensor_tensor(v[:, e, :, :], v[:, e, :, :],
                                      gate_ps[e][:, :].unsqueeze(1).to_broadcast([P, PARTS_C, GPX]),
                                      ALU.mult).then_inc(gate_used, 1)
                dve.drain()
                half = EXPERTS // 2
                dve.tensor_tensor(v[:, 0:half, :, :], v[:, 0:half, :, :], v[:, half:, :, :], ALU.add)
                dve.drain()
                dve.tensor_tensor(v[:, 0, :, :], v[:, 0, :, :], v[:, 1, :, :], ALU.add)
                dve.drain()
                dve.wait_ge(res_in[b], (n - b) * (16 // TILE_BUFS) + 16)
                dve.tensor_tensor(res[b][:, :, :], res[b][:, :, :], v[:, 0, :, :], ALU.add).then_inc(mixed, 1)
            through_tiles(dve, [(mix, 0)])


def constants(nc, k):
    with ExitStack() as ctx:
        zeroed = ctx.enter_context(nc.semaphore("co_zeroed"))
        block = ctx.enter_context(nc.Block())

        @block.gpsimd
        def _(pool):
            pool.memset(k.ident[:, :], 0.0).then_inc(zeroed, 1)
            pool.memset(k.ones_f[:, :], 1.0)
            pool.wait_ge(zeroed, 1)
            pool.affine_select(out=k.ident[:, :], in_=k.ident[:, :], compare_op=ALU.not_equal, fill=1.0, base=0,
                               pattern=[[-1, P]], channel_multiplier=1).then_inc(zeroed, 1)
            pool.memset(k.mean_c[:, :], 1.0 / C)
            pool.memset(k.eps_c[:, :], LN_C_EPS)
            pool.memset(k.eps_t[:, :], LN_T_EPS)
            pool.wait_ge(zeroed, 2)
            pool.tensor_copy(k.ident_b[:, :], k.ident[:, :])
            pool.memset(k.sign[:, :], 1.0).then_inc(zeroed, 1)
            pool.wait_ge(zeroed, 3)
            pool.memset(k.sign[P // QUARTERS:2 * P // QUARTERS, :], -1.0).then_inc(zeroed, 1)
            pool.wait_ge(zeroed, 4)
            pool.memset(k.sign[3 * P // QUARTERS:P, :], -1.0)


def run_edges(nc, k):
    with ExitStack() as ctx:
        expert_buffers(nc, k, ctx)
        expert_constants(nc, k)
        with ExitStack() as sort_ctx:
            k.keys_a = sort_ctx.enter_context(nc.sbuf_tensor("keys_a", [P, LANE], F32))
            k.keys_b = sort_ctx.enter_context(nc.sbuf_tensor("keys_b", [P, LANE], F32))
            edge_keys(nc, k)
            sort_pruned(nc, k)
            sort_all(nc, k)
            store_sorted(nc, k)
        k.first_place, k.last_place = (
            ctx.enter_context(nc.sbuf_tensor(name, [P, TILES], U32)) for name in ("first_place", "last_place"))
        k.has_own, k.has_last, k.count_last = (
            ctx.enter_context(nc.sbuf_tensor(name, [P, TILES], F32)) for name in ("has_own", "has_last", "count_last"))
        count_edges(nc, k)
        place_scores(nc, k)
        edge_softmax(nc, k)
        gates(nc, k)


ARGS = ("x", "w_cat_t", "w_scale_t", "gamma", "beta", "w_gat", "att_src", "att_dst", "b_gat", "ln_gamma",
        "ln_beta", "w1", "b1", "w2", "b2", "edge_index")


def build(nc, args, out):
    k = Ctx()
    (k.x, k.w_cat_t, k.w_scale_t, k.gamma, k.beta, k.w_gat, k.att_src, k.att_dst, k.b_gat, k.ln_gamma, k.ln_beta,
     k.w1, k.b1, k.w2, k.b2, k.edge_index) = (args[name] for name in ARGS)
    declare_scratch(nc, k)
    with ExitStack() as ctx:
        def sb(name, shape, dt):
            return ctx.enter_context(nc.sbuf_tensor(name, shape, dt))
        k.passed = ctx.enter_context(nc.semaphore("passed"))
        k.ident = sb("ident", [P, P], F32)
        k.ones_f = sb("ones_f", [P, P], F32)
        k.mean_c = sb("mean_c", [P, P], F32)
        k.eps_c = sb("eps_c", [P, 1], F32)
        k.eps_t = sb("eps_t", [P, 1], F32)
        k.ident_b = sb("ident_b", [P, P], BF16)
        k.sign = sb("sign", [P, 1], F32)
        k.edge_counts = sb("edge_counts", [P, 3], I32)
        constants(nc, k)
        layer_norm_tiles(nc, k, tokens=False)
        guide_taps(nc, k)
        k.y_stats = sb("y_stats", [P, PARTS_C, TOK // GPX, 6], F32)
        with ExitStack() as conv_ctx:
            k.offsets = [0] + [sign * d for d in DILATIONS for sign in (-1, 1)]
            k.masks = conv_ctx.enter_context(nc.sbuf_tensor("masks", [W, len(k.offsets), GPX], U16))
            k.pick_left = conv_ctx.enter_context(nc.sbuf_tensor("pick_left", [SPLITS * LEFT, LEFT, W], BF16))
            k.pick_right = conv_ctx.enter_context(nc.sbuf_tensor("pick_right", [SPLITS * RIGHT, RIGHT, W], BF16))
            branch_masks(nc, k)
            dilated_branches(nc, k)
        k.bn_scale, k.bn_shift = sb("bn_scale", [P, PARTS_C], F32), sb("bn_shift", [P, PARTS_C], F32)
        k.w_graph = sb("w_graph", [P, PARTS_C, NODE], F32)
        k.node = sb("node", [P, TILES, NODE], F32)
        token_constants(nc, k)
        layer_norm_tiles(nc, k, tokens=True)
        k.gate = sb("gate", [P, TILES, EXPERTS], F32)
        run_edges(nc, k)
        mix_experts(nc, k, out)


def kernel(**inputs):
    import numpy as np
    import concourse.bacc as bacc
    from concourse.bass_utils import run_bass_kernel_spmd

    conv, ffn = "L0_conv_", "L0_ffn_"
    given = {name: np.asarray(a) for name, a in inputs.items()}
    arrays = {
        "x": given["x"],
        "w_cat_t": given[conv + "W_cat"].transpose(1, 2, 3, 0).reshape(C, TAPS, GUIDES),
        "w_scale_t": given[conv + "W_scale"].reshape(C, (BRANCHES + 1) * C).T,
        "gamma": given[conv + "gamma"], "beta": given[conv + "beta"],
        "w_gat": given[ffn + "W_gat"], "att_src": given[ffn + "att_src"], "att_dst": given[ffn + "att_dst"],
        "b_gat": given[ffn + "b_gat"], "ln_gamma": given[ffn + "ln_gamma"], "ln_beta": given[ffn + "ln_beta"],
        "w1": given[ffn + "W1"], "b1": given[ffn + "b1"], "w2": given[ffn + "W2"], "b2": given[ffn + "b2"],
        "edge_index": given[ffn + "edge_index"],
    }
    arrays = {"in_" + name: np.ascontiguousarray(a) for name, a in arrays.items()}
    nc = bacc.Bacc("TRN2", target_bir_lowering=False, num_devices=1)
    args = {name: nc.dram_tensor("in_" + name, arrays["in_" + name].shape,
                                 mybir.dt.from_np(arrays["in_" + name].dtype), kind="ExternalInput").ap()
            for name in ARGS}
    out = nc.dram_tensor("out", (IMGS, C, H, W), F32, kind="ExternalOutput").ap()
    build(nc, args, out)
    return run_bass_kernel_spmd(nc, [arrays], core_ids=[0]).results[0]["out"]
```
